# Optimizing a Trainium2 kernel written in Bass

```python
import numpy as np
import jax
import jax.numpy as jnp

def _softmax(x, axis=-1):
    return jax.nn.softmax(x, axis=axis)

def _gelu(x):
    return jax.nn.gelu(x, approximate=True)

def _silu(x):
    return jax.nn.silu(x)

def _sigmoid(x):
    return jax.nn.sigmoid(x)

def _layernorm(x, axis=-1, eps=1e-05):
    m = jnp.mean(x, axis=axis, keepdims=True)
    v = jnp.var(x, axis=axis, keepdims=True)
    return (x - m) / jnp.sqrt(v + eps)

def _scatter_add(tgt, idx, src, axis=0):
    return tgt.at[idx].add(src)

def _segment_sum(src, seg, n):
    return jax.ops.segment_sum(src, seg, n)
kernel_name = 'mk_macaron_d1_jaxref_r8_70c780'

def setup_inputs(seed: int=0):
    np.random.seed(seed)
    _w = jnp.asarray

    def _L0_attn_setup():
        import jax, jax.numpy as jnp
        import numpy as np
        HEADS = 16

        def _binarize(W):
            alpha = jnp.mean(jnp.abs(W), axis=tuple(range(1, W.ndim)), keepdims=True)
            B = W + jax.lax.stop_gradient(jnp.sign(W) - W)
            return alpha * B

        def _binlinear(x, W, b):
            Wb = _binarize(W)
            return jnp.einsum('btc,oc->bto', x, Wb) + b
        key = jax.random.key(seed)
        ks = jax.random.split(key, 9)
        dim = 128
        B, T = (4, 256)
        inp = {'x': jax.random.normal(ks[0], (B, T, dim), jnp.float32), 'Wq': jax.random.normal(ks[1], (dim, dim), jnp.float32) * 0.02, 'bq': jax.random.normal(ks[2], (dim,), jnp.float32) * 0.02, 'Wk': jax.random.normal(ks[3], (dim, dim), jnp.float32) * 0.02, 'bk': jax.random.normal(ks[4], (dim,), jnp.float32) * 0.02, 'Wv': jax.random.normal(ks[5], (dim, dim), jnp.float32) * 0.02, 'bv': jax.random.normal(ks[6], (dim,), jnp.float32) * 0.02, 'Wp': jax.random.normal(ks[7], (dim, dim), jnp.float32) * 0.02, 'bp': jax.random.normal(ks[8], (dim,), jnp.float32) * 0.02}
        return inp
    _L0_attn_in = _L0_attn_setup()

    def _L0_ffn_setup():
        import jax, jax.numpy as jnp
        import numpy as np
        DIM = 128
        DEPTH = 2
        HEADS = 8
        DIM_HEAD = 64
        WINDOW = 64
        INNER = HEADS * DIM_HEAD
        HID = int(DIM * 4 * 2 / 3)
        B, N = (2, 1024)
        QK_SCALE = 8.0

        def shift_token(t):
            t1, t2 = jnp.split(t, 2, axis=-1)
            t2 = jnp.pad(t2, ((0, 0), (1, 0), (0, 0)))[:, :-1]
            return jnp.concatenate([t1, t2], axis=-1)

        def l2norm(t):
            return t / jnp.clip(jnp.linalg.norm(t, axis=-1, keepdims=True), 1e-12)

        def rotate_half(x):
            x1, x2 = jnp.split(x, 2, axis=-1)
            return jnp.concatenate([-x2, x1], axis=-1)

        def rotary_xpos(q, k):
            n = q.shape[-2]
            half_idx = jnp.arange(0, DIM_HEAD, 2, dtype=jnp.float32)
            inv_freq = 1.0 / 10000.0 ** (half_idx / DIM_HEAD)
            t = jnp.arange(n, dtype=jnp.float32)
            freqs = t[:, None] * inv_freq[None, :]
            freqs = jnp.concatenate([freqs, freqs], axis=-1)
            base = (half_idx + 0.4 * DIM_HEAD) / (1.4 * DIM_HEAD)
            power = (t - n // 2) / float(WINDOW // 2)
            scale = base[None, :] ** power[:, None]
            scale = jnp.concatenate([scale, scale], axis=-1)
            cos, sin = (jnp.cos(freqs), jnp.sin(freqs))
            q = q * cos * scale + rotate_half(q) * sin * scale
            k = k * cos / scale + rotate_half(k) * sin / scale
            return (q, k)

        def local_attention(q, k, v):
            b, h, n, d = q.shape
            w = n // WINDOW
            bq = q.reshape(b, h, w, WINDOW, d) * QK_SCALE
            bk = k.reshape(b, h, w, WINDOW, d)
            bv = v.reshape(b, h, w, WINDOW, d)

            def look_around(t):
                p = jnp.pad(t, ((0, 0), (0, 0), (1, 0), (0, 0), (0, 0)))
                return jnp.concatenate([p[:, :, :w], p[:, :, 1:]], axis=3)
            bk, bv = (look_around(bk), look_around(bv))
            bt = jnp.arange(n).reshape(w, WINDOW)
            btp = jnp.pad(bt, ((1, 0), (0, 0)), constant_values=-1)
            btk = jnp.concatenate([btp[:w], btp[1:]], axis=1)
            sim = jnp.einsum('bhwid,bhwjd->bhwij', bq, bk)
            i = bt[:, :, None]
            j = btk[:, None, :]
            mask = (i < j) | (i > j + WINDOW) | (j == -1)
            sim = jnp.where(mask, -jnp.finfo(sim.dtype).max, sim)
            attn = jax.nn.softmax(sim, axis=-1)
            out = jnp.einsum('bhwij,bhwjd->bhwid', attn, bv)
            return out.reshape(b, h, n, d)

        def _layer(x, wqkv, qs, ksc, wo, lg, lb, w1, b1, w2, b2):
            b, n, _ = x.shape
            h = shift_token(x)
            qkv = h @ wqkv
            q, k, v = jnp.split(qkv, 3, axis=-1)
            to_heads = lambda t: t.reshape(b, n, HEADS, DIM_HEAD).transpose(0, 2, 1, 3)
            q, k, v = (to_heads(q), to_heads(k), to_heads(v))
            q = l2norm(q) * qs
            k = l2norm(k) * ksc
            q, k = rotary_xpos(q, k)
            o = local_attention(q, k, v)
            o = o.transpose(0, 2, 1, 3).reshape(b, n, INNER)
            x = x + o @ wo
            h = shift_token(x)
            mu = h.mean(-1, keepdims=True)
            var = h.var(-1, keepdims=True)
            h = (h - mu) / jnp.sqrt(var + 1e-05) * lg + lb
            h = h @ w1 + b1
            a, g = jnp.split(h, 2, axis=-1)
            h = a * jax.nn.gelu(g, approximate=False)
            x = x + h @ w2 + b2
            return x
        key = jax.random.key(seed)
        ks = jax.random.split(key, 6)
        return {'x': jax.random.normal(ks[0], (B, N, DIM), jnp.float32), 'wqkv': jax.random.normal(ks[1], (DEPTH, DIM, 3 * INNER), jnp.float32) * 0.02, 'q_scale': jnp.ones((DEPTH, DIM_HEAD), jnp.float32), 'k_scale': jnp.ones((DEPTH, DIM_HEAD), jnp.float32), 'wo': jax.random.normal(ks[2], (DEPTH, INNER, DIM), jnp.float32) * 0.02, 'ln_g': jnp.ones((DEPTH, DIM), jnp.float32), 'ln_b': jnp.zeros((DEPTH, DIM), jnp.float32), 'w1': jax.random.normal(ks[3], (DEPTH, DIM, 2 * HID), jnp.float32) * 0.02, 'b1': jnp.zeros((DEPTH, 2 * HID), jnp.float32), 'w2': jax.random.normal(ks[4], (DEPTH, HID, DIM), jnp.float32) * 0.02, 'b2': jnp.zeros((DEPTH, DIM), jnp.float32)}
    _L0_ffn_in = _L0_ffn_setup()
    _d = {'L0_attn_x': _L0_attn_in['x'], 'L0_attn_Wq': _L0_attn_in['Wq'], 'L0_attn_bq': _L0_attn_in['bq'], 'L0_attn_Wk': _L0_attn_in['Wk'], 'L0_attn_bk': _L0_attn_in['bk'], 'L0_attn_Wv': _L0_attn_in['Wv'], 'L0_attn_bv': _L0_attn_in['bv'], 'L0_attn_Wp': _L0_attn_in['Wp'], 'L0_attn_bp': _L0_attn_in['bp'], 'L0_ffn_wqkv': _L0_ffn_in['wqkv'], 'L0_ffn_q_scale': _L0_ffn_in['q_scale'], 'L0_ffn_k_scale': _L0_ffn_in['k_scale'], 'L0_ffn_wo': _L0_ffn_in['wo'], 'L0_ffn_ln_g': _L0_ffn_in['ln_g'], 'L0_ffn_ln_b': _L0_ffn_in['ln_b'], 'L0_ffn_w1': _L0_ffn_in['w1'], 'L0_ffn_b1': _L0_ffn_in['b1'], 'L0_ffn_w2': _L0_ffn_in['w2'], 'L0_ffn_b2': _L0_ffn_in['b2']}
    _x0 = _d['L0_attn_x']
    _d['L0_attn_x'] = jax.random.normal(jax.random.fold_in(jax.random.key(seed), 1), (4, 1024, 128), dtype=_x0.dtype)
    del _x0
    return _d

def reference(L0_attn_x, L0_attn_Wq, L0_attn_bq, L0_attn_Wk, L0_attn_bk, L0_attn_Wv, L0_attn_bv, L0_attn_Wp, L0_attn_bp, L0_ffn_wqkv, L0_ffn_q_scale, L0_ffn_k_scale, L0_ffn_wo, L0_ffn_ln_g, L0_ffn_ln_b, L0_ffn_w1, L0_ffn_b1, L0_ffn_w2, L0_ffn_b2):

    def _L0_attn_ref(x, Wq, bq, Wk, bk, Wv, bv, Wp, bp):
        import jax, jax.numpy as jnp
        import numpy as np
        HEADS = 16

        def _binarize(W):
            alpha = jnp.mean(jnp.abs(W), axis=tuple(range(1, W.ndim)), keepdims=True)
            B = W + jax.lax.stop_gradient(jnp.sign(W) - W)
            return alpha * B

        def _binlinear(x, W, b):
            Wb = _binarize(W)
            return jnp.einsum('btc,oc->bto', x, Wb) + b
        B, T, C = x.shape
        H = HEADS
        Dh = C // H
        scale = Dh ** (-0.5)

        def split_heads(t):
            return t.reshape(B, T, H, Dh).transpose(0, 2, 1, 3)
        q = split_heads(_binlinear(x, Wq, bq))
        k = split_heads(_binlinear(x, Wk, bk))
        v = split_heads(_binlinear(x, Wv, bv))
        att = jnp.einsum('bhtd,bhsd->bhts', q, k) * scale
        att = jax.nn.softmax(att, axis=-1)
        y = jnp.einsum('bhts,bhsd->bhtd', att, v)
        y = y.transpose(0, 2, 1, 3).reshape(B, T, C)
        return _binlinear(y, Wp, bp)

    def _L0_ffn_ref(x, wqkv, q_scale, k_scale, wo, ln_g, ln_b, w1, b1, w2, b2):
        import jax, jax.numpy as jnp
        import numpy as np
        DIM = 128
        DEPTH = 2
        HEADS = 8
        DIM_HEAD = 64
        WINDOW = 64
        INNER = HEADS * DIM_HEAD
        HID = int(DIM * 4 * 2 / 3)
        B, N = (2, 1024)
        QK_SCALE = 8.0

        def shift_token(t):
            t1, t2 = jnp.split(t, 2, axis=-1)
            t2 = jnp.pad(t2, ((0, 0), (1, 0), (0, 0)))[:, :-1]
            return jnp.concatenate([t1, t2], axis=-1)

        def l2norm(t):
            return t / jnp.clip(jnp.linalg.norm(t, axis=-1, keepdims=True), 1e-12)

        def rotate_half(x):
            x1, x2 = jnp.split(x, 2, axis=-1)
            return jnp.concatenate([-x2, x1], axis=-1)

        def rotary_xpos(q, k):
            n = q.shape[-2]
            half_idx = jnp.arange(0, DIM_HEAD, 2, dtype=jnp.float32)
            inv_freq = 1.0 / 10000.0 ** (half_idx / DIM_HEAD)
            t = jnp.arange(n, dtype=jnp.float32)
            freqs = t[:, None] * inv_freq[None, :]
            freqs = jnp.concatenate([freqs, freqs], axis=-1)
            base = (half_idx + 0.4 * DIM_HEAD) / (1.4 * DIM_HEAD)
            power = (t - n // 2) / float(WINDOW // 2)
            scale = base[None, :] ** power[:, None]
            scale = jnp.concatenate([scale, scale], axis=-1)
            cos, sin = (jnp.cos(freqs), jnp.sin(freqs))
            q = q * cos * scale + rotate_half(q) * sin * scale
            k = k * cos / scale + rotate_half(k) * sin / scale
            return (q, k)

        def local_attention(q, k, v):
            b, h, n, d = q.shape
            w = n // WINDOW
            bq = q.reshape(b, h, w, WINDOW, d) * QK_SCALE
            bk = k.reshape(b, h, w, WINDOW, d)
            bv = v.reshape(b, h, w, WINDOW, d)

            def look_around(t):
                p = jnp.pad(t, ((0, 0), (0, 0), (1, 0), (0, 0), (0, 0)))
                return jnp.concatenate([p[:, :, :w], p[:, :, 1:]], axis=3)
            bk, bv = (look_around(bk), look_around(bv))
            bt = jnp.arange(n).reshape(w, WINDOW)
            btp = jnp.pad(bt, ((1, 0), (0, 0)), constant_values=-1)
            btk = jnp.concatenate([btp[:w], btp[1:]], axis=1)
            sim = jnp.einsum('bhwid,bhwjd->bhwij', bq, bk)
            i = bt[:, :, None]
            j = btk[:, None, :]
            mask = (i < j) | (i > j + WINDOW) | (j == -1)
            sim = jnp.where(mask, -jnp.finfo(sim.dtype).max, sim)
            attn = jax.nn.softmax(sim, axis=-1)
            out = jnp.einsum('bhwij,bhwjd->bhwid', attn, bv)
            return out.reshape(b, h, n, d)

        def _layer(x, wqkv, qs, ksc, wo, lg, lb, w1, b1, w2, b2):
            b, n, _ = x.shape
            h = shift_token(x)
            qkv = h @ wqkv
            q, k, v = jnp.split(qkv, 3, axis=-1)
            to_heads = lambda t: t.reshape(b, n, HEADS, DIM_HEAD).transpose(0, 2, 1, 3)
            q, k, v = (to_heads(q), to_heads(k), to_heads(v))
            q = l2norm(q) * qs
            k = l2norm(k) * ksc
            q, k = rotary_xpos(q, k)
            o = local_attention(q, k, v)
            o = o.transpose(0, 2, 1, 3).reshape(b, n, INNER)
            x = x + o @ wo
            h = shift_token(x)
            mu = h.mean(-1, keepdims=True)
            var = h.var(-1, keepdims=True)
            h = (h - mu) / jnp.sqrt(var + 1e-05) * lg + lb
            h = h @ w1 + b1
            a, g = jnp.split(h, 2, axis=-1)
            h = a * jax.nn.gelu(g, approximate=False)
            x = x + h @ w2 + b2
            return x
        for l in range(DEPTH):
            x = _layer(x, wqkv[l], q_scale[l], k_scale[l], wo[l], ln_g[l], ln_b[l], w1[l], b1[l], w2[l], b2[l])
        return x
    x = L0_attn_x
    x = x + 0.5 * _L0_ffn_ref(_layernorm(x, axis=-1), L0_ffn_wqkv, L0_ffn_q_scale, L0_ffn_k_scale, L0_ffn_wo, L0_ffn_ln_g, L0_ffn_ln_b, L0_ffn_w1, L0_ffn_b1, L0_ffn_w2, L0_ffn_b2)
    x = x + _L0_attn_ref(_layernorm(x, axis=-1), L0_attn_Wq, L0_attn_bq, L0_attn_Wk, L0_attn_bk, L0_attn_Wv, L0_attn_bv, L0_attn_Wp, L0_attn_bp)
    x = x + 0.5 * _L0_ffn_ref(_layernorm(x, axis=-1), L0_ffn_wqkv, L0_ffn_q_scale, L0_ffn_k_scale, L0_ffn_wo, L0_ffn_ln_g, L0_ffn_ln_b, L0_ffn_w1, L0_ffn_b1, L0_ffn_w2, L0_ffn_b2)
    return x

_drawn_inputs = setup_inputs


def setup_inputs(seed=0):
    import zlib

    import numpy as np

    out = dict(_drawn_inputs(seed))
    spreads = {'L0_ffn_q_scale': (1.0, 0.6),
     'L0_ffn_k_scale': (1.0, 0.6),
     'L0_ffn_ln_g': (1.0, 0.6),
     'L0_ffn_ln_b': (0.0, 0.8),
     'L0_ffn_b1': (0.0, 0.8),
     'L0_ffn_b2': (0.0, 0.1)}
    factors = {'L0_attn_Wq': 8.0,
     'L0_attn_bq': 28.756,
     'L0_attn_Wk': 8.0,
     'L0_attn_bk': 64.0,
     'L0_attn_Wv': 8.0,
     'L0_attn_bv': 8.0,
     'L0_attn_Wp': 8.0,
     'L0_attn_bp': 4.052,
     'L0_ffn_wqkv': 3.361,
     'L0_ffn_wo': 3.327,
     'L0_ffn_w1': 5.291,
     'L0_ffn_w2': 5.212}
    for name, (base, spread) in spreads.items():
        noise = np.random.default_rng([zlib.crc32(name.encode()), seed]).standard_normal(out[name].shape)
        drawn = base * np.exp(spread * noise) if base else spread * noise
        out[name] = jnp.asarray(drawn.astype(out[name].dtype))
    for name, factor in factors.items():
        out[name] = (out[name] * factor).astype(out[name].dtype)
    return out
```

```python
from contextlib import ExitStack

import numpy as np

import concourse.bass as bass
from concourse import mybir

FP32 = mybir.dt.float32
BF16 = mybir.dt.bfloat16
ALU = mybir.AluOpType
ACT = mybir.ActivationFunctionType
AX = mybir.AxisListType

P = 128
B, T, C = 4, 1024, 128
NT = T // P
LAYERS = 2
FH, FD, WIN = 8, 64, 64
PAIRS = FH // 2
INNER = FH * FD
HID = int(C * 4 * 2 / 3)
CH = 3
HC = -(-HID // CH)
QK_SCALE = 8.0
H, DH = 16, 8
QUADS = H // 4
PARTS = 3
KROWS = PARTS * PARTS * DH
MASKED = -1e30


def rotary_tables():
    half = np.arange(0, FD, 2, dtype=np.float32)
    inv = (np.float32(1.0) / np.float32(10000.0) ** (half / np.float32(FD))).astype(np.float32)
    t = np.arange(T, dtype=np.float32)
    freqs = (t[:, None] * inv[None, :]).astype(np.float32)
    freqs = np.concatenate([freqs, freqs], axis=-1)
    base = ((half + np.float32(0.4 * FD)) / np.float32(1.4 * FD)).astype(np.float32)
    power = ((t - T // 2) / np.float32(WIN // 2)).astype(np.float32)
    scale = (base[None, :].astype(np.float64) ** power[:, None]).astype(np.float32)
    scale = np.concatenate([scale, scale], axis=-1)
    cos, sin = np.cos(freqs), np.sin(freqs)
    sign = np.concatenate([-np.ones(FD // 2), np.ones(FD // 2)]).astype(np.float32)
    out = np.empty((2, T, 2, FD), np.float32)
    out[0, :, 0] = cos * scale * np.float32(QK_SCALE)
    out[1, :, 0] = sin * scale * sign * np.float32(QK_SCALE)
    out[0, :, 1] = cos / scale
    out[1, :, 1] = sin / scale * sign
    return np.ascontiguousarray(out.reshape(2, NT, P, 2, FD).transpose(0, 2, 1, 3, 4))


C_ID, C_CENTRE, C_ID64, C_SELW, C_MASK_Q, C_MASK_K = 0, 128, 256, 320, 576, 832
C_END = C_MASK_K + 3 * 64


def constants():
    c = np.zeros((P, C_END), np.float32)
    p = np.arange(P)
    c[:, C_ID:C_ID + P] = np.eye(P)
    c[:, C_CENTRE:C_CENTRE + P] = np.eye(P) - 1.0 / P
    c[:, C_ID64:C_ID64 + WIN] = p[:, None] % WIN == np.arange(WIN)[None]
    for w in range(2):
        c[:, C_SELW + P * w:C_SELW + P * (w + 1)] = (p // WIN == w)[:, None]
    i, j = np.arange(WIN)[:, None], np.arange(WIN)[None]
    causal, back = j <= i, i <= j
    for later in range(2):
        m = c[:, C_MASK_Q + P * later:C_MASK_Q + P * (later + 1)]
        m[:WIN, :WIN] = np.where(causal, 0, MASKED)
        m[:WIN, WIN:] = np.where(back, 0, MASKED) if later else MASKED
        m[WIN:, :WIN] = np.where(back, 0, MASKED)
        m[WIN:, WIN:] = np.where(causal, 0, MASKED)
    q = c[:, C_MASK_Q:C_MASK_Q + 2 * P]
    c[:, C_MASK_K:C_MASK_K + WIN] = q[:WIN, :P].T
    c[:, C_MASK_K + WIN:C_MASK_K + 2 * WIN] = q[:WIN, P:].T
    c[:, C_MASK_K + 2 * WIN:C_MASK_K + 3 * WIN] = q[WIN:, P:].T
    return c


class Memory:

    def __init__(self):
        self.used_semaphores = []


def semaphore(nc, m, ctx, name):
    handle = ctx.enter_context(nc.semaphore(name))
    m.used_semaphores.append(handle)
    return handle


def clear_semaphores(nc, m):
    for handle in m.used_semaphores:
        nc.sync.sem_clear(handle)
    m.used_semaphores.clear()
    nc.all_engine_barrier()


def setup_phase(nc, m, a):
    ctx = ExitStack()
    with ctx:
        def sb(name, shape, dt=FP32):
            return ctx.enter_context(nc.sbuf_tensor(name, shape, dt))

        def sem(name):
            return semaphore(nc, m, ctx, name)

        x_rows = sb("su_x_rows", [P, B * NT, C])
        consts = sb("su_consts", [P, C_END])
        base = sb("su_base", [P, 2, NT, 2, FD])
        scales = sb("su_scales", [P, 2, LAYERS, 2, FD])
        ln_g = sb("su_ln_g", [P, LAYERS])
        ln_b = sb("su_ln_b", [P, LAYERS])
        b1_raw = sb("su_b1_raw", [HC, LAYERS, 2 * CH])

        zeroed = sem("su_zeroed")
        x_in = sem("su_x_in")
        c_in = sem("su_c_in")
        w_in = sem("su_w_in")
        t_in = sem("su_t_in")
        ready = sem("su_ready")
        x_tr = sem("su_x_tr")
        x_ev = sem("su_x_ev")
        bias_mm = sem("su_bias_mm")
        bias_done = sem("su_bias_done")
        tables = sem("su_tables")
        ctx.enter_context(nc.allow_non_contiguous_dma(reason="a few columns of parameters"))
        block = ctx.enter_context(nc.Block())

        w1_jobs = []
        for l in range(LAYERS):
            for k in range(2 * CH):
                lo = (k // CH) * HID + (k % CH) * HC
                w1_jobs.append((l, k, lo, min(HC, HID - (k % CH) * HC)))

        @block.sync
        def _(sp):
            sp.dma_start(consts[:, :], a["consts"]).then_inc(c_in, 16)
            for b in range(B):
                sp.dma_start(x_rows[:, b * NT:(b + 1) * NT, :],
                             a["L0_attn_x"][b].rearrange("(t p) c -> p t c", p=P)).then_inc(x_in, 16)
            sp.wait_ge(zeroed, 1)
            for l, k, lo, n in w1_jobs:
                sp.dma_start(m.w_all[:, l, 512 + k * HC:512 + k * HC + n],
                             a["L0_ffn_w1"][l, :, lo:lo + n]).then_inc(w_in, 16)
            for l in range(LAYERS):
                for k in range(CH):
                    n = min(HC, HID - k * HC)
                    o = 512 + 2 * CH * HC + k * P
                    sp.dma_start(m.w_all[0:n, l, o:o + P],
                                 a["L0_ffn_w2"][l, k * HC:k * HC + n, :]).then_inc(w_in, 16)
                sp.dma_start(m.w_all[:, l, 0:512].rearrange("p (k c) -> p k c", k=4),
                             a["L0_ffn_wo"][l].rearrange("(k p) c -> p k c", p=P)).then_inc(w_in, 16)
            sp.wait_ge(w_in, 16 * (len(w1_jobs) + LAYERS * (CH + 1)))

        @block.gpsimd
        def _(pool):
            nc.gpsimd.memset(m.w_all[:, :, 512:], 0.0)
            nc.gpsimd.memset(b1_raw[:, :, :], 0.0)
            nc.gpsimd.memset(m.xs[:, :, :, 0:1], 0.0)
            nc.gpsimd.memset(m.eps[:, :], 1e-5)
            nc.gpsimd.memset(m.mean_ones[:, :], 1.0 / C).then_inc(zeroed, 1)

        @block.scalar
        def _(act):
            act.wait_ge(zeroed, 1)
            for l in range(LAYERS):
                for q, name in enumerate(("L0_ffn_q_scale", "L0_ffn_k_scale")):
                    row = a[name][l:l + 1, :]
                    act.dma_start(scales[:, 0, l, q, :], row.broadcast_to([P, FD])).then_inc(t_in, 16)
                    for h in range(2):
                        o = 32 * h
                        act.dma_start(scales[:, 1, l, q, 32 - o:64 - o],
                                      row[:, o:o + 32].broadcast_to([P, 32])).then_inc(t_in, 16)
            act.dma_start(base[:, :, :, :, :], a["rot"].rearrange("a p t q d -> p a t q d")).then_inc(t_in, 16)
            act.dma_start(ln_g[:, :], a["L0_ffn_ln_g"].rearrange("l p -> p l")).then_inc(t_in, 16)
            act.dma_start(ln_b[:, :], a["L0_ffn_ln_b"].rearrange("l p -> p l")).then_inc(t_in, 16)
            act.dma_start(m.b2_all[:, :], a["L0_ffn_b2"].rearrange("l p -> p l")).then_inc(t_in, 16)
            for l, k, lo, n in w1_jobs:
                act.dma_start(b1_raw[0:n, l, k:k + 1],
                              a["L0_ffn_b1"][l:l + 1, lo:lo + n].rearrange("a p -> p a")).then_inc(t_in, 16)
            act.dma_start(m.wqkv[:, :, :], a["L0_ffn_wqkv"].rearrange("l p n -> p l n")).then_inc(t_in, 16)
            for n in range(B * NT // 4):
                act.wait_ge(x_tr, n + 1)
                nc.scalar.activation(m.X[:, n * 512:(n + 1) * 512], m.bank[n % 4][:, :], ACT.Copy).then_inc(x_ev, 1)

        t_total = LAYERS * 2 * 3 + 4 + len(w1_jobs) + 1

        @block.vector
        def _(dve):
            dve.wait_ge(c_in, 16)
            nc.vector.tensor_copy(m.ident[:, :], consts[:, C_ID:C_ID + P])
            nc.vector.tensor_copy(m.centre[:, :], consts[:, C_CENTRE:C_CENTRE + P])
            nc.vector.tensor_copy(m.ident_b[:, :], consts[:, C_ID:C_ID + P])
            nc.vector.tensor_copy(m.id64[:, :], consts[:, C_ID64:C_ID64 + WIN])
            nc.vector.tensor_copy(m.sel_w[:, :, :], consts[:, C_SELW:C_SELW + 2 * P].rearrange("p (w n) -> p w n", w=2))
            nc.vector.tensor_copy(m.mask_q[:, :, :], consts[:, C_MASK_Q:C_MASK_Q + 2 * P].rearrange("p (a n) -> p a n", a=2))
            nc.vector.tensor_copy(m.mask_k[:, :, :], consts[:, C_MASK_K:C_MASK_K + 3 * WIN].rearrange("p (a n) -> p a n", a=3)).then_inc(ready, 1)
            dve.wait_ge(t_in, 16 * t_total)
            for l in range(LAYERS):
                for k in range(2):
                    nc.vector.tensor_tensor(
                        m.tab[:, (l * 2 + k) * NT:(l * 2 + k + 1) * NT, :], base[:, k, :, :, :].rearrange("p t q d -> p t (q d)"),
                        scales[:, k, l, :, :].rearrange("p q d -> p (q d)").unsqueeze(1).broadcast_to([P, NT, 2 * FD]),
                        ALU.mult)
            dve.wait_ge(bias_mm, 1)
            nc.vector.tensor_tensor(m.b1_all[:, :, :], m.bank[4][0:HC, 0:LAYERS * 2 * CH].rearrange("p (l k) -> p l k", l=LAYERS),
                                    b1_raw[:, :, :], ALU.add)
            for l in range(LAYERS):
                last = nc.vector.tensor_scalar(m.w_all[:, l, 512:512 + 2 * CH * HC], m.w_all[:, l, 512:512 + 2 * CH * HC],
                                               ln_g[:, l:l + 1], None, ALU.mult)
            last.then_inc(tables, 1)

        @block.tensor
        def _(pe):
            pe.wait_ge(ready, 1)
            for n in range(B * NT // 4):
                if n % NT == 0 or n % 2 == 0:
                    pe.wait_ge(x_in, 16 * B)
                if n >= 4:
                    pe.wait_ge(x_ev, n - 3)
                for i in range(4):
                    last = nc.tensor.transpose(m.bank[n % 4][:, i * P:(i + 1) * P], x_rows[:, 4 * n + i, :], m.ident[:, :])
                last.then_inc(x_tr, 1)
            pe.wait_ge(w_in, 16 * (len(w1_jobs) + LAYERS * (CH + 1)))
            pe.wait_ge(t_in, 16 * t_total)
            for l, k, lo, n in w1_jobs:
                last = nc.tensor.matmul(m.bank[4][0:HC, l * 2 * CH + k:l * 2 * CH + k + 1],
                                        m.w_all[:, l, 512 + k * HC:512 + (k + 1) * HC], ln_b[:, l:l + 1],
                                        start=True, stop=True)
            last.then_inc(bias_mm, 1)


def layernorm_phase(nc, m, name, dst):
    N = B * T // 512
    ctx = ExitStack()
    with ctx:
        def sb(n, shape, dt=FP32):
            return ctx.enter_context(nc.sbuf_tensor(f"{name}_{n}", shape, dt))

        def sem(n):
            return semaphore(nc, m, ctx, f"{name}_{n}")

        sq = sb("sq", [P, 2, 512])
        log_var = sb("log_var", [P, 2, 512])
        rstd = sb("rstd", [P, 2, 512])
        centred, squared, varred, logged, rstd_ready, normed = (
            sem(s) for s in ("centred", "squared", "varred", "logged", "rstd_ready", "normed"))
        block = ctx.enter_context(nc.Block())

        @block.tensor
        def _(pe):
            for n in range(N + 1):
                if n < N:
                    if n >= 4:
                        pe.wait_ge(normed, n - 3)
                    nc.tensor.matmul(m.bank[n % 4][:, :], m.centre[:, :], m.X[:, n * 512:(n + 1) * 512],
                                     start=True, stop=True).then_inc(centred, 1)
                if n >= 1:
                    k = n - 1
                    pe.wait_ge(squared, k + 1)
                    if k >= 2:
                        pe.wait_ge(logged, k - 1)
                    nc.tensor.matmul(m.bank[4 + k % 2][:, :], m.mean_ones[:, :], sq[:, k % 2, :],
                                     start=True, stop=True).then_inc(varred, 1)

        @block.scalar
        def _(act):
            nc.scalar.preload_act_table_set("natural_log_exp_and_others")
            for n in range(N + 1):
                if n < N:
                    act.wait_ge(centred, n + 1)
                    if n >= 2:
                        act.wait_ge(varred, n - 1)
                    nc.scalar.activation(sq[:, n % 2, :], m.bank[n % 4][:, :], ACT.Square).then_inc(squared, 1)
                if n >= 1:
                    k = n - 1
                    act.wait_ge(varred, k + 1)
                    nc.scalar.activation(log_var[:, k % 2, :], m.bank[4 + k % 2][:, :], ACT.Ln,
                                         bias=m.eps[:, :]).then_inc(logged, 1)
                    act.wait_ge(logged, k + 1)
                    if k >= 2:
                        act.wait_ge(normed, k - 1)
                    nc.scalar.activation(rstd[:, k % 2, :], log_var[:, k % 2, :], ACT.Exp,
                                         scale=-0.5).then_inc(rstd_ready, 1)

        @block.vector
        def _(dve):
            for n in range(N):
                dve.wait_ge(rstd_ready, n + 1)
                nc.vector.tensor_tensor(dst(n), m.bank[n % 4][:, :], rstd[:, n % 2, :], ALU.mult).then_inc(normed, 1)


def ffn_phase(nc, m, name):
    ctx = ExitStack()
    with ctx:
        def sb(n, shape, dt=FP32):
            return ctx.enter_context(nc.sbuf_tensor(f"{name}_{n}", shape, dt))

        def sem(n):
            return semaphore(nc, m, ctx, f"{name}_{n}")

        w_cur = sb("w_cur", [P, m.w_cols])
        b1 = sb("b1", [HC, 2 * CH])
        b2 = sb("b2", [P, 1])
        hT = sb("hT", [P, B, P])
        rot = [sb(f"rot{b}", [P, 2 * INNER]) for b in range(B)]
        rot2 = [sb(f"rot2{i}", [P, 2 * INNER]) for i in range(2)]
        sq = [sb(f"sq{i}", [P, 2 * INNER]) for i in range(2)]
        ss = sb("ss", [P, B, 2 * FH])
        ssc = sb("ssc", [P, B, 2 * FH])
        log_ss = sb("log_ss", [P, B, 2 * FH])
        rnorm = sb("rnorm", [P, B, 2 * FH])
        q_pad = [sb(f"q_pad{b}", [P, PAIRS, 2, P]) for b in range(B)]
        k_blk = [sb(f"k_blk{b}", [P, PAIRS, 4, WIN]) for b in range(B)]
        v_cur = [sb(f"v_cur{b}", [P, FH, FD + 1]) for b in range(B)]
        v_mix = [sb(f"v_mix{b}", [P, FH, FD + 1]) for b in range(B)]
        neg_max = sb("neg_max", [P, B, FH])
        diag = [sb(f"diag{b}", [P, FH, WIN], BF16) for b in range(B)]
        rden = sb("rden", [P, B, FH])
        o = [sq[b % 2][:, (b // 2) * INNER:(b // 2 + 1) * INNER] for b in range(B)]
        oT = sb("oT", [P, 4, B, P])
        x1 = sb("x1", [P, B, P + 1])
        h2 = sb("h2", [P, B, P])
        hn = sb("hn", [P, B * P])
        u = sb("u", [HC, CH, B * P])

        weights, zeroed, ht_staged, x1_zero, x1_before = (
            sem(s) for s in ("weights", "zeroed", "ht_staged", "x1_zero", "x1_before"))
        kprev_done, vprev_done, vmix_done = ([sem(f"{s}{b}") for b in range(B)]
                                             for s in ("kprev_done", "vprev_done", "vmix_done"))
        per_b = ("qk_ready", "v_ready", "sq_ready", "ss_ready", "ssc_ready", "rn_log", "rn_ready",
                 "rot_done", "add_done", "qkn_ready", "tr_ready", "qk_evicted",
                 "v_evicted", "s_ready", "max_ready", "d_ready", "st_ready", "p_ready",
                 "pv_ready", "rd_ready", "o_ready", "ot_ready", "ot_evicted")
        per_it = ("wo_ready", "x1_done", "h2_staged", "cen_ready", "csq_ready", "var_ready",
                  "lv_ready", "rstd_ready", "hn_ready", "w2_ready", "out_done")
        (qk_ready, v_ready, sq_ready, ss_ready, ssc_ready, rn_log, rn_ready,
         rot_done, add_done, qkn_ready, tr_ready, qk_evicted,
         v_evicted, s_ready, max_ready, d_ready, st_ready, p_ready,
         pv_ready, rd_ready, o_ready, ot_ready, ot_evicted) = [sem(s) for s in per_b]
        (wo_ready, x1_done, h2_staged, cen_ready, csq_ready, var_ready,
         lv_ready, rstd_ready, hn_ready, w2_ready, out_done) = [sem(s) for s in per_it]
        a_ready, g_ready, gelu_done, u_ready = sem("a_ready"), sem("g_ready"), sem("gelu_done"), sem("u_ready")

        bank = m.bank
        block = ctx.enter_context(nc.Block())

        def pair(slot):
            return m.psum[:, 2 * slot:2 * slot + 2, :]

        single = bank[4:8]

        class Count:

            def __init__(self, it):
                self.it, self.it4, self.it3 = it, it * B, it * CH

            def cur(self, b):
                return self.it4 + (B + b + 1)

            def prev(self, b):
                return self.it4 + (b + 1)

            def now(self):
                return self.it + 2

            def before(self):
                return self.it + 1

            def chunk(self, k):
                return self.it3 + (k + 1)

            def copied(self, copies=1):
                return self.it * (16 * copies) + 16 * copies

        @block.tensor
        def _(pe):
            for s in (qk_ready, v_ready, tr_ready, s_ready, st_ready, pv_ready, ot_ready):
                pe.sem_inc(s, B)
            for s in (wo_ready, cen_ready, var_ready, w2_ready):
                pe.sem_inc(s, 1)
            with pe.Fori(0, LAYERS) as l:
                with pe.Fori(0, NT) as t:
                    n = Count(l * NT + t)
                    for b in range(B):
                        s = b % 2
                        pe.wait_ge(ht_staged, n.copied(2))
                        if b < 2:
                            pe.wait_ge(o_ready, n.prev(b + 2))
                        else:
                            pe.wait_ge(rot_done, n.cur(b - 2))
                            pe.wait_ge(sq_ready, n.cur(b - 2))
                        for i in range(2):
                            last = nc.tensor.matmul(pair(s)[:, i, :], hT[:, b, :],
                                                    m.wqkv[:, bass.ds(l, 1), i * INNER:(i + 1) * INNER].rearrange("p a n -> p (a n)"),
                                                    start=True, stop=True)
                        last.then_inc(qk_ready, 1)
                        if b == 1:
                            pe.wait_ge(out_done, n.it + NT)
                        elif b == 3:
                            pe.wait_ge(u_ready, n.it3)
                        else:
                            pe.wait_ge(gelu_done, n.it3)
                        nc.tensor.matmul(single[b][:, :], hT[:, b, :],
                                         m.wqkv[:, bass.ds(l, 1), 2 * INNER:3 * INNER].rearrange("p a n -> p (a n)"),
                                         start=True, stop=True).then_inc(v_ready, 1)
                    for b in range(B):
                        s = b % 2
                        pe.wait_ge(qkn_ready, n.cur(b))
                        if b < 2:
                            pe.wait_ge(rot_done, n.cur(b + 2))
                            pe.wait_ge(sq_ready, n.cur(b + 2))
                        else:
                            pe.wait_ge(qk_evicted, n.cur(b - 2))
                        for i in range(8):
                            last = nc.tensor.transpose(pair(s)[:, i // 4, (i % 4) * P:(i % 4 + 1) * P],
                                                       rot[b][:, i * P:(i + 1) * P], m.ident[:, :])
                        last.then_inc(tr_ready, 1)
                    later = (t + NT - 1) // NT
                    for b in range(B):
                        s = b % 2
                        pe.wait_ge(qk_evicted, n.cur(b + 2 if b < 2 else b))
                        pe.wait_ge(kprev_done[b], n.copied())
                        if b >= 2:
                            pe.wait_ge(max_ready, n.cur(b - 2))
                        for i in range(2):
                            nc.tensor.matmul(pair(s)[:, i, :].rearrange("p (h j) -> p h j", h=4), m.ident_b[:, :],
                                             m.mask_q[:, bass.ds(later, 1), :].broadcast_to([P, 4, P]),
                                             start=True, stop=False, skip_group_check=True)
                        for h in range(FH):
                            for w in range(2):
                                last = nc.tensor.matmul(
                                    pair(s)[WIN * w:WIN * (w + 1), h // 4, (h % 4) * P:(h % 4 + 1) * P],
                                    q_pad[b][:, h // 2, h % 2, WIN * w:WIN * (w + 1)],
                                    k_blk[b][:, h // 2, 2 - 2 * w:4 - 2 * w, :].rearrange("p a j -> p (a j)"),
                                    start=False, stop=True, skip_group_check=True)
                        last.then_inc(s_ready, 1)
                    for b in range(B):
                        s = b % 2
                        pe.wait_ge(d_ready, n.cur(b))
                        if b < 2:
                            pe.wait_ge(max_ready, n.cur(b + 2))
                        else:
                            pe.wait_ge(p_ready, n.cur(b - 2))
                        for w in range(2):
                            mask = m.mask_k[:, bass.ds(later, 1), :] if w == 0 else m.mask_k[:, 2:3, :]
                            nc.tensor.matmul(pair(s)[:, w, :].rearrange("p (h i) -> p h i", h=FH), m.ident_b[:, :],
                                             mask.broadcast_to([P, FH, WIN]),
                                             start=True, stop=False, skip_group_check=True)
                            nc.tensor.matmul(pair(s)[:, w, :], m.sel_w[:, w, :], diag[b][:, :, :].rearrange("p h i -> p (h i)"),
                                             start=False, stop=False, skip_group_check=True)
                            for j in range(PAIRS):
                                last = nc.tensor.matmul(
                                    pair(s)[:, w, j * P:(j + 1) * P], k_blk[b][:, j, 2 - 2 * w:4 - 2 * w, :].rearrange("p a j -> p (a j)"),
                                    q_pad[b][:, j, :, WIN * w:WIN * (w + 1)],
                                    start=False, stop=True, skip_group_check=True)
                        last.then_inc(st_ready, 1)
                    for b in range(B):
                        s = b % 2
                        pe.wait_ge(p_ready, n.cur(b + 2 if b < 2 else b))
                        pe.wait_ge(v_evicted, n.cur(b))
                        pe.wait_ge(vmix_done[b], n.copied())
                        pe.wait_ge(vprev_done[b], n.copied())
                        if b >= 2:
                            pe.wait_ge(o_ready, n.cur(b - 2))
                        probs = rot[b][:, :].rearrange("p (w h i) -> p w h i", w=2, h=FH)
                        for h in range(FH):
                            for w in range(2):
                                last = nc.tensor.matmul(
                                    pair(s)[WIN * w:WIN * (w + 1), h // 4, (h % 4) * (FD + 1):(h % 4 + 1) * (FD + 1)],
                                    probs[:, w, h, :], (v_cur if w else v_mix)[b][:, h, :], start=True, stop=True)
                        last.then_inc(pv_ready, 1)
                    for b in range(B):
                        pe.wait_ge(o_ready, n.cur(b))
                        for i in range(4):
                            last = nc.tensor.transpose(single[b][:, i * P:(i + 1) * P], o[b][:, i * P:(i + 1) * P], m.ident[:, :])
                        last.then_inc(ot_ready, 1)
                    pe.wait_ge(ot_evicted, n.cur(B - 1))
                    pe.wait_ge(weights, l + 1)
                    for k in range(4):
                        last = nc.tensor.matmul(single[0][:, :], w_cur[:, k * P:(k + 1) * P],
                                                oT[:, k, :, :].rearrange("p b t -> p (b t)"), start=k == 0, stop=k == 3)
                    last.then_inc(wo_ready, 1)
                    pe.wait_ge(h2_staged, n.now())
                    nc.tensor.matmul(single[1][:, :], m.centre[:, :], h2[:, :, :].rearrange("p b t -> p (b t)"),
                                     start=True, stop=True).then_inc(cen_ready, 1)
                    pe.wait_ge(csq_ready, n.now())
                    nc.tensor.matmul(single[2][:, :], m.mean_ones[:, :], hn[:, :], start=True, stop=True).then_inc(var_ready, 1)
                    pe.wait_ge(hn_ready, n.now())
                    for k in range(CH):
                        if k == 2:
                            pe.wait_ge(u_ready, n.chunk(0))
                            pe.wait_ge(gelu_done, n.chunk(0))
                        nc.tensor.matmul(single[(3, 1, 3)[k]][0:HC, :], w_cur[:, 512 + k * HC:512 + (k + 1) * HC],
                                         hn[:, :], start=True, stop=True).then_inc(a_ready, 1)
                        nc.tensor.matmul(single[(0, 2, 0)[k]][0:HC, :], w_cur[:, 512 + (CH + k) * HC:512 + (CH + k + 1) * HC],
                                         hn[:, :], start=True, stop=True).then_inc(g_ready, 1)
                    pe.wait_ge(u_ready, n.chunk(1))
                    for k in range(CH):
                        pe.wait_ge(u_ready, n.chunk(k))
                        last = nc.tensor.matmul(single[1][:, :], w_cur[0:HC, 512 + 2 * CH * HC + k * P:512 + 2 * CH * HC + (k + 1) * P],
                                                u[:, k, :], start=k == 0, stop=k == CH - 1)
                    last.then_inc(w2_ready, 1)

        @block.scalar
        def _(act):
            for s in (sq_ready, v_evicted, rn_log, rn_ready, qk_evicted, p_ready, ot_evicted):
                act.sem_inc(s, B)
            for s in (csq_ready, lv_ready, rstd_ready):
                act.sem_inc(s, 1)
            act.wait_ge(zeroed, 1)
            with act.Fori(0, LAYERS) as l:
                with act.Fori(0, NT) as t:
                    n = Count(l * NT + t)
                    nc.scalar.preload_act_table_set("natural_log_exp_and_others")

                    def squares(b):
                        act.wait_ge(qk_ready, n.cur(b))
                        act.wait_ge(ss_ready, n.prev(b + 2) if b < 2 else n.cur(b - 2))
                        nc.scalar.activation(sq[b % 2][:, :], pair(b % 2), ACT.Square).then_inc(sq_ready, 1)

                    def values(b):
                        act.wait_ge(v_ready, n.cur(b))
                        act.wait_ge(pv_ready, n.prev(b))
                        act.wait_ge(vprev_done[b], n.copied())
                        act.wait_ge(vmix_done[b], n.it * 16)
                        nc.scalar.activation(v_cur[b][:, :, 0:FD], single[b][:, :].rearrange("p (h d) -> p h d", h=FH),
                                             ACT.Copy).then_inc(v_evicted, 1)

                    def norms(b):
                        act.wait_ge(ssc_ready, n.cur(b))
                        nc.scalar.activation(log_ss[:, b, :], ssc[:, b, :], ACT.Ln).then_inc(rn_log, 1)
                        act.wait_ge(rn_log, n.cur(b))
                        act.wait_ge(qkn_ready, n.prev(b))
                        nc.scalar.activation(rnorm[:, b, :], log_ss[:, b, :], ACT.Exp, scale=-0.5).then_inc(rn_ready, 1)

                    for b in range(B):
                        squares(b)
                        values(b)
                        if b:
                            norms(b - 1)
                    norms(B - 1)
                    for b in range(B):
                        act.wait_ge(tr_ready, n.cur(b))
                        act.wait_ge(st_ready, n.prev(b))
                        act.wait_ge(kprev_done[b], n.copied())
                        kt = pair(b % 2)[:, 1, :].rearrange("p (j w i) -> p j w i", j=PAIRS, w=2)
                        nc.scalar.activation(k_blk[b][:, :, 0:2, :], kt, ACT.Copy)
                        nc.scalar.activation(k_blk[b][:, :, 2, :], kt[:, :, 0, :], ACT.Copy)
                        qt = pair(b % 2)[:, 0, :].rearrange("p (j i) -> p j i", j=PAIRS)
                        nc.scalar.activation(q_pad[b][0:64, :, 0, :], qt[0:64], ACT.Copy)
                        nc.scalar.activation(q_pad[b][64:128, :, 1, :], qt[64:128], ACT.Copy).then_inc(qk_evicted, 1)
                    for b in range(B):
                        act.wait_ge(st_ready, n.cur(b))
                        nc.scalar.activation(rot[b][:, :].rearrange("p (w n) -> p w n", w=2), pair(b % 2), ACT.Exp).then_inc(p_ready, 1)
                    for b in range(B):
                        act.wait_ge(ot_ready, n.cur(b))
                        act.wait_ge(wo_ready, n.before())
                        nc.scalar.activation(oT[:, :, b, :], single[b][:, :].rearrange("p (k t) -> p k t", k=4),
                                             ACT.Copy).then_inc(ot_evicted, 1)
                    act.wait_ge(cen_ready, n.now())
                    act.wait_ge(var_ready, n.before())
                    nc.scalar.activation(hn[:, :], single[1][:, :], ACT.Square).then_inc(csq_ready, 1)
                    act.wait_ge(var_ready, n.now())
                    nc.scalar.activation(hn[:, :], single[2][:, :], ACT.Ln, bias=m.eps[:, :]).then_inc(lv_ready, 1)
                    act.wait_ge(lv_ready, n.now())
                    act.wait_ge(hn_ready, n.before())
                    nc.scalar.activation(hn[:, :], hn[:, :], ACT.Exp, scale=-0.5).then_inc(rstd_ready, 1)
                    act.wait_ge(weights, l + 1)
                    for k in range(CH):
                        act.wait_ge(g_ready, n.chunk(k))
                        nc.scalar.activation(u[:, k, :], single[(0, 2, 0)[k]][0:HC, :], ACT.Gelu,
                                             bias=b1[:, CH + k:CH + k + 1]).then_inc(gelu_done, 1)

        @block.vector
        def _(dve):
            for s in (ss_ready, ssc_ready, rot_done, qkn_ready, max_ready, rd_ready, o_ready):
                dve.sem_inc(s, B)
            for s in (x1_done, h2_staged, hn_ready):
                dve.sem_inc(s, 1)
            dve.sem_inc(out_done, NT)
            with dve.Fori(0, LAYERS) as l:
                dve.wait_ge(w2_ready, l * NT + 1)
                dve.wait_ge(out_done, l * NT + NT)
                dve.wait_ge(zeroed, 1)
                nc.vector.tensor_copy(w_cur[:, :], m.w_all[:, bass.ds(l, 1), :].rearrange("p a n -> p (a n)"))
                nc.vector.tensor_copy(b1[:, :], m.b1_all[:, bass.ds(l, 1), :].rearrange("p a n -> p (a n)"))
                nc.vector.tensor_copy(b2[:, :], m.b2_all[:, bass.ds(l, 1)]).then_inc(weights, 1)
                nc.vector.memset(x1[:, :, P:P + 1], 0.0).then_inc(x1_zero, 1)
                with dve.Fori(0, NT) as t:
                    n = Count(l * NT + t)

                    def rotate(b):
                        qk = pair(b % 2)
                        dve.wait_ge(sq_ready, n.cur(b))
                        nc.vector.tensor_reduce(ss[:, b, :], sq[b % 2][:, :].rearrange("p (h d) -> p h d", d=FD),
                                                AX.X, ALU.add).then_inc(ss_ready, 1)
                        dve.wait_ge(ss_ready, n.cur(b))
                        dve.wait_ge(rn_log, n.prev(b))
                        nc.vector.tensor_scalar(ssc[:, b, :], ss[:, b, :], 1e-24, None, ALU.max).then_inc(ssc_ready, 1)
                        dve.wait_ge(pv_ready, n.prev(b))
                        one = m.tab[:, bass.ds(l * (2 * NT) + t, 1), :].rearrange("p a (q d) -> p (a q) d", q=2).unsqueeze(2).broadcast_to([P, 2, FH, FD])
                        nc.vector.tensor_tensor(rot[b][:, :].rearrange("p (q h d) -> p q h d", q=2, h=FH),
                                                qk.rearrange("p q (h d) -> p q h d", h=FH), one, ALU.mult)
                        dve.wait_ge(add_done, n.prev(b + 2) if b < 2 else n.cur(b - 2))
                        two = m.tab[:, bass.ds(l * (2 * NT) + t + NT, 1), :].rearrange("p a (q d) -> p (a q) d", q=2).unsqueeze(2).broadcast_to([P, 2, FH, FD])
                        dst = rot2[b % 2][:, :].rearrange("p (q h d) -> p q h d", q=2, h=FH)
                        src = qk.rearrange("p q (h d) -> p q h d", h=FH)
                        for i in range(2):
                            last = nc.vector.tensor_tensor(dst[:, :, :, 32 * i:32 * i + 32], src[:, :, :, 32 - 32 * i:64 - 32 * i],
                                                           two[:, :, :, 32 * i:32 * i + 32], ALU.mult)
                        last.then_inc(rot_done, 1)

                    def normalise(b):
                        dve.wait_ge(add_done, n.cur(b))
                        dve.wait_ge(rn_ready, n.cur(b))
                        r = rot[b][:, :].rearrange("p (h d) -> p h d", d=FD)
                        nc.vector.tensor_tensor(r, r, rnorm[:, b, :].unsqueeze(2).broadcast_to([P, 2 * FH, FD]),
                                                ALU.mult).then_inc(qkn_ready, 1)

                    for b in range(B):
                        rotate(b)
                        if b:
                            normalise(b - 1)
                    normalise(B - 1)
                    for b in range(B):
                        dve.wait_ge(s_ready, n.cur(b))
                        nc.vector.tensor_reduce(neg_max[:, b, :], pair(b % 2).rearrange("p a (h j) -> p (a h) j", h=4),
                                                AX.X, ALU.max, negate=True).then_inc(max_ready, 1)
                    for b in range(B):
                        dve.wait_ge(pv_ready, n.cur(b))
                        out = pair(b % 2)[:, :, 0:4 * (FD + 1)].rearrange("p a (h d) -> p a h d", h=4)
                        nc.vector.reciprocal(rden[:, b, :].rearrange("p (a h) -> p a h", a=2), out[:, :, :, FD]).then_inc(rd_ready, 1)
                        dve.wait_ge(rd_ready, n.cur(b))
                        nc.vector.tensor_tensor(o[b].rearrange("p (a h d) -> p a h d", a=2, h=4), out[:, :, :, 0:FD],
                                                rden[:, b, :].rearrange("p (a h) -> p a h", a=2).unsqueeze(3).broadcast_to([P, 2, 4, FD]),
                                                ALU.mult).then_inc(o_ready, 1)
                    x_in = m.xs[:, bass.ds(l, 1), :, bass.ds(t * P + 1, P)].rearrange("p a b t -> p (a b) t")
                    x_out = m.xs[:, bass.ds(1 - l, 1), :, bass.ds(t * P + 1, P)].rearrange("p a b t -> p (a b) t")
                    dve.wait_ge(wo_ready, n.now())
                    dve.wait_ge(x1_zero, l + 1)
                    dve.wait_ge(out_done, n.it + NT)
                    nc.vector.tensor_copy(x1[:, :, 0:1], x1[:, :, P:P + 1]).then_inc(x1_before, 1)
                    dve.wait_ge(x1_before, n.it + 1)
                    nc.vector.tensor_tensor(x1[:, :, 1:P + 1], single[0][:, :].rearrange("p (b t) -> p b t", b=B),
                                            x_in, ALU.add).then_inc(x1_done, 1)
                    dve.wait_ge(x1_done, n.now())
                    nc.vector.tensor_copy(h2[0:64, :, :], x1[0:64, :, 1:P + 1])
                    nc.vector.tensor_copy(h2[64:128, :, :], x1[64:128, :, 0:P]).then_inc(h2_staged, 1)
                    dve.wait_ge(rstd_ready, n.now())
                    nc.vector.tensor_tensor(hn[:, :], single[1][:, :], hn[:, :], ALU.mult).then_inc(hn_ready, 1)
                    for k in range(CH):
                        dve.wait_ge(a_ready, n.chunk(k))
                        dve.wait_ge(gelu_done, n.chunk(k))
                        nc.vector.scalar_tensor_tensor(u[:, k, :], single[(3, 1, 3)[k]][0:HC, :], b1[:, k:k + 1], u[:, k, :],
                                                       ALU.add, ALU.mult).then_inc(u_ready, 1)
                    dve.wait_ge(zeroed, 1)
                    dve.wait_ge(w2_ready, n.now())
                    nc.vector.scalar_tensor_tensor(x_out, single[1][:, :].rearrange("p (b t) -> p b t", b=B), b2[:, :],
                                                   x1[:, :, 1:P + 1], ALU.add, ALU.add).then_inc(out_done, 1)
            dve.wait_ge(out_done, NT + LAYERS * NT)
            nc.vector.scalar_tensor_tensor(m.X[:, :].rearrange("p (b t) -> p b t", b=B), m.xs[:, 0, :, 1:], 0.5,
                                           m.X[:, :].rearrange("p (b t) -> p b t", b=B), ALU.mult, ALU.add)

        @block.gpsimd
        def _(pool):
            for s in (add_done, d_ready):
                pool.sem_inc(s, B)
            for b in range(B):
                nc.gpsimd.memset(q_pad[b][:, :, :, :], 0.0)
                nc.gpsimd.memset(k_blk[b][:, :, :, :], 0.0)
                nc.gpsimd.memset(v_cur[b][:, :, :], 1.0)
                nc.gpsimd.memset(v_mix[b][:, :, :], 1.0)
            nc.gpsimd.memset(x1[:, :, :], 0.0).then_inc(zeroed, 1)
            with pool.Fori(0, LAYERS) as l:
                with pool.Fori(0, NT) as t:
                    n = Count(l * NT + t)
                    for b in range(B):
                        pool.wait_ge(rot_done, n.cur(b))
                        nc.gpsimd.tensor_tensor(rot[b][:, :], rot[b][:, :], rot2[b % 2][:, :], ALU.add).then_inc(add_done, 1)
                    for b in range(B):
                        pool.wait_ge(max_ready, n.cur(b))
                        nc.gpsimd.tensor_tensor(diag[b][:, :, :], neg_max[:, b, :].unsqueeze(2).broadcast_to([P, FH, WIN]),
                                                m.id64[:, :].unsqueeze(1).broadcast_to([P, FH, WIN]), ALU.mult).then_inc(d_ready, 1)

        @block.sync
        def _(sp):
            with sp.Fori(0, LAYERS) as l:
                with sp.Fori(0, NT) as t:
                    n = Count(l * NT + t)
                    sp.lower_val(n.it + 1)
                    sp.wait_ge(zeroed, 1)
                    sp.wait_ge(v_ready, n.prev(B - 1))
                    sp.wait_ge(out_done, n.it + 1)
                    for half in range(2):
                        rows = slice(64 * half, 64 * half + 64)
                        sp.dma_start(hT[rows, :, :], m.xs[rows, bass.ds(l, 1), :, bass.ds(t * P + (1 - half), P)]
                                     .rearrange("p a b t -> p (a b) t")).then_inc(ht_staged, 16)
                    for b in range(B):
                        sp.wait_ge(st_ready, n.prev(b))
                        sp.dma_start(k_blk[b][:, :, 3, :], k_blk[b][:, :, 1, :]).then_inc(kprev_done[b], 16)
                        sp.wait_ge(pv_ready, n.prev(b))
                        sp.dma_start(v_mix[b][64:128, :, :], v_cur[b][64:128, :, :]).then_inc(vprev_done[b], 16)
                    for b in range(B):
                        sp.wait_ge(v_evicted, n.cur(b))
                        sp.dma_start(v_mix[b][0:64, :, :], v_cur[b][0:64, :, :]).then_inc(vmix_done[b], 16)

def binarise_phase(nc, m, a):
    ctx = ExitStack()
    with ctx:
        def sb(n, shape, dt=FP32):
            return ctx.enter_context(nc.sbuf_tensor(f"bin_{n}", shape, dt))

        def sem(n):
            return semaphore(nc, m, ctx, f"bin_{n}")

        w = sb("w", [P, 4, C])
        positive = sb("positive", [P, 4, C])
        neg_sign = sb("neg_sign", [P, 4, C])
        total = sb("total", [P, 4])
        loaded, summed, signs, scaled, turned = (sem(s) for s in ("loaded", "summed", "signs", "scaled", "turned"))
        ctx.enter_context(nc.allow_non_contiguous_dma(reason="a few columns of parameters"))
        block = ctx.enter_context(nc.Block())

        @block.sync
        def _(sp):
            for i, name in enumerate(("Wq", "Wk", "Wv", "Wp")):
                sp.dma_start(w[:, i, :], a["L0_attn_" + name]).then_inc(loaded, 16)
            for i, name in enumerate(("bq", "bk", "bp")):
                sp.dma_start(m.att_bias[:, i:i + 1], a["L0_attn_" + name].rearrange("(p a) -> p a", a=1)).then_inc(loaded, 16)
            sp.dma_start(m.bv_row[:, :], a["L0_attn_bv"].rearrange("(a n) -> a n", a=1).broadcast_to([P, C])).then_inc(loaded, 16)
            sp.wait_ge(loaded, 16 * 8)

        @block.vector
        def _(dve):
            dve.wait_ge(loaded, 16 * 8)
            nc.vector.tensor_reduce(total[:, :], w[:, :, :], AX.X, ALU.add, apply_absolute_value=True)
            nc.vector.tensor_scalar(positive[:, :, :], w[:, :, :], 0.0, None, ALU.is_gt).then_inc(summed, 1)
            dve.wait_ge(summed, 1)
            nc.vector.scalar_tensor_tensor(neg_sign[:, :, :], w[:, :, :], 0.0, positive[:, :, :],
                                           ALU.is_lt, ALU.subtract).then_inc(signs, 1)
            dve.wait_ge(signs, 1)
            for i in range(4):
                last = nc.vector.tensor_scalar(w[:, i, :], neg_sign[:, i, :], total[:, i:i + 1], -1.0 / C, ALU.mult, ALU.mult)
            last.then_inc(scaled, 1)
            dve.wait_ge(turned, 1)
            nc.vector.tensor_copy(m.att_w[:, :, :], m.bank[0][:, :].rearrange("p (i o) -> p i o", i=4))

        @block.tensor
        def _(pe):
            pe.wait_ge(scaled, 1)
            for i in range(4):
                last = nc.tensor.transpose(m.bank[0][:, i * P:(i + 1) * P], w[:, i, :], m.ident[:, :])
            last.then_inc(turned, 1)


def project_phase(nc, m, V, scratch):
    N = B * T // 512
    ctx = ExitStack()
    with ctx:
        def sb(n, shape, dt=FP32):
            return ctx.enter_context(nc.sbuf_tensor(f"prj_{n}", shape, dt))

        def sem(n):
            return semaphore(nc, m, ctx, f"prj_{n}")

        parts = sb("parts", [P, 2, PARTS, 512], BF16)
        rest = sb("rest", [P, 2, 512])
        qk_ready, part1, rest_ready, part2, part3, v_ready, v_done = (
            sem(s) for s in ("qk_ready", "part1", "rest_ready", "part2", "part3", "v_ready", "v_done"))
        stored = [sem(f"stored{i}") for i in range(2)]
        block = ctx.enter_context(nc.Block())

        def stream(n):
            return m.xs[:, 0, n // 2, 1 + (n % 2) * 512:1 + (n % 2 + 1) * 512]

        @block.tensor
        def _(pe):
            for u in range(2 * N):
                if u >= 4:
                    pe.wait_ge(rest_ready, u - 3)
                nc.tensor.matmul(m.bank[u % 4][:, :], m.att_w[:, u % 2, :], stream(u // 2),
                                 start=True, stop=True).then_inc(qk_ready, 1)
                if u % 2:
                    n = u // 2
                    if n >= 4:
                        pe.wait_ge(v_done, n - 3)
                    for i in range(4):
                        last = nc.tensor.matmul(m.bank[4 + n % 4][:, i * P:(i + 1) * P], stream(n)[:, i * P:(i + 1) * P],
                                                m.att_w[:, 2, :], start=True, stop=True)
                    last.then_inc(v_ready, 1)

        @block.scalar
        def _(act):
            for u in range(2 * N):
                act.wait_ge(qk_ready, u + 1)
                if u >= 2:
                    act.wait_ge(stored[u % 2], 16 * PARTS * (u // 2))
                nc.scalar.activation(parts[:, u % 2, 0, :], m.bank[u % 4][:, :], ACT.Identity,
                                     bias=m.att_bias[:, u % 2:u % 2 + 1]).then_inc(part1, 1)

        @block.vector
        def _(dve):
            for u in range(2 * N):
                dve.wait_ge(part1, u + 1)
                if u >= 2:
                    dve.wait_ge(part3, u - 1)
                nc.vector.scalar_tensor_tensor(rest[:, u % 2, :], m.bank[u % 4][:, :], m.att_bias[:, u % 2:u % 2 + 1],
                                               parts[:, u % 2, 0, :], ALU.add, ALU.subtract).then_inc(rest_ready, 1)
                dve.wait_ge(rest_ready, u + 1)
                nc.vector.tensor_copy(parts[:, u % 2, 1, :], rest[:, u % 2, :]).then_inc(part2, 1)
                if u % 2:
                    n = u // 2
                    dve.wait_ge(v_ready, n + 1)
                    nc.vector.tensor_tensor(V[:, 4 * n:4 * n + 4, :], m.bank[4 + n % 4][:, :].rearrange("p (i o) -> p i o", i=4),
                                            m.bv_row[:, :].unsqueeze(1).broadcast_to([P, 4, C]), ALU.add).then_inc(v_done, 1)

        @block.gpsimd
        def _(pool):
            for u in range(2 * N):
                pool.wait_ge(part2, u + 1)
                nc.gpsimd.tensor_tensor(parts[:, u % 2, 2, :], rest[:, u % 2, :], parts[:, u % 2, 1, :],
                                        ALU.subtract).then_inc(part3, 1)

        @block.sync
        def _(sp):
            for u in range(2 * N):
                sp.wait_ge(part3, u + 1)
                n = u // 2
                for i in range(PARTS):
                    dst = scratch[u % 2, n // 2, i, :, :, (n % 2) * 512:(n % 2 + 1) * 512].rearrange("d h t -> h d t")
                    sp.dma_start(dst, parts[:, u % 2, i, :]).then_inc(stored[u % 2], 16)
            for which in range(2):
                sp.wait_ge(stored[which], 16 * PARTS * N)


LEAD = 12
UNITS = 64
STEPS = 16
SLOTS = 3
ROWS = 96


def attention_phase(nc, m, a, V, Y, scratch, m_scratch):
    ctx = ExitStack()
    with ctx:
        def sb(n, shape, dt=FP32):
            return ctx.enter_context(nc.sbuf_tensor(f"att_{n}", shape, dt))

        def sem(n):
            return semaphore(nc, m, ctx, f"att_{n}")

        Q = [sb(f"Q{s}", [ROWS, 4, T], BF16) for s in range(SLOTS)]
        K = [sb(f"K{s}", [ROWS, 4, T], BF16) for s in range(SLOTS)]
        vq = [sb(f"vq{s}", [P, NT, 4, DH + 1]) for s in range(SLOTS)]
        probs = [sb(f"probs{r}", [P, 4, 512]) for r in range(2)]
        neg_half = sb("neg_half", [P, 32, 2])
        neg_max = sb("neg_max", [P, 32])
        m_rows = sb("m_rows", [32, P], BF16)
        o_sb = sb("o_sb", [P, 2, 512])
        rden = sb("rden", [P, 2, 4, 4])

        (set_up, ring_filled, ring_freed, combined, rows_out, rows_in, e_filled, e_done, av_done,
         o_evicted, rd_ready, v_staged) = (sem(s) for s in (
             "set_up", "ring_filled", "ring_freed", "combined", "rows_out", "rows_in", "e_filled",
             "e_done", "av_done", "o_evicted", "rd_ready", "v_staged"))
        stack_in = [sem(f"stack_in{s}") for s in range(SLOTS)]
        LOADS = 2 * PARTS + 1
        block = ctx.enter_context(nc.Block())

        ring = m.bank[0:3]
        O = m.bank[7]

        def e_slot(e):
            return m.psum[:, 3 + 2 * e:5 + 2 * e, :]

        def ring_uses(ahead):
            uses = [[] for _ in range(STEPS + 1)]
            for u in range(UNITS):
                k = LEAD + u
                if ahead:
                    uses[u // 4].append(("max", 1 + k // UNITS, k % UNITS))
                    if k == UNITS - 1:
                        uses[u // 4].append(("rows", 1))
            uses[10].append(("out", 0))
            uses[STEPS].append(("out", 1))
            return uses

        USES = UNITS + 3
        BEFORE = UNITS + 1 + LEAD
        first_uses = [("max", 0, u) for u in range(UNITS)] + [("rows", 0)] + [("max", 1, u) for u in range(LEAD)]

        class Quad:

            def __init__(self, i, c):
                self.i, self.c = i, c
                self.n = i * SLOTS + c

            def slot(self, ahead=0):
                return (self.c + ahead) % SLOTS

            def stack(self, ahead):
                return self.i * (16 * LOADS) + 16 * LOADS * ((self.c + ahead) // SLOTS + 1)

            def ring(self, local):
                return self.i * (SLOTS * USES) + (BEFORE + self.c * USES + local + 1)

            def bank(self, local):
                return ring[(BEFORE + self.c * USES + local) % 3]

            def step(self, u):
                return self.i * (SLOTS * STEPS) + (self.c * STEPS + u + 1)

            def pairs(self, u, e):
                return self.i * (SLOTS * STEPS * 2) + ((self.c * STEPS + u) * 2 + e + 1)

            def half(self, qc):
                return self.i * (SLOTS * 2) + (self.c * 2 + qc + 1)

        def body(engine, turn):
            with engine.Fori(0, (B * QUADS - 1) // SLOTS) as i:
                for c in range(SLOTS):
                    turn(Quad(i, c), True)
            turn(Quad((B * QUADS - 1) // SLOTS, 0), False)

        @block.tensor
        def _(pe):
            def fill(use, q, bank, freed):
                if freed is not None:
                    pe.wait_ge(ring_freed, freed)
                if use[0] == "max":
                    _, ahead, u = use
                    h, qt, kc = u // 16, u // 2 % 8, u % 2
                    if u == 0:
                        pe.wait_ge(stack_in[q.slot(ahead)], q.stack(ahead))
                    last = nc.tensor.matmul(bank[:, :], Q[q.slot(ahead)][:, h, qt * P:(qt + 1) * P],
                                            K[q.slot(ahead)][:, h, kc * 512:(kc + 1) * 512], start=True, stop=True)
                elif use[0] == "rows":
                    pe.wait_ge(combined, q.n + use[1] + 1)
                    last = nc.tensor.transpose(bank[0:32, 0:P], neg_max[:, :], m.ident[:, :])
                else:
                    pe.wait_ge(o_evicted, q.half(use[1]) + 1)
                    for i in range(4):
                        last = nc.tensor.transpose(bank[:, i * P:(i + 1) * P], o_sb[:, use[1], i * P:(i + 1) * P], m.ident[:, :])
                last.then_inc(ring_filled, 1)

            pe.wait_ge(set_up, 2)
            start = Quad(0, 0)
            for k, use in enumerate(first_uses):
                fill(use, start, ring[k % 3], k - 2 if k >= 3 else None)

            def turn(q, ahead):
                uses = ring_uses(ahead)
                local = 0
                s = q.slot()
                pe.wait_ge(rows_in, q.n * 16 + 16)
                pe.wait_ge(v_staged, q.n + 1)

                def products(u):
                    qc, kt = u // NT, u % NT
                    if kt == 0:
                        pe.wait_ge(o_evicted, q.half(qc))
                    pe.wait_ge(e_done, q.pairs(u, 1) + 2)
                    for h in range(4):
                        last = nc.tensor.matmul(O[32 * h:32 * h + DH + 1, :], vq[s][:, kt, h, :], probs[u % 2][:, h, :],
                                                start=kt == 0, stop=kt == NT - 1)
                    last.then_inc(av_done, 1)

                for u in range(STEPS):
                    qc, kt = u // NT, u % NT
                    for e in range(2):
                        pe.wait_ge(e_done, q.pairs(u, e))
                        for h in (2 * e, 2 * e + 1):
                            last = nc.tensor.matmul(e_slot(e)[:, h % 2, :], K[s][:, h, kt * P:(kt + 1) * P],
                                                    Q[s][:, h, qc * 512:(qc + 1) * 512], start=True, stop=True)
                        last.then_inc(e_filled, 1)
                    for k, use in enumerate(uses[u]):
                        if k == 2 and u:
                            products(u - 1)
                        fill(use, q, q.bank(local), q.ring(local) - 3)
                        local += 1
                    if len(uses[u]) < 3 and u:
                        products(u - 1)
                products(STEPS - 1)
                for use in uses[STEPS]:
                    fill(use, q, q.bank(local), q.ring(local) - 3)
                    local += 1

            body(pe, turn)

        @block.scalar
        def _(act):
            def turn(q, ahead):
                def evict(qc):
                    act.wait_ge(av_done, q.step(NT * qc + NT - 1) + 2)
                    act.wait_ge(rd_ready, q.half(qc))
                    nc.scalar.activation(o_sb[:, qc, :], O[:, :], ACT.Copy).then_inc(o_evicted, 1)

                for u in range(STEPS):
                    for e in range(2):
                        act.wait_ge(e_filled, q.pairs(u, e))
                        if e == 0:
                            act.wait_ge(av_done, q.step(u))
                        nc.scalar.activation(probs[u % 2][:, 2 * e:2 * e + 2, :], e_slot(e), ACT.Exp,
                                             scale=float(DH) ** -0.5).then_inc(e_done, 1)
                    if u == NT:
                        evict(0)
                evict(1)

            act.sem_inc(e_done, 2)
            act.sem_inc(av_done, 2)
            act.sem_inc(rd_ready, 2)
            act.sem_inc(o_evicted, 1)
            body(act, turn)

        @block.vector
        def _(dve):
            def drain(use, q, bank, filled):
                dve.wait_ge(ring_filled, filled)
                if use[0] == "max":
                    _, ahead, u = use
                    h, qt, kc = u // 16, u // 2 % 8, u % 2
                    last = nc.vector.tensor_reduce(neg_half[:, h * 8 + qt, kc:kc + 1], bank[:, :], AX.X, ALU.max, negate=True)
                elif use[0] == "rows":
                    last = nc.vector.tensor_copy(m_rows[:, :], bank[0:32, 0:P])
                else:
                    out = bank[:, :].rearrange("p (i g r) -> p i g r", i=4, g=4)
                    nc.vector.reciprocal(rden[:, use[1], :, :], out[:, :, :, DH]).then_inc(rd_ready, 1)
                    dve.wait_ge(rd_ready, q.half(use[1]) + 2)
                    b, j = q.n // QUADS, q.n % QUADS
                    dst = Y[:, bass.ds(b * NT + 4 * use[1], 4), bass.ds(j * 32, 32)].rearrange("p i (g d) -> p i g d", g=4)
                    last = nc.vector.tensor_tensor(dst, out[:, :, :, 0:DH], rden[:, use[1], :, :].unsqueeze(3).broadcast_to([P, 4, 4, DH]), ALU.mult)
                last.then_inc(ring_freed, 1)

            def combine(q, ahead, uses_done):
                dve.wait_ge(ring_freed, uses_done)
                nc.vector.tensor_tensor(neg_max[:, :], neg_half[:, :, 0], neg_half[:, :, 1], ALU.min).then_inc(combined, 1)

            def stage(q, ahead):
                k = q.n + ahead
                src = V[:, bass.ds(k // QUADS * NT, NT), bass.ds(k % QUADS * 32, 32)].rearrange("p t (h d) -> p t h d", h=4)
                nc.vector.tensor_copy(vq[q.slot(ahead)][:, :, :, 0:DH], src).then_inc(v_staged, 1)

            start = Quad(0, 0)
            for s in range(SLOTS):
                nc.vector.memset(vq[s][:, :, :, :], 1.0)
            nc.vector.memset(O[:, :], 0.0).then_inc(set_up, 1)
            dve.wait_ge(set_up, 2)
            stage(start, 0)
            for k, use in enumerate(first_uses):
                if use[0] == "rows":
                    combine(start, 0, k)
                drain(use, start, ring[k % 3], k + 1)

            def turn(q, ahead):
                local = 0
                if ahead:
                    stage(q, 1)
                for step in ring_uses(ahead):
                    for use in step:
                        if use[0] == "rows":
                            combine(q, 1, q.ring(local) - 1)
                        drain(use, q, q.bank(local), q.ring(local))
                        local += 1

            body(dve, turn)

        @block.gpsimd
        def _(pool):
            for s in range(SLOTS):
                nc.gpsimd.memset(Q[s][64:ROWS, :, :], 0.0)
                last = nc.gpsimd.memset(K[s][64:ROWS, :, :], 1.0)
            last.then_inc(set_up, 1)

        @block.sync
        def _(sp):
            def load(slot, b, j):
                for i in range(PARTS):
                    rows = slice(i * PARTS * DH, (i + 1) * PARTS * DH)
                    src_q = scratch_quad(0, b, j)[i:i + 1].broadcast_to([PARTS, DH, 4 * T])
                    src_k = scratch_quad(1, b, j)
                    sp.dma_start(Q[slot][rows, :, :].rearrange("p h t -> p (h t)"), src_q).then_inc(stack_in[slot], 16)
                    sp.dma_start(K[slot][rows, :, :].rearrange("p h t -> p (h t)"), src_k).then_inc(stack_in[slot], 16)
                sp.dma_start(Q[slot][KROWS:KROWS + 1, :, :].rearrange("p h t -> p (h t)"), a["zeros"].bitcast(BF16)).then_inc(stack_in[slot], 16)

            def scratch_quad(which, b, j):
                if isinstance(b, int):
                    v = scratch[which, b:b + 1, :, :, 4 * j:4 * j + 4, :]
                else:
                    v = scratch[which, bass.ds(b, 1), :, :, bass.ds(j * 4, 4), :]
                return v.rearrange("a i d h t -> (a i) d (h t)")

            def rows(count, slot, written):
                sp.wait_ge(ring_freed, written)
                sp.dma_start(m_scratch, m_rows[:, :]).then_inc(rows_out, 16)
                sp.wait_ge(rows_out, count * 16)
                sp.dma_start(Q[slot][KROWS:KROWS + 1, :, :].rearrange("p h t -> p (h t)"),
                             m_scratch.rearrange("(a r) q -> a (r q)", a=1)).then_inc(rows_in, 16)

            sp.wait_ge(set_up, 2)
            load(0, 0, 0)
            load(1, 0, 1)
            rows(1, 0, UNITS + 1)

            def turn(q, ahead):
                if not ahead:
                    return
                k = (q.n + 2) % (B * QUADS)
                sp.wait_ge(ring_freed, q.ring(-1))
                load(q.slot(2), k // QUADS, k % QUADS)
                order = [use[0] for step in ring_uses(True) for use in step]
                rows(q.n + 2, q.slot(1), q.ring(order.index("rows")))

            body(sp, turn)


def output_phase(nc, m, Y):
    N = B * T // 512
    ctx = ExitStack()
    with ctx:
        def sem(n):
            return semaphore(nc, m, ctx, f"outp_{n}")

        yT = ctx.enter_context(nc.sbuf_tensor("outp_yT", [P, 2, 512], FP32))
        turned, evicted, projected, added = (sem(s) for s in ("turned", "evicted", "projected", "added"))
        block = ctx.enter_context(nc.Block())

        @block.tensor
        def _(pe):
            for n in range(N + 1):
                if n < N:
                    if n >= 2:
                        pe.wait_ge(evicted, n - 1)
                    for i in range(4):
                        last = nc.tensor.transpose(m.bank[n % 2][:, i * P:(i + 1) * P], Y[:, 4 * n + i, :], m.ident[:, :])
                    last.then_inc(turned, 1)
                if n >= 1:
                    k = n - 1
                    pe.wait_ge(evicted, k + 1)
                    if k >= 2:
                        pe.wait_ge(added, k - 1)
                    nc.tensor.matmul(m.bank[2 + k % 2][:, :], m.att_w[:, 3, :], yT[:, k % 2, :],
                                     start=True, stop=True).then_inc(projected, 1)

        @block.scalar
        def _(act):
            for n in range(N):
                act.wait_ge(turned, n + 1)
                if n >= 2:
                    act.wait_ge(projected, n - 1)
                nc.scalar.activation(yT[:, n % 2, :], m.bank[n % 2][:, :], ACT.Copy).then_inc(evicted, 1)

        @block.vector
        def _(dve):
            for n in range(N):
                x = m.X[:, n * 512:(n + 1) * 512]
                dve.wait_ge(projected, n + 1)
                nc.vector.scalar_tensor_tensor(x, m.bank[2 + n % 2][:, :], m.att_bias[:, 2:3], x,
                                               ALU.add, ALU.add).then_inc(added, 1)


def store_phase(nc, m, a):
    ctx = ExitStack()
    with ctx:
        rows = ctx.enter_context(nc.sbuf_tensor("st_rows", [P, B * NT, C], FP32))
        back = semaphore(nc, m, ctx, "st_back")
        evicted = semaphore(nc, m, ctx, "st_evicted")
        stored = semaphore(nc, m, ctx, "st_stored")
        block = ctx.enter_context(nc.Block())
        N = B * NT // 4

        @block.tensor
        def _(pe):
            for n in range(N):
                if n >= 4:
                    pe.wait_ge(evicted, n - 3)
                for i in range(4):
                    last = nc.tensor.transpose(m.bank[n % 4][:, i * P:(i + 1) * P], m.X[:, (4 * n + i) * P:(4 * n + i + 1) * P], m.ident[:, :])
                last.then_inc(back, 1)

        @block.vector
        def _(dve):
            for n in range(N):
                dve.wait_ge(back, n + 1)
                nc.vector.tensor_copy(rows[:, 4 * n:4 * n + 4, :], m.bank[n % 4][:, :].rearrange("p (i c) -> p i c", i=4)).then_inc(evicted, 1)

        @block.sync
        def _(sp):
            for b in range(B):
                sp.wait_ge(evicted, (b + 1) * NT // 4)
                sp.dma_start(a["out"][b].rearrange("(t p) c -> p t c", p=P), rows[:, b * NT:(b + 1) * NT, :]).then_inc(stored, 16)
            sp.wait_ge(stored, 16 * B)


def build(nc, a):
    ctx = ExitStack()
    with ctx:
        m = Memory()

        def sb(name, shape, dt=FP32):
            return ctx.enter_context(nc.sbuf_tensor(name, shape, dt))

        m.w_cols = 512 + 2 * CH * HC + CH * P
        m.psum = ctx.enter_context(nc.psum_tensor("psum", [P, 8, 512], FP32))
        m.bank = [m.psum[:, i, :] for i in range(8)]
        m.X = sb("X", [P, B * T])
        m.xs = sb("xs", [P, 2, B, T + 1])
        m.wqkv = sb("wqkv", [P, LAYERS, 3 * INNER])
        m.w_all = sb("w_all", [P, LAYERS, m.w_cols])
        m.b1_all = sb("b1_all", [HC, LAYERS, 2 * CH])
        m.b2_all = sb("b2_all", [P, LAYERS])
        m.tab = sb("tab", [P, LAYERS * 2 * NT, 2 * FD])
        m.ident = sb("ident", [P, P])
        m.centre = sb("centre", [P, P])
        m.mean_ones = sb("mean_ones", [P, P])
        m.eps = sb("eps", [P, 1])
        m.ident_b = sb("ident_b", [P, P], BF16)
        m.id64 = sb("id64", [P, WIN])
        m.sel_w = sb("sel_w", [P, 2, P], BF16)
        m.mask_q = sb("mask_q", [P, 2, P], BF16)
        m.mask_k = sb("mask_k", [P, 3, WIN], BF16)
        scratch = nc.dram_tensor("qk_parts", (2, B, PARTS, DH, H, T), BF16, kind="Internal").ap()
        m_scratch = nc.dram_tensor("maxima", (32, P), BF16, kind="Internal").ap()

        def stream(n):
            return m.xs[:, 0, n // 2, 1 + (n % 2) * 512:1 + (n % 2 + 1) * 512]

        setup_phase(nc, m, a)
        clear_semaphores(nc, m)
        layernorm_phase(nc, m, "ln0", stream)
        clear_semaphores(nc, m)
        ffn_phase(nc, m, "f0")
        clear_semaphores(nc, m)
        layernorm_phase(nc, m, "ln1", stream)
        clear_semaphores(nc, m)
        with ExitStack() as branch:
            m.att_w, m.att_bias, m.bv_row, V, Y = (
                branch.enter_context(nc.sbuf_tensor(name, shape, FP32)) for name, shape in (
                    ("att_w", [P, 4, C]), ("att_bias", [P, 3]), ("bv_row", [P, C]),
                    ("V", [P, B * NT, C]), ("Y", [P, B * NT, C])))
            binarise_phase(nc, m, a)
            clear_semaphores(nc, m)
            project_phase(nc, m, V, scratch)
            clear_semaphores(nc, m)
            attention_phase(nc, m, a, V, Y, scratch, m_scratch)
            clear_semaphores(nc, m)
            output_phase(nc, m, Y)
            clear_semaphores(nc, m)
        layernorm_phase(nc, m, "ln2", stream)
        clear_semaphores(nc, m)
        ffn_phase(nc, m, "f1")
        clear_semaphores(nc, m)
        store_phase(nc, m, a)


def host_constants():
    return {"rot": rotary_tables(), "consts": constants(), "zeros": np.zeros((1, 4 * T // 2), np.float32)}


INPUTS = ("L0_attn_x", "L0_attn_Wq", "L0_attn_bq", "L0_attn_Wk", "L0_attn_bk", "L0_attn_Wv", "L0_attn_bv",
          "L0_attn_Wp", "L0_attn_bp", "L0_ffn_wqkv", "L0_ffn_q_scale", "L0_ffn_k_scale", "L0_ffn_wo",
          "L0_ffn_ln_g", "L0_ffn_ln_b", "L0_ffn_w1", "L0_ffn_b1", "L0_ffn_w2", "L0_ffn_b2")


def kernel(**inputs):
    import concourse.bacc as bacc
    from concourse.bass_utils import run_bass_kernel_spmd

    nc = bacc.Bacc("TRN2", target_bir_lowering=False, num_devices=1)
    arrays = {name: np.ascontiguousarray(inputs[name]) for name in INPUTS}
    arrays.update(host_constants())
    a = {name: nc.dram_tensor(f"in_{name}", v.shape, mybir.dt.from_np(v.dtype), kind="ExternalInput").ap()
         for name, v in arrays.items()}
    a["out"] = nc.dram_tensor("out", (B, T, C), FP32, kind="ExternalOutput").ap()
    build(nc, a)
    r = run_bass_kernel_spmd(nc, [{f"in_{name}": v for name, v in arrays.items()}], core_ids=[0])
    return r.results[0]["out"]
```

```python
from contextlib import ExitStack

import numpy as np

import concourse.bass as bass
from concourse import mybir

FP32 = mybir.dt.float32
BF16 = mybir.dt.bfloat16
ALU = mybir.AluOpType
ACT = mybir.ActivationFunctionType
AX = mybir.AxisListType

P = 128
B, T, C = 4, 1024, 128
NT = T // P
LAYERS = 2
FH, FD, WIN = 8, 64, 64
PAIRS = FH // 2
INNER = FH * FD
HID = int(C * 4 * 2 / 3)
CH = 3
HC = -(-HID // CH)
QK_SCALE = 8.0
H, DH = 16, 8
QUADS = H // 4
PARTS = 3
KROWS = PARTS * PARTS * DH
MASKED = -1e30


def rotary_tables():
    half = np.arange(0, FD, 2, dtype=np.float32)
    inv = (np.float32(1.0) / np.float32(10000.0) ** (half / np.float32(FD))).astype(np.float32)
    t = np.arange(T, dtype=np.float32)
    freqs = (t[:, None] * inv[None, :]).astype(np.float32)
    freqs = np.concatenate([freqs, freqs], axis=-1)
    base = ((half + np.float32(0.4 * FD)) / np.float32(1.4 * FD)).astype(np.float32)
    power = ((t - T // 2) / np.float32(WIN // 2)).astype(np.float32)
    scale = (base[None, :].astype(np.float64) ** power[:, None]).astype(np.float32)
    scale = np.concatenate([scale, scale], axis=-1)
    cos, sin = np.cos(freqs), np.sin(freqs)
    sign = np.concatenate([-np.ones(FD // 2), np.ones(FD // 2)]).astype(np.float32)
    out = np.empty((2, T, 2, FD), np.float32)
    out[0, :, 0] = cos * scale * np.float32(QK_SCALE)
    out[1, :, 0] = sin * scale * sign * np.float32(QK_SCALE)
    out[0, :, 1] = cos / scale
    out[1, :, 1] = sin / scale * sign
    return np.ascontiguousarray(out.reshape(2, NT, P, 2, FD).transpose(0, 2, 1, 3, 4))


C_ID, C_CENTRE, C_MASK_Q = 0, P, 2 * P
C_MASK_K = C_MASK_Q + 4 * P
C_END = C_MASK_K + 3 * WIN


def constants():
    c = np.zeros((P, C_END), np.float32)
    c[:, C_ID:C_ID + P] = np.eye(P)
    c[:, C_CENTRE:C_CENTRE + P] = np.eye(P) - 1.0 / P
    i, j = np.arange(WIN)[:, None], np.arange(WIN)[None]
    causal, back = j <= i, i <= j
    rows = np.empty((2, 2, WIN, P), np.float32)
    for later in range(2):
        rows[later, 0] = np.concatenate([np.where(causal, 0, MASKED), np.where(back & bool(later), 0, MASKED)], axis=1)
        rows[later, 1] = np.concatenate([np.where(back, 0, MASKED), np.where(causal, 0, MASKED)], axis=1)
    for head in range(2):
        c[head * WIN:(head + 1) * WIN, C_MASK_Q:C_MASK_K] = rows.transpose(2, 0, 1, 3).reshape(WIN, 4 * P)
    for k, mask in enumerate((rows[0, 0], rows[1, 0], rows[1, 1])):
        c[:, C_MASK_K + k * WIN:C_MASK_K + (k + 1) * WIN] = mask.T
    return c


class Memory:

    def __init__(self):
        self.used_semaphores = []


def semaphore(nc, m, ctx, name):
    handle = ctx.enter_context(nc.semaphore(name))
    m.used_semaphores.append(handle)
    return handle


def clear_semaphores(nc, m):
    for handle in m.used_semaphores:
        nc.sync.sem_clear(handle)
    m.used_semaphores.clear()
    nc.all_engine_barrier()


def setup_phase(nc, m, a):
    ctx = ExitStack()
    with ctx:
        def sb(name, shape, dt=FP32):
            return ctx.enter_context(nc.sbuf_tensor(name, shape, dt))

        def sem(name):
            return semaphore(nc, m, ctx, name)

        x_rows = sb("su_x_rows", [P, B * NT, C])
        consts = sb("su_consts", [P, C_END])
        base = sb("su_base", [P, 2, NT, 2, FD])
        scales = sb("su_scales", [P, 2, LAYERS, 2, FD])
        ln_g = sb("su_ln_g", [P, LAYERS])
        ln_b = sb("su_ln_b", [P, LAYERS])
        b1_raw = sb("su_b1_raw", [HC, LAYERS, 2 * CH])

        zeroed = sem("su_zeroed")
        x_in = sem("su_x_in")
        c_in = sem("su_c_in")
        w_in = sem("su_w_in")
        t_in = sem("su_t_in")
        ready = sem("su_ready")
        x_tr = sem("su_x_tr")
        x_ev = sem("su_x_ev")
        bias_mm = sem("su_bias_mm")
        bias_done = sem("su_bias_done")
        tables = sem("su_tables")
        ctx.enter_context(nc.allow_non_contiguous_dma(reason="a few columns of parameters"))
        block = ctx.enter_context(nc.Block())

        w1_jobs = []
        for l in range(LAYERS):
            for k in range(2 * CH):
                lo = (k // CH) * HID + (k % CH) * HC
                w1_jobs.append((l, k, lo, min(HC, HID - (k % CH) * HC)))

        @block.sync
        def _(sp):
            sp.dma_start(consts[:, :], a["consts"]).then_inc(c_in, 16)
            for b in range(B):
                sp.dma_start(x_rows[:, b * NT:(b + 1) * NT, :],
                             a["L0_attn_x"][b].rearrange("(t p) c -> p t c", p=P)).then_inc(x_in, 16)
            sp.wait_ge(zeroed, 1)
            for l, k, lo, n in w1_jobs:
                sp.dma_start(m.w_all[:, l, 512 + k * HC:512 + k * HC + n],
                             a["L0_ffn_w1"][l, :, lo:lo + n]).then_inc(w_in, 16)
            for l in range(LAYERS):
                for k in range(CH):
                    n = min(HC, HID - k * HC)
                    o = 512 + 2 * CH * HC + k * P
                    sp.dma_start(m.w_all[0:n, l, o:o + P],
                                 a["L0_ffn_w2"][l, k * HC:k * HC + n, :]).then_inc(w_in, 16)
                sp.dma_start(m.w_all[:, l, 0:512].rearrange("p (k c) -> p k c", k=4),
                             a["L0_ffn_wo"][l].rearrange("(k p) c -> p k c", p=P)).then_inc(w_in, 16)
            sp.wait_ge(w_in, 16 * (len(w1_jobs) + LAYERS * (CH + 1)))

        @block.gpsimd
        def _(pool):
            nc.gpsimd.memset(m.w_all[:, :, 512:], 0.0)
            nc.gpsimd.memset(b1_raw[:, :, :], 0.0)
            nc.gpsimd.memset(m.xs[:, :, :, 0:1], 0.0)
            nc.gpsimd.memset(m.eps[:, :], 1e-5)
            nc.gpsimd.memset(m.mean_ones[:, :], 1.0 / C).then_inc(zeroed, 1)

        @block.scalar
        def _(act):
            act.wait_ge(zeroed, 1)
            for l in range(LAYERS):
                for q, name in enumerate(("L0_ffn_q_scale", "L0_ffn_k_scale")):
                    row = a[name][l:l + 1, :]
                    act.dma_start(scales[:, 0, l, q, :], row.broadcast_to([P, FD])).then_inc(t_in, 16)
                    for h in range(2):
                        o = 32 * h
                        act.dma_start(scales[:, 1, l, q, 32 - o:64 - o],
                                      row[:, o:o + 32].broadcast_to([P, 32])).then_inc(t_in, 16)
            act.dma_start(base[:, :, :, :, :], a["rot"].rearrange("a p t q d -> p a t q d")).then_inc(t_in, 16)
            act.dma_start(ln_g[:, :], a["L0_ffn_ln_g"].rearrange("l p -> p l")).then_inc(t_in, 16)
            act.dma_start(ln_b[:, :], a["L0_ffn_ln_b"].rearrange("l p -> p l")).then_inc(t_in, 16)
            act.dma_start(m.b2_all[:, :], a["L0_ffn_b2"].rearrange("l p -> p l")).then_inc(t_in, 16)
            for l, k, lo, n in w1_jobs:
                act.dma_start(b1_raw[0:n, l, k:k + 1],
                              a["L0_ffn_b1"][l:l + 1, lo:lo + n].rearrange("a p -> p a")).then_inc(t_in, 16)
            act.dma_start(m.wqkv[:, :, :], a["L0_ffn_wqkv"].rearrange("l p n -> p l n")).then_inc(t_in, 16)
            for n in range(B * NT // 4):
                act.wait_ge(x_tr, n + 1)
                nc.scalar.activation(m.X[:, n * 512:(n + 1) * 512], m.bank[n % 4][:, :], ACT.Copy).then_inc(x_ev, 1)

        t_total = LAYERS * 2 * 3 + 4 + len(w1_jobs) + 1

        @block.vector
        def _(dve):
            dve.wait_ge(c_in, 16)
            nc.vector.tensor_copy(m.ident[:, :], consts[:, C_ID:C_ID + P])
            nc.vector.tensor_copy(m.centre[:, :], consts[:, C_CENTRE:C_CENTRE + P])
            nc.vector.tensor_copy(m.ident_b[:, :], consts[:, C_ID:C_ID + P])
            nc.vector.memset(m.ones_b[:, :], 1.0)
            nc.vector.tensor_copy(m.mask_q[:, :, :], consts[:, C_MASK_Q:C_MASK_K].rearrange("p (a n) -> p a n", a=2))
            nc.vector.tensor_copy(m.mask_k[:, :, :], consts[:, C_MASK_K:C_MASK_K + 3 * WIN].rearrange("p (a n) -> p a n", a=3)).then_inc(ready, 1)
            dve.wait_ge(t_in, 16 * t_total)
            for l in range(LAYERS):
                for k in range(2):
                    nc.vector.tensor_tensor(
                        m.tab[:, (l * 2 + k) * NT:(l * 2 + k + 1) * NT, :], base[:, k, :, :, :].rearrange("p t q d -> p t (q d)"),
                        scales[:, k, l, :, :].rearrange("p q d -> p (q d)").unsqueeze(1).broadcast_to([P, NT, 2 * FD]),
                        ALU.mult)
            dve.wait_ge(bias_mm, 1)
            nc.vector.tensor_tensor(m.b1_all[:, :, :], m.bank[4][0:HC, 0:LAYERS * 2 * CH].rearrange("p (l k) -> p l k", l=LAYERS),
                                    b1_raw[:, :, :], ALU.add)
            for l in range(LAYERS):
                last = nc.vector.tensor_scalar(m.w_all[:, l, 512:512 + 2 * CH * HC], m.w_all[:, l, 512:512 + 2 * CH * HC],
                                               ln_g[:, l:l + 1], None, ALU.mult)
            last.then_inc(tables, 1)

        @block.tensor
        def _(pe):
            pe.wait_ge(ready, 1)
            for n in range(B * NT // 4):
                if n % NT == 0 or n % 2 == 0:
                    pe.wait_ge(x_in, 16 * B)
                if n >= 4:
                    pe.wait_ge(x_ev, n - 3)
                for i in range(4):
                    last = nc.tensor.transpose(m.bank[n % 4][:, i * P:(i + 1) * P], x_rows[:, 4 * n + i, :], m.ident[:, :])
                last.then_inc(x_tr, 1)
            pe.wait_ge(w_in, 16 * (len(w1_jobs) + LAYERS * (CH + 1)))
            pe.wait_ge(t_in, 16 * t_total)
            for l, k, lo, n in w1_jobs:
                last = nc.tensor.matmul(m.bank[4][0:HC, l * 2 * CH + k:l * 2 * CH + k + 1],
                                        m.w_all[:, l, 512 + k * HC:512 + (k + 1) * HC], ln_b[:, l:l + 1],
                                        start=True, stop=True)
            last.then_inc(bias_mm, 1)


def layernorm_phase(nc, m, name, dst):
    N = B * T // 512
    ctx = ExitStack()
    with ctx:
        def sb(n, shape, dt=FP32):
            return ctx.enter_context(nc.sbuf_tensor(f"{name}_{n}", shape, dt))

        def sem(n):
            return semaphore(nc, m, ctx, f"{name}_{n}")

        sq = sb("sq", [P, 2, 512])
        log_var = sb("log_var", [P, 2, 512])
        rstd = sb("rstd", [P, 2, 512])
        centred, squared, varred, logged, rstd_ready, normed = (
            sem(s) for s in ("centred", "squared", "varred", "logged", "rstd_ready", "normed"))
        block = ctx.enter_context(nc.Block())

        @block.tensor
        def _(pe):
            for n in range(N + 1):
                if n < N:
                    if n >= 4:
                        pe.wait_ge(normed, n - 3)
                    nc.tensor.matmul(m.bank[n % 4][:, :], m.centre[:, :], m.X[:, n * 512:(n + 1) * 512],
                                     start=True, stop=True).then_inc(centred, 1)
                if n >= 1:
                    k = n - 1
                    pe.wait_ge(squared, k + 1)
                    if k >= 2:
                        pe.wait_ge(logged, k - 1)
                    nc.tensor.matmul(m.bank[4 + k % 2][:, :], m.mean_ones[:, :], sq[:, k % 2, :],
                                     start=True, stop=True).then_inc(varred, 1)

        @block.scalar
        def _(act):
            nc.scalar.preload_act_table_set("natural_log_exp_and_others")
            for n in range(N + 1):
                if n < N:
                    act.wait_ge(centred, n + 1)
                    if n >= 2:
                        act.wait_ge(varred, n - 1)
                    nc.scalar.activation(sq[:, n % 2, :], m.bank[n % 4][:, :], ACT.Square).then_inc(squared, 1)
                if n >= 1:
                    k = n - 1
                    act.wait_ge(varred, k + 1)
                    nc.scalar.activation(log_var[:, k % 2, :], m.bank[4 + k % 2][:, :], ACT.Ln,
                                         bias=m.eps[:, :]).then_inc(logged, 1)
                    act.wait_ge(logged, k + 1)
                    if k >= 2:
                        act.wait_ge(normed, k - 1)
                    nc.scalar.activation(rstd[:, k % 2, :], log_var[:, k % 2, :], ACT.Exp,
                                         scale=-0.5).then_inc(rstd_ready, 1)

        @block.vector
        def _(dve):
            for n in range(N):
                dve.wait_ge(rstd_ready, n + 1)
                nc.vector.tensor_tensor(dst(n), m.bank[n % 4][:, :], rstd[:, n % 2, :], ALU.mult).then_inc(normed, 1)


def ffn_phase(nc, m, name):
    ctx = ExitStack()
    with ctx:
        def sb(n, shape, dt=FP32):
            return ctx.enter_context(nc.sbuf_tensor(f"{name}_{n}", shape, dt))

        def sem(n):
            return semaphore(nc, m, ctx, f"{name}_{n}")

        hT = sb("hT", [P, B, P])
        rot = [sb(f"rot{b}", [P, 2 * INNER]) for b in range(B)]
        rot2 = [sb(f"rot2{i}", [P, 2 * INNER]) for i in range(2)]
        sq = [sb(f"sq{i}", [P, 2 * INNER]) for i in range(2)]
        ss = sb("ss", [P, B, 2 * FH])
        ssc = sb("ssc", [P, B, 2 * FH])
        log_ss = sb("log_ss", [P, B, 2 * FH])
        rnorm = sb("rnorm", [P, B, 2 * FH])
        q_pad = [sb(f"q_pad{b}", [P, PAIRS, 2, 2, WIN]) for b in range(B)]
        k_blk = [sb(f"k_blk{b}", [P, PAIRS, 4, WIN]) for b in range(B)]
        v_cur = [sb(f"v_cur{b}", [P, FH, FD + 1]) for b in range(B)]
        v_mix = [sb(f"v_mix{b}", [P, FH, FD + 1]) for b in range(B)]
        neg_max = sb("neg_max", [P, B, PAIRS * 2])
        diag = [sb(f"diag{b}", [P, 2, PAIRS, P], BF16) for b in range(B)]
        rden = sb("rden", [P, B, FH])
        o = [sq[b % 2][:, (b // 2) * INNER:(b // 2 + 1) * INNER] for b in range(B)]
        oT = sb("oT", [P, 4, B, P])
        x1 = sb("x1", [P, B, P + 1])
        h2 = sb("h2", [P, B, P])
        hn = sb("hn", [P, B * P])
        u = sb("u", [HC, CH, B * P])

        zeroed, ht_staged, x1_zero, x1_before = (
            sem(s) for s in ("zeroed", "ht_staged", "x1_zero", "x1_before"))
        kprev_done, vprev_done, vmix_done = ([sem(f"{s}{b}") for b in range(B)]
                                             for s in ("kprev_done", "vprev_done", "vmix_done"))
        per_b = ("qk_ready", "v_ready", "sq_ready", "ss_ready", "ssc_ready", "rn_log", "rn_ready",
                 "rot_done", "add_done", "qkn_ready", "tr_ready", "qk_evicted",
                 "v_evicted", "s_ready", "max_ready", "d_ready", "st_ready", "p_ready",
                 "pv_ready", "rd_ready", "o_ready", "ot_ready", "ot_evicted")
        per_it = ("wo_ready", "x1_done", "h2_staged", "cen_ready", "csq_ready", "var_ready",
                  "lv_ready", "rstd_ready", "hn_ready", "w2_ready", "out_done")
        (qk_ready, v_ready, sq_ready, ss_ready, ssc_ready, rn_log, rn_ready,
         rot_done, add_done, qkn_ready, tr_ready, qk_evicted,
         v_evicted, s_ready, max_ready, d_ready, st_ready, p_ready,
         pv_ready, rd_ready, o_ready, ot_ready, ot_evicted) = [sem(s) for s in per_b]
        (wo_ready, x1_done, h2_staged, cen_ready, csq_ready, var_ready,
         lv_ready, rstd_ready, hn_ready, w2_ready, out_done) = [sem(s) for s in per_it]
        a_ready, g_ready, gelu_done, u_ready = sem("a_ready"), sem("g_ready"), sem("gelu_done"), sem("u_ready")

        block = ctx.enter_context(nc.Block())

        def pair(slot):
            return m.psum[:, 2 * slot:2 * slot + 2, :]

        vo_bank = m.bank[4:6]
        f_bank = m.bank[6:8]
        A_BANK, G_BANK = f_bank

        class Tile:

            def __init__(self, l, t):
                self.l, self.t = l, t
                self.it = l * NT + t
                self.later = (t + NT - 1) // NT

            def cur(self, b):
                return self.it * B + (B + b + 1)

            def prev(self, b):
                return self.it * B + (b + 1)

            def now(self):
                return self.it + 2

            def before(self):
                return self.it + 1

            def chunk(self, k):
                return self.it * CH + (k + 1)

            def copied(self, copies=1):
                return self.it * (16 * copies) + 16 * copies

        def turns(engine, turn, before_layer=None):
            turn(Tile(0, 0), None)
            for l in range(LAYERS):
                if before_layer is not None:
                    before_layer(l)
                last = l == LAYERS - 1
                with engine.Fori(0, NT - 1 if last else NT) as t:
                    turn(Tile(l, t + 1) if last else Tile((t + 1) // NT, (t + 1) % NT), Tile(l, t))
            turn(None, Tile(LAYERS - 1, NT - 1))

        @block.tensor
        def _(pe):
            for s in (qk_ready, v_ready, tr_ready, s_ready, st_ready, pv_ready, ot_ready):
                pe.sem_inc(s, B)
            for s in (wo_ready, cen_ready, var_ready, w2_ready):
                pe.sem_inc(s, 1)

            def project(n, b):
                s = b % 2
                pe.wait_ge(ht_staged, n.copied(2))
                if b < 2:
                    pe.wait_ge(o_ready, n.prev(b + 2))
                else:
                    pe.wait_ge(rot_done, n.cur(b - 2))
                    pe.wait_ge(sq_ready, n.cur(b - 2))
                for i in range(2):
                    last = nc.tensor.matmul(pair(s)[:, i, :], hT[:, b, :],
                                            m.wqkv[:, bass.ds(n.l, 1), i * INNER:(i + 1) * INNER].rearrange("p a n -> p (a n)"),
                                            start=True, stop=True)
                last.then_inc(qk_ready, 1)
                if b < 2:
                    pe.wait_ge(ot_evicted, n.prev(b + 2))
                else:
                    pe.wait_ge(v_evicted, n.cur(b - 2))
                nc.tensor.matmul(vo_bank[s][:, :], hT[:, b, :],
                                 m.wqkv[:, bass.ds(n.l, 1), 2 * INNER:3 * INNER].rearrange("p a n -> p (a n)"),
                                 start=True, stop=True).then_inc(v_ready, 1)

            def turn_qk(n, b):
                s = b % 2
                pe.wait_ge(qkn_ready, n.cur(b))
                if b < 2:
                    pe.wait_ge(rot_done, n.cur(b + 2))
                    pe.wait_ge(sq_ready, n.cur(b + 2))
                else:
                    pe.wait_ge(qk_evicted, n.cur(b - 2))
                for i in range(8):
                    last = nc.tensor.transpose(pair(s)[:, i // 4, (i % 4) * P:(i % 4 + 1) * P],
                                               rot[b][:, i * P:(i + 1) * P], m.ident[:, :])
                last.then_inc(tr_ready, 1)

            def scores(n, b):
                s = b % 2
                pe.wait_ge(qk_evicted, n.cur(b + 2 if b < 2 else b))
                pe.wait_ge(kprev_done[b], n.copied())
                if b >= 2:
                    pe.wait_ge(max_ready, n.cur(b - 2))
                for i in range(2):
                    nc.tensor.matmul(pair(s)[:, i, :].rearrange("p (j n) -> p j n", j=2), m.ident_b[:, :],
                                     m.mask_q[:, bass.ds(n.later, 1), :].broadcast_to([P, 2, 2 * P]),
                                     start=True, stop=False, skip_group_check=True)
                for j in range(PAIRS):
                    for w in range(2):
                        o_ = (j % 2 * 2 + w) * P
                        last = nc.tensor.matmul(
                            pair(s)[:, j // 2, o_:o_ + P], q_pad[b][:, j, w, :, :].rearrange("p h i -> p (h i)"),
                            k_blk[b][:, j, 2 - 2 * w:4 - 2 * w, :].rearrange("p a j -> p (a j)"),
                            start=False, stop=True, skip_group_check=True)
                last.then_inc(s_ready, 1)

            def scores_turned(n, b):
                s = b % 2
                pe.wait_ge(d_ready, n.cur(b))
                if b < 2:
                    pe.wait_ge(max_ready, n.cur(b + 2))
                else:
                    pe.wait_ge(p_ready, n.cur(b - 2))
                for w in range(2):
                    mask = m.mask_k[:, bass.ds(n.later, 1), :] if w == 0 else m.mask_k[:, 2:3, :]
                    nc.tensor.matmul(pair(s)[:, w, :].rearrange("p (h i) -> p h i", h=FH), m.ident_b[:, :],
                                     mask.broadcast_to([P, FH, WIN]),
                                     start=True, stop=False, skip_group_check=True)
                    nc.tensor.matmul(pair(s)[:, w, :], m.ones_b[:, :], diag[b][:, w, :, :].rearrange("p j i -> p (j i)"),
                                     start=False, stop=False, skip_group_check=True)
                    for j in range(PAIRS):
                        last = nc.tensor.matmul(
                            pair(s)[:, w, j * P:(j + 1) * P], k_blk[b][:, j, 2 - 2 * w:4 - 2 * w, :].rearrange("p a j -> p (a j)"),
                            q_pad[b][:, j, w, :, :].rearrange("p h i -> p (h i)"),
                            start=False, stop=True, skip_group_check=True)
                last.then_inc(st_ready, 1)

            def outputs(n, b):
                s = b % 2
                pe.wait_ge(p_ready, n.cur(b + 2 if b < 2 else b))
                pe.wait_ge(v_evicted, n.cur(b))
                pe.wait_ge(vmix_done[b], n.copied() + 16)
                pe.wait_ge(vprev_done[b], n.copied())
                if b >= 2:
                    pe.wait_ge(o_ready, n.cur(b - 2))
                probs = rot[b][:, :].rearrange("p (w h i) -> p w h i", w=2, h=FH)
                for h in range(FH):
                    for w in range(2):
                        last = nc.tensor.matmul(
                            pair(s)[WIN * w:WIN * (w + 1), h // 4, (h % 4) * (FD + 1):(h % 4 + 1) * (FD + 1)],
                            probs[:, w, h, :], (v_cur if w else v_mix)[b][:, h, :], start=True, stop=True)
                last.then_inc(pv_ready, 1)

            def turn_outputs(n, b):
                pe.wait_ge(o_ready, n.cur(b))
                if b < 2:
                    pe.wait_ge(v_evicted, n.cur(b + 2))
                else:
                    pe.wait_ge(ot_evicted, n.cur(b - 2))
                for i in range(4):
                    last = nc.tensor.transpose(vo_bank[b % 2][:, i * P:(i + 1) * P], o[b][:, i * P:(i + 1) * P], m.ident[:, :])
                last.then_inc(ot_ready, 1)

            def project_out(f):
                pe.wait_ge(ot_evicted, f.cur(B - 1))
                pe.wait_ge(out_done, f.it + NT)
                for k in range(4):
                    last = nc.tensor.matmul(A_BANK[:, :], m.w_all[:, f.l, k * P:(k + 1) * P],
                                            oT[:, k, :, :].rearrange("p b t -> p (b t)"), start=k == 0, stop=k == 3)
                last.then_inc(wo_ready, 1)

            def centre(f):
                pe.wait_ge(h2_staged, f.now())
                nc.tensor.matmul(G_BANK[:, :], m.centre[:, :], h2[:, :, :].rearrange("p b t -> p (b t)"),
                                 start=True, stop=True).then_inc(cen_ready, 1)

            def variance(f):
                pe.wait_ge(csq_ready, f.now())
                nc.tensor.matmul(A_BANK[:, :], m.mean_ones[:, :], hn[:, :], start=True, stop=True).then_inc(var_ready, 1)

            def gated(f, k):
                if k == 0:
                    pe.wait_ge(hn_ready, f.now())
                else:
                    pe.wait_ge(u_ready, f.chunk(k - 1))
                nc.tensor.matmul(A_BANK[0:HC, :], m.w_all[:, f.l, 512 + k * HC:512 + (k + 1) * HC],
                                 hn[:, :], start=True, stop=True).then_inc(a_ready, 1)
                nc.tensor.matmul(G_BANK[0:HC, :], m.w_all[:, f.l, 512 + (CH + k) * HC:512 + (CH + k + 1) * HC],
                                 hn[:, :], start=True, stop=True).then_inc(g_ready, 1)

            def project_down(f):
                pe.wait_ge(u_ready, f.chunk(CH - 1))
                for k in range(CH):
                    last = nc.tensor.matmul(A_BANK[:, :], m.w_all[0:HC, f.l, 512 + 2 * CH * HC + k * P:512 + 2 * CH * HC + (k + 1) * P],
                                            u[:, k, :], start=k == 0, stop=k == CH - 1)
                last.then_inc(w2_ready, 1)

            def turn(n, f):
                if n:
                    project(n, 0)
                    project(n, 1)
                if f:
                    project_out(f)
                if n:
                    project(n, 2)
                if f:
                    centre(f)
                if n:
                    project(n, 3)
                if f:
                    variance(f)
                if n:
                    turn_qk(n, 0)
                if f:
                    gated(f, 0)
                if n:
                    turn_qk(n, 1)
                if f:
                    gated(f, 1)
                if n:
                    turn_qk(n, 2)
                    turn_qk(n, 3)
                if f:
                    gated(f, 2)
                if n:
                    scores(n, 0)
                    scores(n, 1)
                if f:
                    project_down(f)
                if n:
                    for part in (scores, scores_turned, outputs, turn_outputs):
                        for b in range(2 if part is scores else 0, B):
                            part(n, b)

            turns(pe, turn)

        @block.scalar
        def _(act):
            for s in (sq_ready, v_evicted, rn_log, rn_ready, qk_evicted, p_ready, ot_evicted):
                act.sem_inc(s, B)
            for s in (csq_ready, lv_ready, rstd_ready):
                act.sem_inc(s, 1)
            for b in range(B):
                act.sem_inc(vmix_done[b], 16)
            act.wait_ge(zeroed, 1)

            def squares(n, b):
                act.wait_ge(qk_ready, n.cur(b))
                act.wait_ge(ss_ready, n.prev(b + 2) if b < 2 else n.cur(b - 2))
                nc.scalar.activation(sq[b % 2][:, :], pair(b % 2), ACT.Square).then_inc(sq_ready, 1)

            def values(n, b):
                act.wait_ge(v_ready, n.cur(b))
                act.wait_ge(pv_ready, n.prev(b))
                act.wait_ge(vprev_done[b], n.copied())
                act.wait_ge(vmix_done[b], n.copied())
                nc.scalar.activation(v_cur[b][:, :, 0:FD], vo_bank[b % 2][:, :].rearrange("p (h d) -> p h d", h=FH),
                                     ACT.Copy).then_inc(v_evicted, 1)

            def norms(n, b):
                act.wait_ge(ssc_ready, n.cur(b))
                nc.scalar.activation(log_ss[:, b, :], ssc[:, b, :], ACT.Ln).then_inc(rn_log, 1)
                act.wait_ge(rn_log, n.cur(b))
                act.wait_ge(qkn_ready, n.prev(b))
                nc.scalar.activation(rnorm[:, b, :], log_ss[:, b, :], ACT.Exp, scale=-0.5).then_inc(rn_ready, 1)

            def evict_qk(n, b):
                act.wait_ge(tr_ready, n.cur(b))
                act.wait_ge(st_ready, n.prev(b))
                act.wait_ge(kprev_done[b], n.copied())
                kt = pair(b % 2)[:, 1, :].rearrange("p (j w i) -> p j w i", j=PAIRS, w=2)
                nc.scalar.activation(k_blk[b][:, :, 0:2, :], kt, ACT.Copy)
                nc.scalar.activation(k_blk[b][:, :, 2, :], kt[:, :, 0, :], ACT.Copy)
                qt = pair(b % 2)[:, 0, :].rearrange("p (j w i) -> p j w i", j=PAIRS, w=2)
                nc.scalar.activation(q_pad[b][0:64, :, :, 0, :], qt[0:64], ACT.Copy)
                nc.scalar.activation(q_pad[b][64:128, :, :, 1, :], qt[64:128], ACT.Copy).then_inc(qk_evicted, 1)

            def square_centred(f):
                act.wait_ge(cen_ready, f.now())
                nc.scalar.activation(hn[:, :], G_BANK[:, :], ACT.Square).then_inc(csq_ready, 1)

            def deviation(f):
                act.wait_ge(var_ready, f.now())
                nc.scalar.activation(hn[:, :], A_BANK[:, :], ACT.Ln, bias=m.eps[:, :]).then_inc(lv_ready, 1)
                act.wait_ge(lv_ready, f.now())
                nc.scalar.activation(hn[:, :], hn[:, :], ACT.Exp, scale=-0.5).then_inc(rstd_ready, 1)

            def gelu(f, k):
                act.wait_ge(g_ready, f.chunk(k))
                nc.scalar.activation(u[:, k, :], G_BANK[0:HC, :], ACT.Gelu,
                                     bias=m.b1_all[:, f.l, CH + k:CH + k + 1]).then_inc(gelu_done, 1)

            def turn(n, f):
                nc.scalar.preload_act_table_set("natural_log_exp_and_others")
                if n:
                    squares(n, 0)
                    values(n, 0)
                    squares(n, 1)
                    values(n, 1)
                    norms(n, 0)
                    squares(n, 2)
                    values(n, 2)
                    norms(n, 1)
                if f:
                    square_centred(f)
                if n:
                    squares(n, 3)
                    values(n, 3)
                if f:
                    deviation(f)
                if n:
                    norms(n, 2)
                    norms(n, 3)
                    evict_qk(n, 0)
                if f:
                    gelu(f, 0)
                if n:
                    evict_qk(n, 1)
                if f:
                    gelu(f, 1)
                if n:
                    evict_qk(n, 2)
                    evict_qk(n, 3)
                if f:
                    gelu(f, 2)
                if n:
                    if f:
                        nc.scalar.preload_act_table_set("natural_log_exp_and_others")
                    for b in range(B):
                        act.wait_ge(st_ready, n.cur(b))
                        nc.scalar.activation(rot[b][:, :].rearrange("p (w n) -> p w n", w=2), pair(b % 2), ACT.Exp).then_inc(p_ready, 1)
                    for b in range(B):
                        act.wait_ge(ot_ready, n.cur(b))
                        act.wait_ge(wo_ready, n.before())
                        nc.scalar.activation(oT[:, :, b, :], vo_bank[b % 2][:, :].rearrange("p (k t) -> p k t", k=4),
                                             ACT.Copy).then_inc(ot_evicted, 1)

            turns(act, turn)

        @block.vector
        def _(dve):
            for s in (ss_ready, ssc_ready, rot_done, qkn_ready, max_ready, rd_ready, o_ready):
                dve.sem_inc(s, B)
            for s in (x1_done, h2_staged, hn_ready):
                dve.sem_inc(s, 1)
            dve.sem_inc(out_done, NT)

            def before_layer(l):
                dve.wait_ge(out_done, l * NT + NT)
                dve.wait_ge(zeroed, 1)
                nc.vector.memset(x1[:, :, P:P + 1], 0.0).then_inc(x1_zero, 1)
                dve.wait_ge(x1_zero, l + 1)

            def rotate(n, b):
                qk = pair(b % 2)
                dve.wait_ge(sq_ready, n.cur(b))
                nc.vector.tensor_reduce(ss[:, b, :], sq[b % 2][:, :].rearrange("p (h d) -> p h d", d=FD),
                                        AX.X, ALU.add).then_inc(ss_ready, 1)
                dve.wait_ge(ss_ready, n.cur(b))
                dve.wait_ge(rn_log, n.prev(b))
                nc.vector.tensor_scalar(ssc[:, b, :], ss[:, b, :], 1e-24, None, ALU.max).then_inc(ssc_ready, 1)
                dve.wait_ge(pv_ready, n.prev(b))
                one = m.tab[:, bass.ds(n.l * (2 * NT) + n.t, 1), :].rearrange("p a (q d) -> p (a q) d", q=2).unsqueeze(2).broadcast_to([P, 2, FH, FD])
                nc.vector.tensor_tensor(rot[b][:, :].rearrange("p (q h d) -> p q h d", q=2, h=FH),
                                        qk.rearrange("p q (h d) -> p q h d", h=FH), one, ALU.mult)
                dve.wait_ge(add_done, n.prev(b + 2) if b < 2 else n.cur(b - 2))
                two = m.tab[:, bass.ds(n.l * (2 * NT) + n.t + NT, 1), :].rearrange("p a (q d) -> p (a q) d", q=2).unsqueeze(2).broadcast_to([P, 2, FH, FD])
                dst = rot2[b % 2][:, :].rearrange("p (q h d) -> p q h d", q=2, h=FH)
                src = qk.rearrange("p q (h d) -> p q h d", h=FH)
                for i in range(2):
                    last = nc.vector.tensor_tensor(dst[:, :, :, 32 * i:32 * i + 32], src[:, :, :, 32 - 32 * i:64 - 32 * i],
                                                   two[:, :, :, 32 * i:32 * i + 32], ALU.mult)
                last.then_inc(rot_done, 1)

            def normalise(n, b):
                dve.wait_ge(add_done, n.cur(b))
                dve.wait_ge(rn_ready, n.cur(b))
                r = rot[b][:, :].rearrange("p (h d) -> p h d", d=FD)
                nc.vector.tensor_tensor(r, r, rnorm[:, b, :].unsqueeze(2).broadcast_to([P, 2 * FH, FD]),
                                        ALU.mult).then_inc(qkn_ready, 1)

            def maximum(n, b):
                dve.wait_ge(s_ready, n.cur(b))
                nc.vector.tensor_reduce(neg_max[:, b, :], pair(b % 2).rearrange("p a (h j) -> p (a h) j", h=4),
                                        AX.X, ALU.max, negate=True).then_inc(max_ready, 1)

            def divide(n, b):
                dve.wait_ge(pv_ready, n.cur(b))
                out = pair(b % 2)[:, :, 0:4 * (FD + 1)].rearrange("p a (h d) -> p a h d", h=4)
                nc.vector.reciprocal(rden[:, b, :].rearrange("p (a h) -> p a h", a=2), out[:, :, :, FD]).then_inc(rd_ready, 1)
                dve.wait_ge(rd_ready, n.cur(b))
                nc.vector.tensor_tensor(o[b].rearrange("p (a h d) -> p a h d", a=2, h=4), out[:, :, :, 0:FD],
                                        rden[:, b, :].rearrange("p (a h) -> p a h", a=2).unsqueeze(3).broadcast_to([P, 2, 4, FD]),
                                        ALU.mult).then_inc(o_ready, 1)

            def add_attention(f):
                x_in = m.xs[:, f.l, :, bass.ds(f.t * P + 1, P)]
                dve.wait_ge(zeroed, 1)
                dve.wait_ge(out_done, f.it + NT)
                nc.vector.tensor_copy(x1[:, :, 0:1], x1[:, :, P:P + 1]).then_inc(x1_before, 1)
                dve.wait_ge(x1_before, f.it + 1)
                dve.wait_ge(wo_ready, f.now())
                nc.vector.tensor_tensor(x1[:, :, 1:P + 1], A_BANK[:, :].rearrange("p (b t) -> p b t", b=B),
                                        x_in, ALU.add).then_inc(x1_done, 1)
                dve.wait_ge(x1_done, f.now())
                nc.vector.tensor_copy(h2[0:64, :, :], x1[0:64, :, 1:P + 1])
                nc.vector.tensor_copy(h2[64:128, :, :], x1[64:128, :, 0:P]).then_inc(h2_staged, 1)

            def scale_centred(f):
                dve.wait_ge(rstd_ready, f.now())
                nc.vector.tensor_tensor(hn[:, :], G_BANK[:, :], hn[:, :], ALU.mult).then_inc(hn_ready, 1)

            def gate(f, k):
                dve.wait_ge(a_ready, f.chunk(k))
                dve.wait_ge(gelu_done, f.chunk(k))
                nc.vector.scalar_tensor_tensor(u[:, k, :], A_BANK[0:HC, :], m.b1_all[:, f.l, k:k + 1], u[:, k, :],
                                               ALU.add, ALU.mult).then_inc(u_ready, 1)

            def add_gated(f):
                x_out = m.xs[:, 1 - f.l, :, bass.ds(f.t * P + 1, P)]
                dve.wait_ge(zeroed, 1)
                dve.wait_ge(w2_ready, f.now())
                nc.vector.scalar_tensor_tensor(x_out, A_BANK[:, :].rearrange("p (b t) -> p b t", b=B), m.b2_all[:, f.l:f.l + 1],
                                               x1[:, :, 1:P + 1], ALU.add, ALU.add).then_inc(out_done, 1)

            def turn(n, f):
                if n:
                    rotate(n, 0)
                    rotate(n, 1)
                if f:
                    add_attention(f)
                if n:
                    normalise(n, 0)
                    rotate(n, 2)
                    normalise(n, 1)
                if f:
                    scale_centred(f)
                if n:
                    rotate(n, 3)
                    normalise(n, 2)
                if f:
                    gate(f, 0)
                if n:
                    normalise(n, 3)
                if f:
                    gate(f, 1)
                    gate(f, 2)
                if n:
                    maximum(n, 0)
                    maximum(n, 1)
                if f:
                    add_gated(f)
                if n:
                    maximum(n, 2)
                    maximum(n, 3)
                    for b in range(B):
                        divide(n, b)

            turns(dve, turn, before_layer)
            dve.wait_ge(out_done, NT + LAYERS * NT)
            nc.vector.scalar_tensor_tensor(m.X[:, :].rearrange("p (b t) -> p b t", b=B), m.xs[:, 0, :, 1:], 0.5,
                                           m.X[:, :].rearrange("p (b t) -> p b t", b=B), ALU.mult, ALU.add)

        @block.gpsimd
        def _(pool):
            for s in (add_done, d_ready):
                pool.sem_inc(s, B)
            for b in range(B):
                nc.gpsimd.memset(q_pad[b][:, :, :, :, :], 0.0)
                nc.gpsimd.memset(k_blk[b][:, :, :, :], 0.0)
                nc.gpsimd.memset(v_cur[b][:, :, :], 1.0)
                nc.gpsimd.memset(v_mix[b][:, :, :], 1.0)
            nc.gpsimd.memset(x1[:, :, :], 0.0).then_inc(zeroed, 1)

            def turn(n, f):
                if n is None:
                    return
                for b in range(B):
                    pool.wait_ge(rot_done, n.cur(b))
                    nc.gpsimd.tensor_tensor(rot[b][:, :], rot[b][:, :], rot2[b % 2][:, :], ALU.add).then_inc(add_done, 1)
                for b in range(B):
                    pool.wait_ge(max_ready, n.cur(b))
                    nc.gpsimd.tensor_tensor(diag[b][:, :, :, :],
                                            neg_max[:, b, :].rearrange("p (j w) -> p w j", w=2).unsqueeze(3).broadcast_to([P, 2, PAIRS, P]),
                                            m.ident[:, :].unsqueeze(1).unsqueeze(1).broadcast_to([P, 2, PAIRS, P]),
                                            ALU.mult).then_inc(d_ready, 1)

            turns(pool, turn)

        @block.sync
        def _(sp):
            def turn(n, f):
                if n is None:
                    return
                if f:
                    sp.lower_val(n.it + 1)
                sp.wait_ge(zeroed, 1)
                sp.wait_ge(v_ready, n.prev(B - 1))
                sp.wait_ge(out_done, n.it + 1)
                for half in range(2):
                    rows = slice(64 * half, 64 * half + 64)
                    sp.dma_start(hT[rows, :, :], m.xs[rows, bass.ds(n.l, 1), :, bass.ds(n.t * P + (1 - half), P)]
                                 .rearrange("p a b t -> p (a b) t")).then_inc(ht_staged, 16)
                for b in range(B):
                    sp.wait_ge(st_ready, n.prev(b))
                    sp.dma_start(k_blk[b][:, :, 3, :], k_blk[b][:, :, 1, :]).then_inc(kprev_done[b], 16)
                    sp.wait_ge(pv_ready, n.prev(b))
                    sp.dma_start(v_mix[b][64:128, :, :], v_cur[b][64:128, :, :]).then_inc(vprev_done[b], 16)
                for b in range(B):
                    sp.wait_ge(v_evicted, n.cur(b))
                    sp.dma_start(v_mix[b][0:64, :, :], v_cur[b][0:64, :, :]).then_inc(vmix_done[b], 16)

            turns(sp, turn)


def binarise_phase(nc, m, a):
    ctx = ExitStack()
    with ctx:
        def sb(n, shape, dt=FP32):
            return ctx.enter_context(nc.sbuf_tensor(f"bin_{n}", shape, dt))

        def sem(n):
            return semaphore(nc, m, ctx, f"bin_{n}")

        w = sb("w", [P, 4, C])
        positive = sb("positive", [P, 4, C])
        neg_sign = sb("neg_sign", [P, 4, C])
        total = sb("total", [P, 4])
        loaded, summed, signs, scaled, turned = (sem(s) for s in ("loaded", "summed", "signs", "scaled", "turned"))
        ctx.enter_context(nc.allow_non_contiguous_dma(reason="a few columns of parameters"))
        block = ctx.enter_context(nc.Block())

        @block.sync
        def _(sp):
            for i, name in enumerate(("Wq", "Wk", "Wv", "Wp")):
                sp.dma_start(w[:, i, :], a["L0_attn_" + name]).then_inc(loaded, 16)
            for i, name in enumerate(("bq", "bk", "bp")):
                sp.dma_start(m.att_bias[:, i:i + 1], a["L0_attn_" + name].rearrange("(p a) -> p a", a=1)).then_inc(loaded, 16)
            sp.dma_start(m.bv_row[:, :], a["L0_attn_bv"].rearrange("(a n) -> a n", a=1).broadcast_to([P, C])).then_inc(loaded, 16)
            sp.wait_ge(loaded, 16 * 8)

        @block.vector
        def _(dve):
            dve.wait_ge(loaded, 16 * 8)
            nc.vector.tensor_reduce(total[:, :], w[:, :, :], AX.X, ALU.add, apply_absolute_value=True)
            nc.vector.tensor_scalar(positive[:, :, :], w[:, :, :], 0.0, None, ALU.is_gt).then_inc(summed, 1)
            dve.wait_ge(summed, 1)
            nc.vector.scalar_tensor_tensor(neg_sign[:, :, :], w[:, :, :], 0.0, positive[:, :, :],
                                           ALU.is_lt, ALU.subtract).then_inc(signs, 1)
            dve.wait_ge(signs, 1)
            for i in range(4):
                last = nc.vector.tensor_scalar(w[:, i, :], neg_sign[:, i, :], total[:, i:i + 1], -1.0 / C, ALU.mult, ALU.mult)
            last.then_inc(scaled, 1)
            dve.wait_ge(turned, 1)
            nc.vector.tensor_copy(m.att_w[:, :, :], m.bank[0][:, :].rearrange("p (i o) -> p i o", i=4))

        @block.tensor
        def _(pe):
            pe.wait_ge(scaled, 1)
            for i in range(4):
                last = nc.tensor.transpose(m.bank[0][:, i * P:(i + 1) * P], w[:, i, :], m.ident[:, :])
            last.then_inc(turned, 1)


def project_phase(nc, m, V, scratch):
    N = B * T // 512
    ctx = ExitStack()
    with ctx:
        def sb(n, shape, dt=FP32):
            return ctx.enter_context(nc.sbuf_tensor(f"prj_{n}", shape, dt))

        def sem(n):
            return semaphore(nc, m, ctx, f"prj_{n}")

        parts = sb("parts", [P, 2, PARTS, 512], BF16)
        rest = sb("rest", [P, 2, 512])
        qk_ready, part1, rest_ready, part2, part3, v_ready, v_done = (
            sem(s) for s in ("qk_ready", "part1", "rest_ready", "part2", "part3", "v_ready", "v_done"))
        stored = [sem(f"stored{i}") for i in range(2)]
        block = ctx.enter_context(nc.Block())

        def stream(n):
            return m.xs[:, 0, n // 2, 1 + (n % 2) * 512:1 + (n % 2 + 1) * 512]

        @block.tensor
        def _(pe):
            for u in range(2 * N):
                if u >= 4:
                    pe.wait_ge(rest_ready, u - 3)
                nc.tensor.matmul(m.bank[u % 4][:, :], m.att_w[:, u % 2, :], stream(u // 2),
                                 start=True, stop=True).then_inc(qk_ready, 1)
                if u % 2:
                    n = u // 2
                    if n >= 4:
                        pe.wait_ge(v_done, n - 3)
                    for i in range(4):
                        last = nc.tensor.matmul(m.bank[4 + n % 4][:, i * P:(i + 1) * P], stream(n)[:, i * P:(i + 1) * P],
                                                m.att_w[:, 2, :], start=True, stop=True)
                    last.then_inc(v_ready, 1)

        @block.scalar
        def _(act):
            for u in range(2 * N):
                act.wait_ge(qk_ready, u + 1)
                if u >= 2:
                    act.wait_ge(stored[u % 2], 16 * PARTS * (u // 2))
                nc.scalar.activation(parts[:, u % 2, 0, :], m.bank[u % 4][:, :], ACT.Identity,
                                     bias=m.att_bias[:, u % 2:u % 2 + 1]).then_inc(part1, 1)

        @block.vector
        def _(dve):
            for u in range(2 * N):
                dve.wait_ge(part1, u + 1)
                if u >= 2:
                    dve.wait_ge(part3, u - 1)
                nc.vector.scalar_tensor_tensor(rest[:, u % 2, :], m.bank[u % 4][:, :], m.att_bias[:, u % 2:u % 2 + 1],
                                               parts[:, u % 2, 0, :], ALU.add, ALU.subtract).then_inc(rest_ready, 1)
                dve.wait_ge(rest_ready, u + 1)
                nc.vector.tensor_copy(parts[:, u % 2, 1, :], rest[:, u % 2, :]).then_inc(part2, 1)
                if u % 2:
                    n = u // 2
                    dve.wait_ge(v_ready, n + 1)
                    nc.vector.tensor_tensor(V[:, 4 * n:4 * n + 4, :], m.bank[4 + n % 4][:, :].rearrange("p (i o) -> p i o", i=4),
                                            m.bv_row[:, :].unsqueeze(1).broadcast_to([P, 4, C]), ALU.add).then_inc(v_done, 1)

        @block.gpsimd
        def _(pool):
            for u in range(2 * N):
                pool.wait_ge(part2, u + 1)
                nc.gpsimd.tensor_tensor(parts[:, u % 2, 2, :], rest[:, u % 2, :], parts[:, u % 2, 1, :],
                                        ALU.subtract).then_inc(part3, 1)

        @block.sync
        def _(sp):
            for u in range(2 * N):
                sp.wait_ge(part3, u + 1)
                n = u // 2
                for i in range(PARTS):
                    dst = scratch[u % 2, n // 2, i, :, :, (n % 2) * 512:(n % 2 + 1) * 512].rearrange("d h t -> h d t")
                    sp.dma_start(dst, parts[:, u % 2, i, :]).then_inc(stored[u % 2], 16)
            for which in range(2):
                sp.wait_ge(stored[which], 16 * PARTS * N)


LEAD = 12
UNITS = 64
STEPS = 16
SLOTS = 3
ROWS = 96


def attention_phase(nc, m, a, V, Y, scratch, m_scratch):
    ctx = ExitStack()
    with ctx:
        def sb(n, shape, dt=FP32):
            return ctx.enter_context(nc.sbuf_tensor(f"att_{n}", shape, dt))

        def sem(n):
            return semaphore(nc, m, ctx, f"att_{n}")

        Q = [sb(f"Q{s}", [ROWS, 4, T], BF16) for s in range(SLOTS)]
        K = [sb(f"K{s}", [ROWS, 4, T], BF16) for s in range(SLOTS)]
        vq = [sb(f"vq{s}", [P, NT, 4, DH + 1]) for s in range(SLOTS)]
        probs = [sb(f"probs{r}", [P, 4, 512]) for r in range(2)]
        neg_half = sb("neg_half", [P, 32, 2])
        neg_max = sb("neg_max", [P, 32])
        m_rows = sb("m_rows", [32, P], BF16)
        o_sb = sb("o_sb", [P, 2, 512])
        rden = sb("rden", [P, 2, 4, 4])

        (set_up, ring_filled, ring_freed, combined, rows_out, rows_in, e_filled, e_done, av_done,
         o_evicted, rd_ready, v_staged) = (sem(s) for s in (
             "set_up", "ring_filled", "ring_freed", "combined", "rows_out", "rows_in", "e_filled",
             "e_done", "av_done", "o_evicted", "rd_ready", "v_staged"))
        stack_in = [sem(f"stack_in{s}") for s in range(SLOTS)]
        LOADS = 2 * PARTS + 1
        block = ctx.enter_context(nc.Block())

        ring = m.bank[0:3]
        O = m.bank[7]

        def e_slot(e):
            return m.psum[:, 3 + 2 * e:5 + 2 * e, :]

        def ring_uses(ahead):
            uses = [[] for _ in range(STEPS + 1)]
            for u in range(UNITS):
                k = LEAD + u
                if ahead:
                    uses[u // 4].append(("max", 1 + k // UNITS, k % UNITS))
                    if k == UNITS - 1:
                        uses[u // 4].append(("rows", 1))
            uses[10].append(("out", 0))
            uses[STEPS].append(("out", 1))
            return uses

        USES = UNITS + 3
        BEFORE = UNITS + 1 + LEAD
        first_uses = [("max", 0, u) for u in range(UNITS)] + [("rows", 0)] + [("max", 1, u) for u in range(LEAD)]

        class Quad:

            def __init__(self, i, c):
                self.i, self.c = i, c
                self.n = i * SLOTS + c

            def slot(self, ahead=0):
                return (self.c + ahead) % SLOTS

            def stack(self, ahead):
                return self.i * (16 * LOADS) + 16 * LOADS * ((self.c + ahead) // SLOTS + 1)

            def ring(self, local):
                return self.i * (SLOTS * USES) + (BEFORE + self.c * USES + local + 1)

            def bank(self, local):
                return ring[(BEFORE + self.c * USES + local) % 3]

            def step(self, u):
                return self.i * (SLOTS * STEPS) + (self.c * STEPS + u + 1)

            def pairs(self, u, e):
                return self.i * (SLOTS * STEPS * 2) + ((self.c * STEPS + u) * 2 + e + 1)

            def half(self, qc):
                return self.i * (SLOTS * 2) + (self.c * 2 + qc + 1)

        def body(engine, turn):
            with engine.Fori(0, (B * QUADS - 1) // SLOTS) as i:
                for c in range(SLOTS):
                    turn(Quad(i, c), True)
            turn(Quad((B * QUADS - 1) // SLOTS, 0), False)

        @block.tensor
        def _(pe):
            def fill(use, q, bank, freed):
                if freed is not None:
                    pe.wait_ge(ring_freed, freed)
                if use[0] == "max":
                    _, ahead, u = use
                    h, qt, kc = u // 16, u // 2 % 8, u % 2
                    if u == 0:
                        pe.wait_ge(stack_in[q.slot(ahead)], q.stack(ahead))
                    last = nc.tensor.matmul(bank[:, :], Q[q.slot(ahead)][:, h, qt * P:(qt + 1) * P],
                                            K[q.slot(ahead)][:, h, kc * 512:(kc + 1) * 512], start=True, stop=True)
                elif use[0] == "rows":
                    pe.wait_ge(combined, q.n + use[1] + 1)
                    last = nc.tensor.transpose(bank[0:32, 0:P], neg_max[:, :], m.ident[:, :])
                else:
                    pe.wait_ge(o_evicted, q.half(use[1]) + 1)
                    for i in range(4):
                        last = nc.tensor.transpose(bank[:, i * P:(i + 1) * P], o_sb[:, use[1], i * P:(i + 1) * P], m.ident[:, :])
                last.then_inc(ring_filled, 1)

            pe.wait_ge(set_up, 2)
            start = Quad(0, 0)
            for k, use in enumerate(first_uses):
                fill(use, start, ring[k % 3], k - 2 if k >= 3 else None)

            def turn(q, ahead):
                uses = ring_uses(ahead)
                local = 0
                s = q.slot()
                pe.wait_ge(rows_in, q.n * 16 + 16)
                pe.wait_ge(v_staged, q.n + 1)

                def products(u):
                    qc, kt = u // NT, u % NT
                    if kt == 0:
                        pe.wait_ge(o_evicted, q.half(qc))
                    pe.wait_ge(e_done, q.pairs(u, 1) + 2)
                    for h in range(4):
                        last = nc.tensor.matmul(O[32 * h:32 * h + DH + 1, :], vq[s][:, kt, h, :], probs[u % 2][:, h, :],
                                                start=kt == 0, stop=kt == NT - 1)
                    last.then_inc(av_done, 1)

                for u in range(STEPS):
                    qc, kt = u // NT, u % NT
                    for e in range(2):
                        pe.wait_ge(e_done, q.pairs(u, e))
                        for h in (2 * e, 2 * e + 1):
                            last = nc.tensor.matmul(e_slot(e)[:, h % 2, :], K[s][:, h, kt * P:(kt + 1) * P],
                                                    Q[s][:, h, qc * 512:(qc + 1) * 512], start=True, stop=True)
                        last.then_inc(e_filled, 1)
                    for k, use in enumerate(uses[u]):
                        if k == 2 and u:
                            products(u - 1)
                        fill(use, q, q.bank(local), q.ring(local) - 3)
                        local += 1
                    if len(uses[u]) < 3 and u:
                        products(u - 1)
                products(STEPS - 1)
                for use in uses[STEPS]:
                    fill(use, q, q.bank(local), q.ring(local) - 3)
                    local += 1

            body(pe, turn)

        @block.scalar
        def _(act):
            def turn(q, ahead):
                def evict(qc):
                    act.wait_ge(av_done, q.step(NT * qc + NT - 1) + 2)
                    act.wait_ge(rd_ready, q.half(qc))
                    nc.scalar.activation(o_sb[:, qc, :], O[:, :], ACT.Copy).then_inc(o_evicted, 1)

                for u in range(STEPS):
                    for e in range(2):
                        act.wait_ge(e_filled, q.pairs(u, e))
                        if e == 0:
                            act.wait_ge(av_done, q.step(u))
                        nc.scalar.activation(probs[u % 2][:, 2 * e:2 * e + 2, :], e_slot(e), ACT.Exp,
                                             scale=float(DH) ** -0.5).then_inc(e_done, 1)
                    if u == NT:
                        evict(0)
                evict(1)

            act.sem_inc(e_done, 2)
            act.sem_inc(av_done, 2)
            act.sem_inc(rd_ready, 2)
            act.sem_inc(o_evicted, 1)
            body(act, turn)

        @block.vector
        def _(dve):
            def drain(use, q, bank, filled):
                dve.wait_ge(ring_filled, filled)
                if use[0] == "max":
                    _, ahead, u = use
                    h, qt, kc = u // 16, u // 2 % 8, u % 2
                    last = nc.vector.tensor_reduce(neg_half[:, h * 8 + qt, kc:kc + 1], bank[:, :], AX.X, ALU.max, negate=True)
                elif use[0] == "rows":
                    last = nc.vector.tensor_copy(m_rows[:, :], bank[0:32, 0:P])
                else:
                    out = bank[:, :].rearrange("p (i g r) -> p i g r", i=4, g=4)
                    nc.vector.reciprocal(rden[:, use[1], :, :], out[:, :, :, DH]).then_inc(rd_ready, 1)
                    dve.wait_ge(rd_ready, q.half(use[1]) + 2)
                    b, j = q.n // QUADS, q.n % QUADS
                    dst = Y[:, bass.ds(b * NT + 4 * use[1], 4), bass.ds(j * 32, 32)].rearrange("p i (g d) -> p i g d", g=4)
                    last = nc.vector.tensor_tensor(dst, out[:, :, :, 0:DH], rden[:, use[1], :, :].unsqueeze(3).broadcast_to([P, 4, 4, DH]), ALU.mult)
                last.then_inc(ring_freed, 1)

            def combine(q, ahead, uses_done):
                dve.wait_ge(ring_freed, uses_done)
                nc.vector.tensor_tensor(neg_max[:, :], neg_half[:, :, 0], neg_half[:, :, 1], ALU.min).then_inc(combined, 1)

            def stage(q, ahead):
                k = q.n + ahead
                src = V[:, bass.ds(k // QUADS * NT, NT), bass.ds(k % QUADS * 32, 32)].rearrange("p t (h d) -> p t h d", h=4)
                nc.vector.tensor_copy(vq[q.slot(ahead)][:, :, :, 0:DH], src).then_inc(v_staged, 1)

            start = Quad(0, 0)
            for s in range(SLOTS):
                nc.vector.memset(vq[s][:, :, :, :], 1.0)
            nc.vector.memset(O[:, :], 0.0).then_inc(set_up, 1)
            dve.wait_ge(set_up, 2)
            stage(start, 0)
            for k, use in enumerate(first_uses):
                if use[0] == "rows":
                    combine(start, 0, k)
                drain(use, start, ring[k % 3], k + 1)

            def turn(q, ahead):
                local = 0
                if ahead:
                    stage(q, 1)
                for step in ring_uses(ahead):
                    for use in step:
                        if use[0] == "rows":
                            combine(q, 1, q.ring(local) - 1)
                        drain(use, q, q.bank(local), q.ring(local))
                        local += 1

            body(dve, turn)

        @block.gpsimd
        def _(pool):
            for s in range(SLOTS):
                nc.gpsimd.memset(Q[s][64:ROWS, :, :], 0.0)
                last = nc.gpsimd.memset(K[s][64:ROWS, :, :], 1.0)
            last.then_inc(set_up, 1)

        @block.sync
        def _(sp):
            def load(slot, b, j):
                for i in range(PARTS):
                    rows = slice(i * PARTS * DH, (i + 1) * PARTS * DH)
                    src_q = scratch_quad(0, b, j)[i:i + 1].broadcast_to([PARTS, DH, 4 * T])
                    src_k = scratch_quad(1, b, j)
                    sp.dma_start(Q[slot][rows, :, :].rearrange("p h t -> p (h t)"), src_q).then_inc(stack_in[slot], 16)
                    sp.dma_start(K[slot][rows, :, :].rearrange("p h t -> p (h t)"), src_k).then_inc(stack_in[slot], 16)
                sp.dma_start(Q[slot][KROWS:KROWS + 1, :, :].rearrange("p h t -> p (h t)"), a["zeros"].bitcast(BF16)).then_inc(stack_in[slot], 16)

            def scratch_quad(which, b, j):
                if isinstance(b, int):
                    v = scratch[which, b:b + 1, :, :, 4 * j:4 * j + 4, :]
                else:
                    v = scratch[which, bass.ds(b, 1), :, :, bass.ds(j * 4, 4), :]
                return v.rearrange("a i d h t -> (a i) d (h t)")

            def rows(count, slot, written):
                sp.wait_ge(ring_freed, written)
                sp.dma_start(m_scratch, m_rows[:, :]).then_inc(rows_out, 16)
                sp.wait_ge(rows_out, count * 16)
                sp.dma_start(Q[slot][KROWS:KROWS + 1, :, :].rearrange("p h t -> p (h t)"),
                             m_scratch.rearrange("(a r) q -> a (r q)", a=1)).then_inc(rows_in, 16)

            sp.wait_ge(set_up, 2)
            load(0, 0, 0)
            load(1, 0, 1)
            rows(1, 0, UNITS + 1)

            def turn(q, ahead):
                if not ahead:
                    return
                k = (q.n + 2) % (B * QUADS)
                sp.wait_ge(ring_freed, q.ring(-1))
                load(q.slot(2), k // QUADS, k % QUADS)
                order = [use[0] for step in ring_uses(True) for use in step]
                rows(q.n + 2, q.slot(1), q.ring(order.index("rows")))

            body(sp, turn)


def output_phase(nc, m, Y):
    N = B * T // 512
    ctx = ExitStack()
    with ctx:
        def sem(n):
            return semaphore(nc, m, ctx, f"outp_{n}")

        yT = ctx.enter_context(nc.sbuf_tensor("outp_yT", [P, 2, 512], FP32))
        turned, evicted, projected, added = (sem(s) for s in ("turned", "evicted", "projected", "added"))
        block = ctx.enter_context(nc.Block())

        @block.tensor
        def _(pe):
            for n in range(N + 1):
                if n < N:
                    if n >= 2:
                        pe.wait_ge(evicted, n - 1)
                    for i in range(4):
                        last = nc.tensor.transpose(m.bank[n % 2][:, i * P:(i + 1) * P], Y[:, 4 * n + i, :], m.ident[:, :])
                    last.then_inc(turned, 1)
                if n >= 1:
                    k = n - 1
                    pe.wait_ge(evicted, k + 1)
                    if k >= 2:
                        pe.wait_ge(added, k - 1)
                    nc.tensor.matmul(m.bank[2 + k % 2][:, :], m.att_w[:, 3, :], yT[:, k % 2, :],
                                     start=True, stop=True).then_inc(projected, 1)

        @block.scalar
        def _(act):
            for n in range(N):
                act.wait_ge(turned, n + 1)
                if n >= 2:
                    act.wait_ge(projected, n - 1)
                nc.scalar.activation(yT[:, n % 2, :], m.bank[n % 2][:, :], ACT.Copy).then_inc(evicted, 1)

        @block.vector
        def _(dve):
            for n in range(N):
                x = m.X[:, n * 512:(n + 1) * 512]
                dve.wait_ge(projected, n + 1)
                nc.vector.scalar_tensor_tensor(x, m.bank[2 + n % 2][:, :], m.att_bias[:, 2:3], x,
                                               ALU.add, ALU.add).then_inc(added, 1)


def store_phase(nc, m, a):
    ctx = ExitStack()
    with ctx:
        rows = ctx.enter_context(nc.sbuf_tensor("st_rows", [P, B * NT, C], FP32))
        back = semaphore(nc, m, ctx, "st_back")
        evicted = semaphore(nc, m, ctx, "st_evicted")
        stored = semaphore(nc, m, ctx, "st_stored")
        block = ctx.enter_context(nc.Block())
        N = B * NT // 4

        @block.tensor
        def _(pe):
            for n in range(N):
                if n >= 4:
                    pe.wait_ge(evicted, n - 3)
                for i in range(4):
                    last = nc.tensor.transpose(m.bank[n % 4][:, i * P:(i + 1) * P], m.X[:, (4 * n + i) * P:(4 * n + i + 1) * P], m.ident[:, :])
                last.then_inc(back, 1)

        @block.vector
        def _(dve):
            for n in range(N):
                dve.wait_ge(back, n + 1)
                nc.vector.tensor_copy(rows[:, 4 * n:4 * n + 4, :], m.bank[n % 4][:, :].rearrange("p (i c) -> p i c", i=4)).then_inc(evicted, 1)

        @block.sync
        def _(sp):
            for b in range(B):
                sp.wait_ge(evicted, (b + 1) * NT // 4)
                sp.dma_start(a["out"][b].rearrange("(t p) c -> p t c", p=P), rows[:, b * NT:(b + 1) * NT, :]).then_inc(stored, 16)
            sp.wait_ge(stored, 16 * B)


def build(nc, a):
    ctx = ExitStack()
    with ctx:
        m = Memory()

        def sb(name, shape, dt=FP32):
            return ctx.enter_context(nc.sbuf_tensor(name, shape, dt))

        m.w_cols = 512 + 2 * CH * HC + CH * P
        m.psum = ctx.enter_context(nc.psum_tensor("psum", [P, 8, 512], FP32))
        m.bank = [m.psum[:, i, :] for i in range(8)]
        m.X = sb("X", [P, B * T])
        m.xs = sb("xs", [P, 2, B, T + 1])
        m.wqkv = sb("wqkv", [P, LAYERS, 3 * INNER])
        m.w_all = sb("w_all", [P, LAYERS, m.w_cols])
        m.b1_all = sb("b1_all", [HC, LAYERS, 2 * CH])
        m.b2_all = sb("b2_all", [P, LAYERS])
        m.tab = sb("tab", [P, LAYERS * 2 * NT, 2 * FD])
        m.ident = sb("ident", [P, P])
        m.centre = sb("centre", [P, P])
        m.mean_ones = sb("mean_ones", [P, P])
        m.eps = sb("eps", [P, 1])
        m.ident_b = sb("ident_b", [P, P], BF16)
        m.ones_b = sb("ones_b", [P, P], BF16)
        m.mask_q = sb("mask_q", [P, 2, 2 * P], BF16)
        m.mask_k = sb("mask_k", [P, 3, WIN], BF16)
        scratch = nc.dram_tensor("qk_parts", (2, B, PARTS, DH, H, T), BF16, kind="Internal").ap()
        m_scratch = nc.dram_tensor("maxima", (32, P), BF16, kind="Internal").ap()

        def stream(n):
            return m.xs[:, 0, n // 2, 1 + (n % 2) * 512:1 + (n % 2 + 1) * 512]

        setup_phase(nc, m, a)
        clear_semaphores(nc, m)
        layernorm_phase(nc, m, "ln0", stream)
        clear_semaphores(nc, m)
        ffn_phase(nc, m, "f0")
        clear_semaphores(nc, m)
        layernorm_phase(nc, m, "ln1", stream)
        clear_semaphores(nc, m)
        with ExitStack() as branch:
            m.att_w, m.att_bias, m.bv_row, V, Y = (
                branch.enter_context(nc.sbuf_tensor(name, shape, FP32)) for name, shape in (
                    ("att_w", [P, 4, C]), ("att_bias", [P, 3]), ("bv_row", [P, C]),
                    ("V", [P, B * NT, C]), ("Y", [P, B * NT, C])))
            binarise_phase(nc, m, a)
            clear_semaphores(nc, m)
            project_phase(nc, m, V, scratch)
            clear_semaphores(nc, m)
            attention_phase(nc, m, a, V, Y, scratch, m_scratch)
            clear_semaphores(nc, m)
            output_phase(nc, m, Y)
            clear_semaphores(nc, m)
        layernorm_phase(nc, m, "ln2", stream)
        clear_semaphores(nc, m)
        ffn_phase(nc, m, "f1")
        clear_semaphores(nc, m)
        store_phase(nc, m, a)


def host_constants():
    return {"rot": rotary_tables(), "consts": constants(), "zeros": np.zeros((1, 4 * T // 2), np.float32)}


INPUTS = ("L0_attn_x", "L0_attn_Wq", "L0_attn_bq", "L0_attn_Wk", "L0_attn_bk", "L0_attn_Wv", "L0_attn_bv",
          "L0_attn_Wp", "L0_attn_bp", "L0_ffn_wqkv", "L0_ffn_q_scale", "L0_ffn_k_scale", "L0_ffn_wo",
          "L0_ffn_ln_g", "L0_ffn_ln_b", "L0_ffn_w1", "L0_ffn_b1", "L0_ffn_w2", "L0_ffn_b2")


def kernel(**inputs):
    import concourse.bacc as bacc
    from concourse.bass_utils import run_bass_kernel_spmd

    nc = bacc.Bacc("TRN2", target_bir_lowering=False, num_devices=1)
    arrays = {name: np.ascontiguousarray(inputs[name]) for name in INPUTS}
    arrays.update(host_constants())
    a = {name: nc.dram_tensor(f"in_{name}", v.shape, mybir.dt.from_np(v.dtype), kind="ExternalInput").ap()
         for name, v in arrays.items()}
    a["out"] = nc.dram_tensor("out", (B, T, C), FP32, kind="ExternalOutput").ap()
    build(nc, a)
    r = run_bass_kernel_spmd(nc, [{f"in_{name}": v for name, v in arrays.items()}], core_ids=[0])
    return r.results[0]["out"]
```

```python
from contextlib import ExitStack

import numpy as np

import concourse.bass as bass
from concourse import mybir

FP32 = mybir.dt.float32
BF16 = mybir.dt.bfloat16
ALU = mybir.AluOpType
ACT = mybir.ActivationFunctionType
AX = mybir.AxisListType

P = 128
B, T, C = 4, 1024, 128
NT = T // P
LAYERS = 2
FH, FD, WIN = 8, 64, 64
PAIRS = FH // 2
INNER = FH * FD
HID = int(C * 4 * 2 / 3)
CH = 3
HC = -(-HID // CH)
QK_SCALE = 8.0
H, DH = 16, 8
QUADS = H // 4
PARTS = 3
KROWS = PARTS * PARTS * DH
UNITS = 64
LEAD = UNITS // 2 + 12
STEPS = 16
SLOTS = 3
ROWS = 96
LOADS = 2 * PARTS + 1
MASKED = -1e30


def rotary_tables():
    half = np.arange(0, FD, 2, dtype=np.float32)
    inv = (np.float32(1.0) / np.float32(10000.0) ** (half / np.float32(FD))).astype(np.float32)
    t = np.arange(T, dtype=np.float32)
    freqs = (t[:, None] * inv[None, :]).astype(np.float32)
    freqs = np.concatenate([freqs, freqs], axis=-1)
    base = ((half + np.float32(0.4 * FD)) / np.float32(1.4 * FD)).astype(np.float32)
    power = ((t - T // 2) / np.float32(WIN // 2)).astype(np.float32)
    scale = (base[None, :].astype(np.float64) ** power[:, None]).astype(np.float32)
    scale = np.concatenate([scale, scale], axis=-1)
    cos, sin = np.cos(freqs), np.sin(freqs)
    sign = np.concatenate([-np.ones(FD // 2), np.ones(FD // 2)]).astype(np.float32)
    out = np.empty((2, T, 2, FD), np.float32)
    out[0, :, 0] = cos * scale * np.float32(QK_SCALE)
    out[1, :, 0] = sin * scale * sign * np.float32(QK_SCALE)
    out[0, :, 1] = cos / scale
    out[1, :, 1] = sin / scale * sign
    return np.ascontiguousarray(out.reshape(2, NT, P, 2, FD).transpose(0, 2, 1, 3, 4))


C_ID, C_CENTRE, C_MASK_Q = 0, P, 2 * P
C_MASK_K = C_MASK_Q + 4 * P
C_END = C_MASK_K + 2 * WIN


def constants():
    c = np.zeros((P, C_END), np.float32)
    c[:, C_ID:C_ID + P] = np.eye(P)
    c[:, C_CENTRE:C_CENTRE + P] = np.eye(P) - 1.0 / P
    i, j = np.arange(WIN)[:, None], np.arange(WIN)[None]
    causal, back = j <= i, i <= j
    rows = np.empty((2, 2, WIN, P), np.float32)
    for later in range(2):
        rows[later, 0] = np.concatenate([np.where(back & bool(later), 0, MASKED), np.where(causal, 0, MASKED)], axis=1)
        rows[later, 1] = np.concatenate([np.where(back, 0, MASKED), np.where(causal, 0, MASKED)], axis=1)
    for head in range(2):
        c[head * WIN:(head + 1) * WIN, C_MASK_Q:C_MASK_K] = rows.transpose(2, 0, 1, 3).reshape(WIN, 4 * P)
    for k, mask in enumerate((rows[0, 0], rows[1, 0])):
        c[:, C_MASK_K + k * WIN:C_MASK_K + (k + 1) * WIN] = mask.T
    return c


class Memory:

    def __init__(self):
        self.used_semaphores = []


def semaphore(nc, m, ctx, name):
    handle = ctx.enter_context(nc.semaphore(name))
    m.used_semaphores.append(handle)
    return handle


def clear_semaphores(nc, m):
    numbers = sorted(handle.num for handle in m.used_semaphores)
    while numbers:
        run = 1
        while run < len(numbers) and numbers[run] == numbers[0] + run:
            run += 1
        nc.sync.sem_clear(range(numbers[0], numbers[0] + run))
        del numbers[:run]
    m.used_semaphores.clear()
    nc.all_engine_barrier()


class LayerNorm:

    def __init__(self, nc, m, ctx, name, dst):
        self.nc, self.m, self.dst = nc, m, dst
        self.sq, self.log_var, self.rstd = (
            ctx.enter_context(nc.sbuf_tensor(f"{name}_{n}", [P, 2, 512], FP32)) for n in ("sq", "log_var", "rstd"))
        self.centred, self.squared, self.varred, self.logged, self.rstd_ready, self.normed = (
            semaphore(nc, m, ctx, f"{name}_{n}")
            for n in ("centred", "squared", "varred", "logged", "rstd_ready", "normed"))

    def tensor(self, pe):
        nc, m, N = self.nc, self.m, B * T // 512
        for n in range(N + 1):
            if n < N:
                if n >= 4:
                    pe.wait_ge(self.normed, n - 3)
                nc.tensor.matmul(m.bank[n % 4][:, :], m.centre[:, :], m.X[:, n * 512:(n + 1) * 512],
                                 start=True, stop=True).then_inc(self.centred, 1)
            if n >= 1:
                k = n - 1
                pe.wait_ge(self.squared, k + 1)
                if k >= 2:
                    pe.wait_ge(self.logged, k - 1)
                nc.tensor.matmul(m.bank[4 + k % 2][:, :], m.mean_ones[:, :], self.sq[:, k % 2, :],
                                 start=True, stop=True).then_inc(self.varred, 1)

    def scalar(self, act):
        nc, m, N = self.nc, self.m, B * T // 512
        nc.scalar.preload_act_table_set("natural_log_exp_and_others")
        for n in range(N + 1):
            if n < N:
                act.wait_ge(self.centred, n + 1)
                if n >= 2:
                    act.wait_ge(self.varred, n - 1)
                nc.scalar.activation(self.sq[:, n % 2, :], m.bank[n % 4][:, :], ACT.Square).then_inc(self.squared, 1)
            if n >= 1:
                k = n - 1
                act.wait_ge(self.varred, k + 1)
                nc.scalar.activation(self.log_var[:, k % 2, :], m.bank[4 + k % 2][:, :], ACT.Ln,
                                     bias=m.eps[:, :]).then_inc(self.logged, 1)
                act.wait_ge(self.logged, k + 1)
                if k >= 2:
                    act.wait_ge(self.normed, k - 1)
                nc.scalar.activation(self.rstd[:, k % 2, :], self.log_var[:, k % 2, :], ACT.Exp,
                                     scale=-0.5).then_inc(self.rstd_ready, 1)

    def vector(self, dve):
        nc, m, N = self.nc, self.m, B * T // 512
        for n in range(N):
            dve.wait_ge(self.rstd_ready, n + 1)
            nc.vector.tensor_tensor(self.dst(n), m.bank[n % 4][:, :], self.rstd[:, n % 2, :], ALU.mult).then_inc(self.normed, 1)


def layernorm_phase(nc, m, name, dst):
    ctx = ExitStack()
    with ctx:
        norm = LayerNorm(nc, m, ctx, name, dst)
        block = ctx.enter_context(nc.Block())

        @block.tensor
        def _(pe):
            norm.tensor(pe)

        @block.scalar
        def _(act):
            norm.scalar(act)

        @block.vector
        def _(dve):
            norm.vector(dve)


def setup_phase(nc, m, a, dst):
    ctx = ExitStack()
    with ctx:
        def sb(name, shape, dt=FP32):
            return ctx.enter_context(nc.sbuf_tensor(name, shape, dt))

        def sem(name):
            return semaphore(nc, m, ctx, name)

        x_rows = sb("su_x_rows", [P, B * NT, C])
        consts = sb("su_consts", [P, C_END])
        base = sb("su_base", [P, 2, NT, 2, FD])
        scales = sb("su_scales", [P, 2, LAYERS, 2, FD])
        ln_g = sb("su_ln_g", [P, LAYERS])
        ln_b = sb("su_ln_b", [P, LAYERS])
        b1_raw = sb("su_b1_raw", [HC, LAYERS, 2 * CH])

        zeroed = sem("su_zeroed")
        x_in = sem("su_x_in")
        c_in = sem("su_c_in")
        w_in = sem("su_w_in")
        qkv_in = sem("su_qkv_in")
        t_in = sem("su_t_in")
        ready = sem("su_ready")
        x_tr = sem("su_x_tr")
        x_ev = sem("su_x_ev")
        bias_mm = sem("su_bias_mm")
        bias_done = sem("su_bias_done")
        tables = sem("su_tables")
        norm = LayerNorm(nc, m, ctx, "ln0", dst)
        ctx.enter_context(nc.allow_non_contiguous_dma(reason="a few columns of parameters"))
        block = ctx.enter_context(nc.Block())

        chunks = [(0, CH - 1, HC), (CH - 1, 1, HID - (CH - 1) * HC)]
        w_total = LAYERS * (2 + len(chunks))

        @block.sync
        def _(sp):
            sp.dma_start(consts[:, :], a["consts"]).then_inc(c_in, 16)
            for b in range(B):
                sp.dma_start(x_rows[:, b * NT:(b + 1) * NT, :],
                             a["L0_attn_x"][b].rearrange("(t p) c -> p t c", p=P)).then_inc(x_in, 16)
            sp.wait_ge(zeroed, 1)
            for l in range(LAYERS):
                dst = m.w_all[:, l, 512:512 + 2 * CH * HC].rearrange("p (g n) -> p g n", g=2)
                sp.dma_start(dst[:, :, 0:HID], a["L0_ffn_w1"][l].rearrange("p (g n) -> p g n", g=2)).then_inc(w_in, 16)
                for k, count, n in chunks:
                    o = 512 + 2 * CH * HC + k * P
                    sp.dma_start(m.w_all[0:n, l, o:o + count * P].rearrange("p (k c) -> p k c", k=count),
                                 a["L0_ffn_w2"][l, k * HC:k * HC + count * n, :].rearrange("(k p) c -> p k c", k=count)
                                 ).then_inc(w_in, 16)
                sp.dma_start(m.w_all[:, l, 0:512].rearrange("p (k c) -> p k c", k=4),
                             a["L0_ffn_wo"][l].rearrange("(k p) c -> p k c", p=P)).then_inc(w_in, 16)
            sp.dma_start(m.wqkv[:, :, :], a["L0_ffn_wqkv"].rearrange("l p n -> p l n")).then_inc(qkv_in, 16)
            sp.wait_ge(w_in, 16 * w_total)
            sp.wait_ge(qkv_in, 16)

        @block.gpsimd
        def _(pool):
            nc.gpsimd.memset(m.w_all[:, :, 512:], 0.0)
            nc.gpsimd.memset(b1_raw[:, :, :], 0.0)
            nc.gpsimd.memset(m.xs[:, :, :, 0:1], 0.0)
            nc.gpsimd.memset(m.eps[:, :], 1e-5)
            nc.gpsimd.memset(m.mean_ones[:, :], 1.0 / C).then_inc(zeroed, 1)

        @block.scalar
        def _(act):
            act.wait_ge(zeroed, 1)
            for q, name in enumerate(("L0_ffn_q_scale", "L0_ffn_k_scale")):
                rows = a[name].rearrange("(a l) d -> a l d", a=1)
                act.dma_start(scales[:, 0, :, q, :], rows.broadcast_to([P, LAYERS, FD])).then_inc(t_in, 16)
                for h in range(2):
                    o = 32 * h
                    act.dma_start(scales[:, 1, :, q, 32 - o:64 - o],
                                  rows[:, :, o:o + 32].broadcast_to([P, LAYERS, 32])).then_inc(t_in, 16)
            for k in range(CH):
                n = min(HC, HID - k * HC)
                act.dma_start(b1_raw[0:n, :, k::CH],
                              a["L0_ffn_b1"].rearrange("l (g n) -> n l g", g=2)[k * HC:k * HC + n, :, :]).then_inc(t_in, 16)
            act.dma_start(ln_b[:, :], a["L0_ffn_ln_b"].rearrange("l p -> p l")).then_inc(t_in, 16)
            act.dma_start(ln_g[:, :], a["L0_ffn_ln_g"].rearrange("l p -> p l")).then_inc(t_in, 16)
            act.dma_start(m.b2_all[:, :], a["L0_ffn_b2"].rearrange("l p -> p l")).then_inc(t_in, 16)
            act.dma_start(base[:, :, :, :, :], a["rot"].rearrange("a p t q d -> p a t q d")).then_inc(t_in, 16)

            norm.scalar(act)

        t_total = 6 + CH + 4

        @block.vector
        def _(dve):
            dve.wait_ge(c_in, 16)
            nc.vector.tensor_copy(m.ident[:, :], consts[:, C_ID:C_ID + P])
            nc.vector.tensor_copy(m.centre[:, :], consts[:, C_CENTRE:C_CENTRE + P])
            nc.vector.tensor_copy(m.ident_b[:, :], consts[:, C_ID:C_ID + P])
            nc.vector.memset(m.ones_b[:, :], 1.0)
            nc.vector.tensor_copy(m.mask_q[:, :, :], consts[:, C_MASK_Q:C_MASK_K].rearrange("p (a n) -> p a n", a=2))
            nc.vector.tensor_copy(m.mask_k[:, :, :], consts[:, C_MASK_K:C_MASK_K + 2 * WIN].rearrange(
                "p (a n) -> p a n", a=2)).then_inc(ready, 1)
            for n in range(B * NT // 4):
                dve.wait_ge(x_tr, n + 1)
                nc.vector.tensor_copy(m.X[:, n * 512:(n + 1) * 512], m.bank[n % 4][:, :]).then_inc(x_ev, 1)
            norm.vector(dve)
            dve.wait_ge(t_in, 16 * t_total)
            for l in range(LAYERS):
                for k in range(2):
                    nc.vector.tensor_tensor(
                        m.tab[:, (l * 2 + k) * NT:(l * 2 + k + 1) * NT, :], base[:, k, :, :, :].rearrange("p t q d -> p t (q d)"),
                        scales[:, k, l, :, :].rearrange("p q d -> p (q d)").unsqueeze(1).broadcast_to([P, NT, 2 * FD]),
                        ALU.mult)
            dve.wait_ge(bias_mm, 1)
            nc.vector.tensor_tensor(m.b1_all[:, :, :], m.bank[7][0:HC, 0:LAYERS * 2 * CH].rearrange("p (l k) -> p l k", l=LAYERS),
                                    b1_raw[:, :, :], ALU.add)
            for l in range(LAYERS):
                last = nc.vector.tensor_scalar(m.w_all[:, l, 512:512 + 2 * CH * HC], m.w_all[:, l, 512:512 + 2 * CH * HC],
                                               ln_g[:, l:l + 1], None, ALU.mult)
            last.then_inc(tables, 1)

        @block.tensor
        def _(pe):
            pe.wait_ge(ready, 1)
            for n in range(B * NT // 4):
                if n == 0:
                    pe.wait_ge(x_in, 16 * B)
                if n >= 4:
                    pe.wait_ge(x_ev, n - 3)
                for i in range(4):
                    last = nc.tensor.transpose(m.bank[n % 4][:, i * P:(i + 1) * P], x_rows[:, 4 * n + i, :], m.ident[:, :])
                last.then_inc(x_tr, 1)
            pe.wait_ge(x_ev, B * NT // 4)
            pe.wait_ge(zeroed, 1)
            norm.tensor(pe)
            pe.wait_ge(w_in, 16 * w_total)
            pe.wait_ge(t_in, 16 * t_total)
            for l in range(LAYERS):
                for k in range(2 * CH):
                    last = nc.tensor.matmul(m.bank[7][0:HC, l * 2 * CH + k:l * 2 * CH + k + 1],
                                            m.w_all[:, l, 512 + k * HC:512 + (k + 1) * HC], ln_b[:, l:l + 1],
                                            start=True, stop=True)
            last.then_inc(bias_mm, 1)


def ffn_phase(nc, m, name):
    ctx = ExitStack()
    with ctx:
        def sb(n, shape, dt=FP32):
            return ctx.enter_context(nc.sbuf_tensor(f"{name}_{n}", shape, dt))

        def sem(n):
            return semaphore(nc, m, ctx, f"{name}_{n}")

        hT = sb("hT", [P, B, P])
        rot = [sb(f"rot{b}", [P, 2 * INNER]) for b in range(B)]
        rot2 = [sb(f"rot2{i}", [P, 2 * INNER]) for i in range(2)]
        sq = [sb(f"sq{i}", [P, 2 * INNER]) for i in range(2)]
        ss = sb("ss", [P, B, 2 * FH])
        ssc = sb("ssc", [P, B, 2 * FH])
        log_ss = sb("log_ss", [P, B, 2 * FH])
        rnorm = sb("rnorm", [P, B, 2 * FH])
        q_pad = [sb(f"q_pad{b}", [P, PAIRS, 2, 2, WIN]) for b in range(B)]
        k_blk = [sb(f"k_blk{b}", [P, PAIRS, 3, WIN]) for b in range(B)]
        q_rnd = [sb(f"q_rnd{i}", [P, PAIRS, 2, 2, WIN], BF16) for i in range(2)]
        k_rnd = [sb(f"k_rnd{i}", [P, PAIRS, 3, WIN], BF16) for i in range(2)]
        v_cur = [sb(f"v_cur{b}", [P, FH, FD + 1]) for b in range(B)]
        v_mix = [sb(f"v_mix{b}", [P, FH, FD + 1]) for b in range(B)]
        neg_max = sb("neg_max", [P, B, PAIRS * 2])
        diag = [sb(f"diag{i}", [P, 2, PAIRS, P], BF16) for i in range(2)]
        rden = sb("rden", [P, B, FH])
        o = [sb(f"o{i}", [P, INNER]) for i in range(2)]
        oT = sb("oT", [P, 4, B, P])
        x1 = sb("x1", [P, B, P + 1])
        h2 = sb("h2", [P, B, P])
        hn = sb("hn", [P, B * P])
        u = sb("u", [HC, CH, B * P])

        zeroed, ht_staged, x1_zero, x1_before = (
            sem(s) for s in ("zeroed", "ht_staged", "x1_zero", "x1_before"))
        kprev_done, vprev_done, vmix_done = ([sem(f"{s}{b}") for b in range(B)]
                                             for s in ("kprev_done", "vprev_done", "vmix_done"))
        per_b = ("qk_ready", "v_ready", "sq_ready", "ss_ready", "ssc_ready", "rn_log", "rn_ready",
                 "rot_done", "add_done", "qkn_ready", "tr_ready", "qk_evicted", "rounded",
                 "v_evicted", "s_ready", "max_ready", "d_ready", "st_ready", "p_ready",
                 "pv_ready", "rd_ready", "o_ready", "ot_ready", "ot_evicted")
        per_it = ("wo_ready", "x1_done", "h2_staged", "cen_ready", "csq_ready", "var_ready",
                  "lv_ready", "rstd_ready", "hn_ready", "w2_ready", "out_done")
        (qk_ready, v_ready, sq_ready, ss_ready, ssc_ready, rn_log, rn_ready,
         rot_done, add_done, qkn_ready, tr_ready, qk_evicted, rounded,
         v_evicted, s_ready, max_ready, d_ready, st_ready, p_ready,
         pv_ready, rd_ready, o_ready, ot_ready, ot_evicted) = [sem(s) for s in per_b]
        (wo_ready, x1_done, h2_staged, cen_ready, csq_ready, var_ready,
         lv_ready, rstd_ready, hn_ready, w2_ready, out_done) = [sem(s) for s in per_it]
        a_ready, g_ready, gelu_done, u_ready = sem("a_ready"), sem("g_ready"), sem("gelu_done"), sem("u_ready")

        block = ctx.enter_context(nc.Block())

        qk_pair = m.psum[:, 0:2, :]

        def pair(b):
            return m.psum[:, 2 + 2 * (b % 2):4 + 2 * (b % 2), :]

        V_BANK = A_BANK = m.bank[6]
        G_BANK = m.bank[7]

        def ag_banks(k, alone):
            return (m.bank[2 * k], m.bank[2 * k + 1]) if alone else (A_BANK, G_BANK)

        class Tile:

            def __init__(self, l, t, it):
                self.l, self.t, self.it = l, t, it
                self.later = (t + NT - 1) // NT

            def cur(self, b):
                return self.it * B + (B + b + 1)

            def prev(self, b):
                return self.it * B + (b + 1)

            def now(self):
                return self.it + 2

            def before(self):
                return self.it + 1

            def chunk(self, k):
                return self.it * CH + (k + 1)

            def copied(self, copies=1):
                return self.it * (16 * copies) + 16 * copies

        def tile(it):
            return Tile(it // NT, it % NT, it)

        def turns(engine, turn, before_layer=None):
            turn(None, None, tile(0))
            turn(tile(0), None, tile(1))
            for l in range(LAYERS):
                last = l == LAYERS - 1
                if before_layer is not None:
                    before_layer(l)
                with engine.Fori(0, NT - 2 if last else NT) as t:
                    def ahead(k):
                        it = t + (l * NT + k)
                        return Tile(l, t + k, it) if last else Tile(it // NT, it % NT, it)
                    turn(ahead(1), Tile(l, t, t + l * NT), ahead(2))
            turn(tile(LAYERS * NT - 1), tile(LAYERS * NT - 2), None)
            turn(None, tile(LAYERS * NT - 1), None)

        @block.tensor
        def _(pe):
            for s in (qk_ready, v_ready, tr_ready, s_ready, st_ready, pv_ready, ot_ready):
                pe.sem_inc(s, B)
            for s in (wo_ready, cen_ready, var_ready, w2_ready):
                pe.sem_inc(s, 1)

            def project(n, b, f=None):
                pe.wait_ge(ht_staged, n.copied(2))
                pe.wait_ge(rot_done, n.cur(b) - 1)
                pe.wait_ge(sq_ready, n.cur(b) - 1)
                for i in range(2):
                    last = nc.tensor.matmul(qk_pair[:, i, :], hT[:, b, :],
                                            m.wqkv[:, bass.ds(n.l, 1), i * INNER:(i + 1) * INNER].rearrange("p a n -> p (a n)"),
                                            start=True, stop=True)
                last.then_inc(qk_ready, 1)
                if b:
                    pe.wait_ge(v_evicted, n.cur(b) - 1)
                elif f:
                    pe.wait_ge(u_ready, f.chunk(CH - 1))
                nc.tensor.matmul(V_BANK[:, :], hT[:, b, :],
                                 m.wqkv[:, bass.ds(n.l, 1), 2 * INNER:3 * INNER].rearrange("p a n -> p (a n)"),
                                 start=True, stop=True).then_inc(v_ready, 1)

            def turn_qk(n, b):
                pe.wait_ge(qkn_ready, n.cur(b))
                pe.wait_ge(ot_evicted, n.cur(b) - 2)
                for i in range(8):
                    last = nc.tensor.transpose(pair(b)[:, i // 4, (i % 4) * P:(i % 4 + 1) * P],
                                               rot[b][:, i * P:(i + 1) * P], m.ident[:, :])
                last.then_inc(tr_ready, 1)

            def scores(n, b):
                pe.wait_ge(rounded, n.cur(b))
                for i in range(2):
                    nc.tensor.matmul(pair(b)[:, i, :].rearrange("p (j n) -> p j n", j=2), m.ident_b[:, :],
                                     m.mask_q[:, bass.ds(n.later, 1), :].broadcast_to([P, 2, 2 * P]),
                                     start=True, stop=False, skip_group_check=True)
                for j in range(PAIRS):
                    for w in range(2):
                        o_ = (j % 2 * 2 + w) * P
                        last = nc.tensor.matmul(
                            pair(b)[:, j // 2, o_:o_ + P], q_rnd[b % 2][:, j, w, :, :].rearrange("p h i -> p (h i)"),
                            k_rnd[b % 2][:, j, w:w + 2, :].rearrange("p a j -> p (a j)"),
                            start=False, stop=True, skip_group_check=True)
                last.then_inc(s_ready, 1)

            def scores_turned(n, b):
                pe.wait_ge(d_ready, n.cur(b))
                for w in range(2):
                    mask = m.mask_k[:, bass.ds(n.later, 1), :] if w == 0 else m.mask_k[:, 1:2, :]
                    nc.tensor.matmul(pair(b)[:, w, :].rearrange("p (h i) -> p h i", h=FH), m.ident_b[:, :],
                                     mask.broadcast_to([P, FH, WIN]),
                                     start=True, stop=False, skip_group_check=True)
                    nc.tensor.matmul(pair(b)[:, w, :], m.ones_b[:, :], diag[b % 2][:, w, :, :].rearrange("p j i -> p (j i)"),
                                     start=False, stop=False, skip_group_check=True)
                    for j in range(PAIRS):
                        last = nc.tensor.matmul(
                            pair(b)[:, w, j * P:(j + 1) * P], k_blk[b][:, j, w:w + 2, :].rearrange("p a j -> p (a j)"),
                            q_pad[b][:, j, w, :, :].rearrange("p h i -> p (h i)"),
                            start=False, stop=True, skip_group_check=True)
                last.then_inc(st_ready, 1)

            def outputs(n, b):
                pe.wait_ge(p_ready, n.cur(b))
                pe.wait_ge(v_evicted, n.cur(b))
                pe.wait_ge(vmix_done[b], n.copied() + 16)
                pe.wait_ge(vprev_done[b], n.copied())
                probs = rot[b][:, :].rearrange("p (w h i) -> p w h i", w=2, h=FH)
                for h in range(FH):
                    for w in range(2):
                        last = nc.tensor.matmul(
                            pair(b)[WIN * w:WIN * (w + 1), h // 4, (h % 4) * (FD + 1):(h % 4 + 1) * (FD + 1)],
                            probs[:, w, h, :], (v_cur if w else v_mix)[b][:, h, :], start=True, stop=True)
                last.then_inc(pv_ready, 1)

            def turn_outputs(n, b):
                pe.wait_ge(o_ready, n.cur(b))
                for i in range(4):
                    last = nc.tensor.transpose(pair(b)[:, 0, i * P:(i + 1) * P], o[b % 2][:, i * P:(i + 1) * P], m.ident[:, :])
                last.then_inc(ot_ready, 1)

            def project_out(f):
                pe.wait_ge(ot_evicted, f.cur(B - 1))
                pe.wait_ge(out_done, f.it + NT)
                for k in range(4):
                    last = nc.tensor.matmul(G_BANK[:, :], m.w_all[:, f.l, k * P:(k + 1) * P],
                                            oT[:, k, :, :].rearrange("p b t -> p (b t)"), start=k == 0, stop=k == 3)
                last.then_inc(wo_ready, 1)

            def centre(f):
                pe.wait_ge(h2_staged, f.now())
                nc.tensor.matmul(G_BANK[:, :], m.centre[:, :], h2[:, :, :].rearrange("p b t -> p (b t)"),
                                 start=True, stop=True).then_inc(cen_ready, 1)

            def variance(f, n):
                if n:
                    pe.wait_ge(v_evicted, n.cur(B - 1))
                pe.wait_ge(csq_ready, f.now())
                nc.tensor.matmul(A_BANK[:, :], m.mean_ones[:, :], hn[:, :], start=True, stop=True).then_inc(var_ready, 1)

            def gated(f, k, alone=False):
                a_bank, g_bank = ag_banks(k, alone)
                if k == 0:
                    pe.wait_ge(hn_ready, f.now())
                elif not alone:
                    pe.wait_ge(u_ready, f.chunk(k - 1))
                nc.tensor.matmul(a_bank[0:HC, :], m.w_all[:, f.l, 512 + k * HC:512 + (k + 1) * HC],
                                 hn[:, :], start=True, stop=True).then_inc(a_ready, 1)
                nc.tensor.matmul(g_bank[0:HC, :], m.w_all[:, f.l, 512 + (CH + k) * HC:512 + (CH + k + 1) * HC],
                                 hn[:, :], start=True, stop=True).then_inc(g_ready, 1)

            def project_down(f, alone=False):
                for k in range(CH):
                    if alone or k == 0:
                        pe.wait_ge(u_ready, f.chunk(k if alone else CH - 1))
                    last = nc.tensor.matmul(G_BANK[:, :], m.w_all[0:HC, f.l, 512 + 2 * CH * HC + k * P:512 + 2 * CH * HC + (k + 1) * P],
                                            u[:, k, :], start=k == 0, stop=k == CH - 1)
                last.then_inc(w2_ready, 1)

            def turn(n, f, x):
                if n:
                    turn_qk(n, 0)
                    turn_qk(n, 1)
                    project(n, 2)
                if f:
                    project_out(f)
                if n:
                    scores(n, 0)
                    scores(n, 1)
                if f:
                    centre(f)
                if n:
                    project(n, 3)
                    scores_turned(n, 0)
                if f:
                    variance(f, n)
                if n:
                    scores_turned(n, 1)
                    outputs(n, 0)
                if f:
                    gated(f, 0, n is None)
                if n:
                    outputs(n, 1)
                    turn_outputs(n, 0)
                if f:
                    gated(f, 1, n is None)
                if n:
                    turn_outputs(n, 1)
                    turn_qk(n, 2)
                    turn_qk(n, 3)
                if f:
                    gated(f, 2, n is None)
                if x:
                    project(x, 0, f)
                if n:
                    scores(n, 2)
                    scores(n, 3)
                if f:
                    project_down(f, n is None)
                if x:
                    project(x, 1)
                if n:
                    scores_turned(n, 2)
                    scores_turned(n, 3)
                    outputs(n, 2)
                    outputs(n, 3)
                    turn_outputs(n, 2)
                    turn_outputs(n, 3)

            turns(pe, turn)

        @block.scalar
        def _(act):
            for s in (sq_ready, v_evicted, rn_log, rn_ready, qk_evicted, p_ready, ot_evicted):
                act.sem_inc(s, B)
            for s in (csq_ready, lv_ready, rstd_ready):
                act.sem_inc(s, 1)
            for b in range(B):
                act.sem_inc(vmix_done[b], 16)
            def squares(n, b):
                act.wait_ge(qk_ready, n.cur(b))
                act.wait_ge(ss_ready, n.cur(b) - 2)
                nc.scalar.activation(sq[b % 2][:, :], qk_pair, ACT.Square).then_inc(sq_ready, 1)

            def values(n, b):
                if isinstance(n.it, int):
                    act.wait_ge(zeroed, 1)
                act.wait_ge(v_ready, n.cur(b))
                act.wait_ge(pv_ready, n.prev(b))
                act.wait_ge(vprev_done[b], n.copied())
                act.wait_ge(vmix_done[b], n.copied())
                nc.scalar.activation(v_cur[b][:, :, 0:FD], V_BANK[:, :].rearrange("p (h d) -> p h d", h=FH),
                                     ACT.Copy).then_inc(v_evicted, 1)

            def norms(n, b):
                act.wait_ge(ssc_ready, n.cur(b))
                nc.scalar.activation(log_ss[:, b, :], ssc[:, b, :], ACT.Ln).then_inc(rn_log, 1)
                act.wait_ge(rn_log, n.cur(b))
                act.wait_ge(qkn_ready, n.prev(b))
                nc.scalar.activation(rnorm[:, b, :], log_ss[:, b, :], ACT.Exp, scale=-0.5).then_inc(rn_ready, 1)

            def evict_qk(n, b):
                if isinstance(n.it, int):
                    act.wait_ge(zeroed, 2)
                act.wait_ge(tr_ready, n.cur(b))
                act.wait_ge(st_ready, n.prev(b))
                act.wait_ge(kprev_done[b], n.copied())
                nc.scalar.activation(k_blk[b][:, :, 1:3, :], pair(b)[:, 1, :].rearrange("p (j w i) -> p j w i", j=PAIRS, w=2), ACT.Copy)
                qt = pair(b)[:, 0, :].rearrange("p (j w i) -> p j w i", j=PAIRS, w=2)
                nc.scalar.activation(q_pad[b][0:64, :, :, 0, :], qt[0:64], ACT.Copy)
                nc.scalar.activation(q_pad[b][64:128, :, :, 1, :], qt[64:128], ACT.Copy).then_inc(qk_evicted, 1)

            def square_centred(f):
                act.wait_ge(cen_ready, f.now())
                nc.scalar.activation(hn[:, :], G_BANK[:, :], ACT.Square).then_inc(csq_ready, 1)

            def deviation(f):
                act.wait_ge(var_ready, f.now())
                nc.scalar.activation(hn[:, :], A_BANK[:, :], ACT.Ln, bias=m.eps[:, :]).then_inc(lv_ready, 1)
                act.wait_ge(lv_ready, f.now())
                nc.scalar.activation(hn[:, :], hn[:, :], ACT.Exp, scale=-0.5).then_inc(rstd_ready, 1)

            def gelu(f, k, alone=False):
                act.wait_ge(g_ready, f.chunk(k))
                nc.scalar.activation(u[:, k, :], ag_banks(k, alone)[1][0:HC, :], ACT.Gelu,
                                     bias=m.b1_all[:, f.l, CH + k:CH + k + 1]).then_inc(gelu_done, 1)

            def exponentials(n, b):
                act.wait_ge(st_ready, n.cur(b))
                nc.scalar.activation(rot[b][:, :].rearrange("p (w n) -> p w n", w=2), pair(b), ACT.Exp).then_inc(p_ready, 1)

            def evict_outputs(n, b):
                act.wait_ge(ot_ready, n.cur(b))
                act.wait_ge(wo_ready, n.before())
                nc.scalar.activation(oT[:, :, b, :], pair(b)[:, 0, :].rearrange("p (k t) -> p k t", k=4),
                                     ACT.Copy).then_inc(ot_evicted, 1)

            def turn(n, f, x):
                if not n:
                    nc.scalar.preload_act_table_set("natural_log_exp_and_others")
                if n:
                    evict_qk(n, 0)
                    evict_qk(n, 1)
                    squares(n, 2)
                    values(n, 2)
                    norms(n, 2)
                if f:
                    square_centred(f)
                if n:
                    squares(n, 3)
                    values(n, 3)
                    exponentials(n, 0)
                if f:
                    deviation(f)
                if n:
                    norms(n, 3)
                    exponentials(n, 1)
                if f:
                    gelu(f, 0, n is None)
                if n:
                    evict_outputs(n, 0)
                if f:
                    gelu(f, 1, n is None)
                if n:
                    evict_outputs(n, 1)
                    evict_qk(n, 2)
                    evict_qk(n, 3)
                if f:
                    gelu(f, 2, n is None)
                    if n:
                        nc.scalar.preload_act_table_set("natural_log_exp_and_others")
                if x:
                    squares(x, 0)
                    values(x, 0)
                    norms(x, 0)
                    squares(x, 1)
                    values(x, 1)
                if n:
                    exponentials(n, 2)
                if x:
                    norms(x, 1)
                if n:
                    exponentials(n, 3)
                    evict_outputs(n, 2)
                    evict_outputs(n, 3)

            turns(act, turn)

        @block.vector
        def _(dve):
            for s in (ss_ready, ssc_ready, rot_done, qkn_ready, rounded, max_ready, rd_ready, o_ready):
                dve.sem_inc(s, B)
            for s in (x1_done, h2_staged, hn_ready):
                dve.sem_inc(s, 1)
            nc.vector.memset(x1[:, :, :], 0.0).then_inc(x1_zero, 1)
            dve.sem_inc(out_done, NT)

            def before_layer(l):
                dve.wait_ge(out_done, l * NT + NT)
                dve.wait_ge(x1_zero, l + 1)
                nc.vector.memset(x1[:, :, P:P + 1], 0.0).then_inc(x1_zero, 1)
                dve.wait_ge(x1_zero, l + 2)

            def rotate(n, b):
                qk = qk_pair.rearrange("p q (h d) -> p q h d", h=FH)
                dve.wait_ge(sq_ready, n.cur(b))
                dve.wait_ge(pv_ready, n.prev(b))
                one = m.tab[:, bass.ds(n.l * (2 * NT) + n.t, 1), :].rearrange("p a (q d) -> p (a q) d", q=2).unsqueeze(2).broadcast_to([P, 2, FH, FD])
                nc.vector.tensor_tensor(rot[b][:, :].rearrange("p (q h d) -> p q h d", q=2, h=FH), qk, one, ALU.mult)
                dve.wait_ge(add_done, n.cur(b) - 2)
                two = m.tab[:, bass.ds(n.l * (2 * NT) + n.t + NT, 1), :].rearrange("p a (q d) -> p (a q) d", q=2).unsqueeze(2).broadcast_to([P, 2, FH, FD])
                dst = rot2[b % 2][:, :].rearrange("p (q h d) -> p q h d", q=2, h=FH)
                for i in range(2):
                    last = nc.vector.tensor_tensor(dst[:, :, :, 32 * i:32 * i + 32], qk[:, :, :, 32 - 32 * i:64 - 32 * i],
                                                   two[:, :, :, 32 * i:32 * i + 32], ALU.mult)
                last.then_inc(rot_done, 1)

            def sums(n, b):
                nc.vector.tensor_reduce(ss[:, b, :], sq[b % 2][:, :].rearrange("p (h d) -> p h d", d=FD),
                                        AX.X, ALU.add).then_inc(ss_ready, 1)
                dve.wait_ge(ss_ready, n.cur(b))
                dve.wait_ge(rn_log, n.prev(b))
                nc.vector.tensor_scalar(ssc[:, b, :], ss[:, b, :], 1e-24, None, ALU.max).then_inc(ssc_ready, 1)

            def normalise(n, b):
                dve.wait_ge(add_done, n.cur(b))
                dve.wait_ge(rn_ready, n.cur(b))
                r = rot[b][:, :].rearrange("p (h d) -> p h d", d=FD)
                nc.vector.tensor_tensor(r, r, rnorm[:, b, :].unsqueeze(2).broadcast_to([P, 2 * FH, FD]),
                                        ALU.mult).then_inc(qkn_ready, 1)

            def round_qk(n, b):
                dve.wait_ge(qk_evicted, n.cur(b))
                dve.wait_ge(s_ready, n.cur(b) - 2)
                nc.vector.tensor_copy(q_rnd[b % 2][:, :, :, :, :].rearrange("p j w h i -> p (j w h i)"),
                                      q_pad[b][:, :, :, :, :].rearrange("p j w h i -> p (j w h i)"))
                dve.wait_ge(kprev_done[b], n.copied())
                nc.vector.tensor_copy(k_rnd[b % 2][:, :, :, :].rearrange("p j a i -> p (j a i)"),
                                      k_blk[b][:, :, :, :].rearrange("p j a i -> p (j a i)")).then_inc(rounded, 1)

            def maximum(n, b):
                dve.wait_ge(s_ready, n.cur(b))
                nc.vector.tensor_reduce(neg_max[:, b, :], pair(b).rearrange("p a (h j) -> p (a h) j", h=4),
                                        AX.X, ALU.max, negate=True).then_inc(max_ready, 1)

            def divide(n, b):
                dve.wait_ge(pv_ready, n.cur(b))
                out = pair(b)[:, :, 0:4 * (FD + 1)].rearrange("p a (h d) -> p a h d", h=4)
                nc.vector.reciprocal(rden[:, b, :].rearrange("p (a h) -> p a h", a=2), out[:, :, :, FD]).then_inc(rd_ready, 1)
                dve.wait_ge(rd_ready, n.cur(b))
                dve.wait_ge(ot_ready, n.cur(b) - 2)
                nc.vector.tensor_tensor(o[b % 2][:, :].rearrange("p (a h d) -> p a h d", a=2, h=4), out[:, :, :, 0:FD],
                                        rden[:, b, :].rearrange("p (a h) -> p a h", a=2).unsqueeze(3).broadcast_to([P, 2, 4, FD]),
                                        ALU.mult).then_inc(o_ready, 1)

            def add_attention(f):
                x_in = m.xs[:, f.l, :, bass.ds(f.t * P + 1, P)]
                dve.wait_ge(x1_zero, 1)
                dve.wait_ge(out_done, f.it + NT)
                nc.vector.tensor_copy(x1[:, :, 0:1], x1[:, :, P:P + 1]).then_inc(x1_before, 1)
                dve.wait_ge(x1_before, f.it + 1)
                dve.wait_ge(wo_ready, f.now())
                nc.vector.tensor_tensor(x1[:, :, 1:P + 1], G_BANK[:, :].rearrange("p (b t) -> p b t", b=B),
                                        x_in, ALU.add).then_inc(x1_done, 1)
                dve.wait_ge(x1_done, f.now())
                nc.vector.tensor_copy(h2[0:64, :, :], x1[0:64, :, 1:P + 1])
                nc.vector.tensor_copy(h2[64:128, :, :], x1[64:128, :, 0:P]).then_inc(h2_staged, 1)

            def scale_centred(f):
                dve.wait_ge(rstd_ready, f.now())
                nc.vector.tensor_tensor(hn[:, :], G_BANK[:, :], hn[:, :], ALU.mult).then_inc(hn_ready, 1)

            def gate(f, k, alone=False):
                dve.wait_ge(a_ready, f.chunk(k))
                dve.wait_ge(gelu_done, f.chunk(k))
                nc.vector.scalar_tensor_tensor(u[:, k, :], ag_banks(k, alone)[0][0:HC, :], m.b1_all[:, f.l, k:k + 1], u[:, k, :],
                                               ALU.add, ALU.mult).then_inc(u_ready, 1)

            def add_gated(f):
                x_out = m.xs[:, 1 - f.l, :, bass.ds(f.t * P + 1, P)]
                dve.wait_ge(x1_zero, 1)
                dve.wait_ge(w2_ready, f.now())
                nc.vector.scalar_tensor_tensor(x_out, G_BANK[:, :].rearrange("p (b t) -> p b t", b=B), m.b2_all[:, f.l:f.l + 1],
                                               x1[:, :, 1:P + 1], ALU.add, ALU.add).then_inc(out_done, 1)
                if f.l == LAYERS - 1:
                    x = m.X[:, :].rearrange("p (b t) -> p b t", b=B)[:, :, bass.ds(f.t * P, P)]
                    dve.wait_ge(x1_zero, 1)
                    dve.wait_ge(out_done, f.it + NT + 1)
                    nc.vector.scalar_tensor_tensor(x, x_out, 0.5, x, ALU.mult, ALU.add)

            def turn(n, f, x):
                if n:
                    round_qk(n, 0)
                    round_qk(n, 1)
                    rotate(n, 2)
                if f:
                    add_attention(f)
                if n:
                    maximum(n, 0)
                    sums(n, 2)
                    maximum(n, 1)
                    normalise(n, 2)
                    rotate(n, 3)
                    sums(n, 3)
                if f:
                    scale_centred(f)
                if n:
                    normalise(n, 3)
                    divide(n, 0)
                if f:
                    gate(f, 0, n is None)
                if n:
                    divide(n, 1)
                if f:
                    gate(f, 1, n is None)
                if n:
                    round_qk(n, 2)
                if f:
                    gate(f, 2, n is None)
                if n:
                    round_qk(n, 3)
                if x:
                    rotate(x, 0)
                if n:
                    maximum(n, 2)
                if x:
                    sums(x, 0)
                if n:
                    maximum(n, 3)
                if x:
                    normalise(x, 0)
                if f:
                    add_gated(f)
                if x:
                    rotate(x, 1)
                    sums(x, 1)
                    normalise(x, 1)
                if n:
                    divide(n, 2)
                    divide(n, 3)

            turns(dve, turn, before_layer)

        @block.gpsimd
        def _(pool):
            for s in (add_done, d_ready):
                pool.sem_inc(s, B)
            for b in range(B):
                nc.gpsimd.memset(k_blk[b][:, :, 2, :], 0.0)
                last = nc.gpsimd.memset(v_cur[b][:, :, :], 1.0)
            last.then_inc(zeroed, 1)
            for b in range(B):
                last = nc.gpsimd.memset(q_pad[b][:, :, :, :, :], 0.0)
            last.then_inc(zeroed, 1)

            def add(n, b):
                pool.wait_ge(rot_done, n.cur(b))
                nc.gpsimd.tensor_tensor(rot[b][:, :], rot[b][:, :], rot2[b % 2][:, :], ALU.add).then_inc(add_done, 1)

            def spread(n, b):
                pool.wait_ge(max_ready, n.cur(b))
                nc.gpsimd.tensor_tensor(diag[b % 2][:, :, :, :],
                                        neg_max[:, b, :].rearrange("p (j w) -> p w j", w=2).unsqueeze(3).broadcast_to([P, 2, PAIRS, P]),
                                        m.ident[:, :].unsqueeze(1).unsqueeze(1).broadcast_to([P, 2, PAIRS, P]),
                                        ALU.mult).then_inc(d_ready, 1)

            def turn(n, f, x):
                if n:
                    add(n, 2)
                    spread(n, 0)
                    spread(n, 1)
                    add(n, 3)
                if x:
                    add(x, 0)
                if n:
                    spread(n, 2)
                    spread(n, 3)
                if x:
                    add(x, 1)

            turns(pool, turn)

        @block.sync
        def _(sp):
            def stage(n):
                if not isinstance(n.it, int):
                    sp.lower_val(n.it + 1)
                    sp.wait_ge(zeroed, 1)
                sp.wait_ge(v_ready, n.prev(B - 1))
                sp.wait_ge(out_done, n.it + 1)
                for half in range(2):
                    rows = slice(64 * half, 64 * half + 64)
                    sp.dma_start(hT[rows, :, :], m.xs[rows, bass.ds(n.l, 1), :, bass.ds(n.t * P + (1 - half), P)]
                                 .rearrange("p a b t -> p (a b) t")).then_inc(ht_staged, 16)

            def keep(n, b):
                if isinstance(n.it, int):
                    sp.wait_ge(zeroed, 1)
                sp.wait_ge(st_ready, n.prev(b))
                sp.dma_start(k_blk[b][:, :, 0, :], k_blk[b][:, :, 2, :]).then_inc(kprev_done[b], 16)
                sp.wait_ge(pv_ready, n.prev(b))
                sp.dma_start(v_mix[b][0:64, :, :], v_cur[b][64:128, :, :]).then_inc(vprev_done[b], 16)

            def mix(n, b):
                sp.wait_ge(v_evicted, n.cur(b))
                sp.dma_start(v_mix[b][64:128, :, :], v_cur[b][0:64, :, :]).then_inc(vmix_done[b], 16)

            def turn(n, f, x):
                if n:
                    mix(n, 2)
                    mix(n, 3)
                if x:
                    stage(x)
                    keep(x, 0)
                    keep(x, 1)
                    mix(x, 0)
                    mix(x, 1)
                    keep(x, 2)
                    keep(x, 3)

            turns(sp, turn)


def load_stacks(sp, a, scratch, Q, K, b, j, done):
    def quad(which):
        if isinstance(b, int):
            v = scratch[which, b:b + 1, :, :, 4 * j:4 * j + 4, :]
        else:
            v = scratch[which, bass.ds(b, 1), :, :, bass.ds(j * 4, 4), :]
        return v.rearrange("a i d h t -> (a i) d (h t)")

    for i in range(PARTS):
        rows = slice(i * PARTS * DH, (i + 1) * PARTS * DH)
        sp.dma_start(Q[rows, :, :].rearrange("p h t -> p (h t)"),
                     quad(0)[i:i + 1].broadcast_to([PARTS, DH, 4 * T])).then_inc(done, 16)
        sp.dma_start(K[rows, :, :].rearrange("p h t -> p (h t)"), quad(1)).then_inc(done, 16)
    sp.dma_start(Q[KROWS:KROWS + 1, :, :].rearrange("p h t -> p (h t)"), a["zeros"].bitcast(BF16)).then_inc(done, 16)


def project_phase(nc, m, a, stream, V, Y, Q, K, scratch):
    N = B * T // 512
    ctx = ExitStack()
    with ctx:
        def sb(n, shape, dt=FP32):
            return ctx.enter_context(nc.sbuf_tensor(f"prj_{n}", shape, dt))

        def sem(n):
            return semaphore(nc, m, ctx, f"prj_{n}")

        w = sb("w", [P, 4, C])
        total = sb("total", [P, 4])
        passing = Y[:, :, :].rearrange("p t c -> p (t c)")
        sq, log_var, rstd = (passing[:, i * 1024:(i + 1) * 1024].rearrange("p (k n) -> p k n", k=2) for i in range(3))
        positive, neg_sign = (passing[:, i * 512:(i + 1) * 512].rearrange("p (k n) -> p k n", k=4) for i in (6, 7))
        SLOT = 8
        parts = sb("parts", [P, SLOT, PARTS, 512], BF16)
        rest = sb("rest", [P, 2, 512])
        loaded, summed, signs, scaled, turned, weights = (
            sem(s) for s in ("loaded", "summed", "signs", "scaled", "turned", "weights"))
        centred, squared, varred, logged, rstd_ready, normed = (
            sem(s) for s in ("centred", "squared", "varred", "logged", "rstd_ready", "normed"))
        qk_ready, part1, rest_ready, part2, part3, v_ready, v_done = (
            sem(s) for s in ("qk_ready", "part1", "rest_ready", "part2", "part3", "v_ready", "v_done"))
        stored = [[sem(f"stored{b}{i}") for i in range(2)] for b in range(B)]
        stacks, zeroed = sem("stacks"), sem("zeroed")
        ctx.enter_context(nc.allow_non_contiguous_dma(reason="a few columns of parameters"))
        block = ctx.enter_context(nc.Block())

        cen_bank, var_bank, qk_bank, v_bank = m.bank[0:2], m.bank[2:4], m.bank[4:7], m.bank[7]

        @block.tensor
        def _(pe):
            for n in range(N + 2):
                if n < N:
                    if n >= 2:
                        pe.wait_ge(normed, n - 1)
                    nc.tensor.matmul(cen_bank[n % 2][:, :], m.centre[:, :], m.X[:, n * 512:(n + 1) * 512],
                                     start=True, stop=True).then_inc(centred, 1)
                if 1 <= n <= N:
                    k = n - 1
                    pe.wait_ge(squared, k + 1)
                    if k >= 2:
                        pe.wait_ge(logged, k - 1)
                    nc.tensor.matmul(var_bank[k % 2][:, :], m.mean_ones[:, :], sq[:, k % 2, :],
                                     start=True, stop=True).then_inc(varred, 1)
                if n == 2:
                    pe.wait_ge(scaled, 1)
                    for i in range(4):
                        last = nc.tensor.transpose(v_bank[:, i * P:(i + 1) * P], w[:, i, :], m.ident[:, :])
                    last.then_inc(turned, 1)
                    pe.wait_ge(weights, 1)
                if n >= 2:
                    k = n - 2
                    pe.wait_ge(normed, k + 1)
                    for u in (2 * k, 2 * k + 1):
                        if u >= 3:
                            pe.wait_ge(rest_ready, u - 2)
                        nc.tensor.matmul(qk_bank[u % 3][:, :], m.att_w[:, u % 2, :], stream(k),
                                         start=True, stop=True).then_inc(qk_ready, 1)
                    if k >= 1:
                        pe.wait_ge(v_done, k)
                    for i in range(4):
                        last = nc.tensor.matmul(v_bank[:, i * P:(i + 1) * P], stream(k)[:, i * P:(i + 1) * P],
                                                m.att_w[:, 2, :], start=True, stop=True)
                    last.then_inc(v_ready, 1)

        @block.scalar
        def _(act):
            nc.scalar.preload_act_table_set("natural_log_exp_and_others")
            for n in range(N + 2):
                if n < N:
                    act.wait_ge(centred, n + 1)
                    if n >= 2:
                        act.wait_ge(varred, n - 1)
                    nc.scalar.activation(sq[:, n % 2, :], cen_bank[n % 2][:, :], ACT.Square).then_inc(squared, 1)
                if 1 <= n <= N:
                    k = n - 1
                    act.wait_ge(varred, k + 1)
                    nc.scalar.activation(log_var[:, k % 2, :], var_bank[k % 2][:, :], ACT.Ln,
                                         bias=m.eps[:, :]).then_inc(logged, 1)
                    act.wait_ge(logged, k + 1)
                    if k >= 2:
                        act.wait_ge(normed, k - 1)
                    nc.scalar.activation(rstd[:, k % 2, :], log_var[:, k % 2, :], ACT.Exp,
                                         scale=-0.5).then_inc(rstd_ready, 1)
                if n >= 2:
                    for u in (2 * n - 4, 2 * n - 3):
                        act.wait_ge(qk_ready, u + 1)
                        if u >= SLOT:
                            act.wait_ge(stored[(u - SLOT) // 4][u % 2], 16 * PARTS * 2)
                        nc.scalar.activation(parts[:, u % SLOT, 0, :], qk_bank[u % 3][:, :], ACT.Identity,
                                             bias=m.att_bias[:, u % 2:u % 2 + 1]).then_inc(part1, 1)

        @block.vector
        def _(dve):
            nc.vector.memset(K[1][64:ROWS, :, :], 1.0).then_inc(zeroed, 1)
            dve.wait_ge(loaded, 16 * 8)
            nc.vector.tensor_reduce(total[:, :], w[:, :, :], AX.X, ALU.add, apply_absolute_value=True)
            nc.vector.tensor_scalar(positive[:, :, :], w[:, :, :], 0.0, None, ALU.is_gt).then_inc(summed, 1)
            dve.wait_ge(summed, 1)
            nc.vector.scalar_tensor_tensor(neg_sign[:, :, :], w[:, :, :], 0.0, positive[:, :, :],
                                           ALU.is_lt, ALU.subtract).then_inc(signs, 1)
            dve.wait_ge(signs, 1)
            for i in range(4):
                last = nc.vector.tensor_scalar(w[:, i, :], neg_sign[:, i, :], total[:, i:i + 1], -1.0 / C,
                                               ALU.mult, ALU.mult)
            last.then_inc(scaled, 1)
            for n in range(1, N + 2):
                if n <= N:
                    k = n - 1
                    dve.wait_ge(rstd_ready, k + 1)
                    nc.vector.tensor_tensor(stream(k), cen_bank[k % 2][:, :], rstd[:, k % 2, :], ALU.mult).then_inc(normed, 1)
                if n == 2:
                    dve.wait_ge(turned, 1)
                    nc.vector.tensor_copy(m.att_w[:, :, :], v_bank[:, :].rearrange("p (i o) -> p i o", i=4)).then_inc(weights, 1)
                if n >= 2:
                    k = n - 2
                    for u in (2 * k, 2 * k + 1):
                        dve.wait_ge(part1, u + 1)
                        if u >= 2:
                            dve.wait_ge(part3, u - 1)
                        nc.vector.scalar_tensor_tensor(rest[:, u % 2, :], qk_bank[u % 3][:, :], m.att_bias[:, u % 2:u % 2 + 1],
                                                       parts[:, u % SLOT, 0, :], ALU.add, ALU.subtract).then_inc(rest_ready, 1)
                        dve.wait_ge(rest_ready, u + 1)
                        nc.vector.tensor_copy(parts[:, u % SLOT, 1, :], rest[:, u % 2, :]).then_inc(part2, 1)
                    dve.wait_ge(v_ready, k + 1)
                    nc.vector.tensor_tensor(V[:, 4 * k:4 * k + 4, :], v_bank[:, :].rearrange("p (i o) -> p i o", i=4),
                                            m.bv_row[:, :].unsqueeze(1).broadcast_to([P, 4, C]), ALU.add).then_inc(v_done, 1)

        @block.gpsimd
        def _(pool):
            nc.gpsimd.memset(Q[0][64:ROWS, :, :], 0.0)
            nc.gpsimd.memset(K[0][64:ROWS, :, :], 1.0)
            nc.gpsimd.memset(Q[1][64:ROWS, :, :], 0.0).then_inc(zeroed, 1)
            pool.wait_ge(zeroed, 2)
            for u in range(2 * N):
                pool.wait_ge(part2, u + 1)
                nc.gpsimd.tensor_tensor(parts[:, u % SLOT, 2, :], rest[:, u % 2, :], parts[:, u % SLOT, 1, :],
                                        ALU.subtract).then_inc(part3, 1)
            pool.wait_ge(part3, 2 * N)
            nc.gpsimd.memset(Q[2][64:ROWS, :, :], 0.0)
            nc.gpsimd.memset(K[2][64:ROWS, :, :], 1.0)

        @block.sync
        def _(sp):
            for i, name in enumerate(("Wq", "Wk", "Wv", "Wp")):
                sp.dma_start(w[:, i, :], a["L0_attn_" + name]).then_inc(loaded, 16)
            for i, name in enumerate(("bq", "bk", "bp")):
                sp.dma_start(m.att_bias[:, i:i + 1], a["L0_attn_" + name].rearrange("(p a) -> p a", a=1)).then_inc(loaded, 16)
            sp.dma_start(m.bv_row[:, :], a["L0_attn_bv"].rearrange("(a n) -> a n", a=1).broadcast_to([P, C])).then_inc(loaded, 16)
            for u in range(2 * N):
                n = u // 2
                for i in range(PARTS):
                    dst = scratch[u % 2, n // 2, i, :, :, (n % 2) * 512:(n % 2 + 1) * 512].rearrange("d h t -> h d t")
                    sp.wait_ge((part1, part2, part3)[i], u + 1)
                    sp.dma_start(dst, parts[:, u % SLOT, i, :]).then_inc(stored[n // 2][u % 2], 16)
                if u == 3:
                    sp.wait_ge(zeroed, 2)
                    for which in range(2):
                        sp.wait_ge(stored[0][which], 16 * PARTS * 2)
                    for quad in range(2):
                        load_stacks(sp, a, scratch, Q[quad], K[quad], 0, quad, stacks)
            for b in range(1, B):
                for which in range(2):
                    sp.wait_ge(stored[b][which], 16 * PARTS * 2)
            sp.wait_ge(stacks, 2 * 16 * LOADS)
            sp.wait_ge(loaded, 16 * 8)


def attention_phase(nc, m, a, V, Y, Q, K, scratch, m_scratch):
    ctx = ExitStack()
    with ctx:
        def sb(n, shape, dt=FP32):
            return ctx.enter_context(nc.sbuf_tensor(f"att_{n}", shape, dt))

        def sem(n):
            return semaphore(nc, m, ctx, f"att_{n}")

        vq = [sb(f"vq{s}", [P, NT, 4, DH + 1]) for s in range(SLOTS)]
        probs = [sb(f"probs{r}", [P, 4, 512]) for r in range(2)]
        neg_half = sb("neg_half", [P, SLOTS, 32, 2])
        neg_max = sb("neg_max", [P, 2, 16])
        m_rows = sb("m_rows", [16, 2, P], BF16)
        o_sb = sb("o_sb", [P, 2, 512])
        rden = sb("rden", [P, 2, 4, 4])

        (set_up, ring_filled, ring_freed, combined, rows_out, rows_in, e_filled, e_done, av_done,
         o_evicted, rd_ready, v_staged) = (sem(s) for s in (
             "set_up", "ring_filled", "ring_freed", "combined", "rows_out", "rows_in", "e_filled",
             "e_done", "av_done", "o_evicted", "rd_ready", "v_staged"))
        stack_in = [sem(f"stack_in{s}") for s in range(SLOTS)]
        block = ctx.enter_context(nc.Block())

        ring = m.bank[0:3]
        O = m.bank[7]

        def e_slot(e):
            return m.psum[:, 3 + 2 * e:5 + 2 * e, :]

        def ring_uses(ahead, first):
            uses = [[] for _ in range(STEPS)]
            for u in range(UNITS):
                k = LEAD + u
                if ahead or k < UNITS:
                    uses[u // 4].append(("max", k // UNITS, k % UNITS))
                    if k in (UNITS + 1, UNITS + UNITS // 2 + 1):
                        uses[u // 4].append(("rows", 0, 1) if k == UNITS + 1 else ("rows", 1, 0))
            if not ahead:
                uses[UNITS // 4 - LEAD // 4].append(("rows", 0, 1))
            if not first:
                uses[2].append(("out", -1, 1))
            uses[10].append(("out", 0, 0))
            return uses

        USES = UNITS + 4
        BEFORE = LEAD + 1
        first_uses = [("max", 0, u) for u in range(LEAD)]
        first_uses.insert(UNITS // 2 + 2, ("rows", 0, 0))

        class Quad:

            def __init__(self, i, c):
                self.i, self.c = i, c
                self.n = i * SLOTS + c
                self.used = BEFORE + c * USES - (1 if c else 0)

            def slot(self, ahead=0):
                return (self.c + ahead) % SLOTS

            def stack(self, ahead):
                return self.i * (16 * LOADS) + 16 * LOADS * ((self.c + ahead) // SLOTS + 1)

            def ring(self, local):
                return self.i * (SLOTS * USES) + (self.used + local + 1)

            def bank(self, local):
                return ring[(self.used + local) % 3]

            def step(self, u):
                return self.i * (SLOTS * STEPS) + (self.c * STEPS + u + 1)

            def pairs(self, u, e):
                return self.i * (SLOTS * STEPS * 2) + ((self.c * STEPS + u) * 2 + e + 1)

            def rows(self, qc, ahead=0):
                return self.i * (SLOTS * 2) + ((self.c + ahead) * 2 + qc + 1)

            def half(self, qc, ahead=0):
                return self.i * (SLOTS * 2) + ((self.c + ahead) * 2 + qc + 1)

        def body(engine, turn):
            turn(Quad(0, 0), True, False)
            rounds = (B * QUADS - 2) // SLOTS
            with engine.Fori(0, rounds) as i:
                for c in range(SLOTS):
                    turn(Quad(i, c + 1), True, True)
            for n in range(rounds * SLOTS + 1, B * QUADS):
                turn(Quad((n - 1) // SLOTS, (n - 1) % SLOTS + 1), n < B * QUADS - 1, True)

        @block.tensor
        def _(pe):
            def fill(use, q, bank, freed):
                if freed is not None:
                    pe.wait_ge(ring_freed, freed)
                if use[0] == "max":
                    _, ahead, u = use
                    h, qt, kc = u // 8 % 4, u // 32 * 4 + u // 2 % 4, u % 2
                    if u == 0:
                        pe.wait_ge(stack_in[q.slot(ahead)], q.stack(ahead))
                    last = nc.tensor.matmul(bank[:, :], Q[q.slot(ahead)][:, h, qt * P:(qt + 1) * P],
                                            K[q.slot(ahead)][:, h, kc * 512:(kc + 1) * 512], start=True, stop=True)
                elif use[0] == "rows":
                    _, ahead, qc = use
                    pe.wait_ge(combined, q.rows(qc, ahead))
                    last = nc.tensor.transpose(bank[0:16, 0:P], neg_max[:, qc, :], m.ident[:, :])
                else:
                    _, ahead, qc = use
                    pe.wait_ge(o_evicted, q.half(qc, ahead) + 1)
                    for i in range(4):
                        last = nc.tensor.transpose(bank[:, i * P:(i + 1) * P], o_sb[:, qc, i * P:(i + 1) * P], m.ident[:, :])
                last.then_inc(ring_filled, 1)

            pe.wait_ge(set_up, 1)
            start = Quad(0, 0)
            for k, use in enumerate(first_uses):
                fill(use, start, ring[k % 3], k - 2 if k >= 3 else None)

            def scores(q, u, e):
                qc, kt = u // NT, u % NT
                pe.wait_ge(e_done, q.pairs(u, e))
                for h in (2 * e, 2 * e + 1):
                    last = nc.tensor.matmul(e_slot(e)[:, h % 2, :], K[q.slot()][:, h, kt * P:(kt + 1) * P],
                                            Q[q.slot()][:, h, qc * 512:(qc + 1) * 512], start=True, stop=True)
                last.then_inc(e_filled, 1)

            def products(q, u, ahead=0):
                qc, kt = u // NT, u % NT
                if kt == 0:
                    pe.wait_ge(o_evicted, q.half(qc, ahead))
                pe.wait_ge(e_done, q.pairs(u + ahead * STEPS, 1) + 2)
                for h in range(4):
                    last = nc.tensor.matmul(O[32 * h:32 * h + DH + 1, :], vq[q.slot(ahead)][:, kt, h, :], probs[u % 2][:, h, :],
                                            start=kt == 0, stop=kt == NT - 1)
                last.then_inc(av_done, 1)

            def turn(q, more, later):
                local = 0
                pe.wait_ge(v_staged, q.n + 1)
                for u, uses in enumerate(ring_uses(more, not later)):
                    if u % NT == 0:
                        pe.wait_ge(rows_in, q.rows(u // NT) * 16)
                    scores(q, u, 0)
                    scores(q, u, 1)
                    for k, use in enumerate(uses + [None] * (4 - len(uses))):
                        if k == 2 and u:
                            products(q, u - 1)
                        elif k == 2 and later:
                            products(q, STEPS - 1, -1)
                        if use:
                            fill(use, q, q.bank(local), q.ring(local) - 3)
                            local += 1
                if not more:
                    products(q, STEPS - 1)
                    fill(("out", 0, 1), q, q.bank(local), q.ring(local) - 3)

            body(pe, turn)

        @block.scalar
        def _(act):
            def evict(q, qc, ahead=0):
                act.wait_ge(av_done, q.step(NT * qc + NT - 1 + ahead * STEPS) + 2)
                act.wait_ge(rd_ready, q.half(qc, ahead))
                nc.scalar.activation(o_sb[:, qc, :], O[:, :], ACT.Copy).then_inc(o_evicted, 1)

            def turn(q, more, later):
                for u in range(STEPS):
                    for e in range(2):
                        act.wait_ge(e_filled, q.pairs(u, e))
                        if e == 0:
                            act.wait_ge(av_done, q.step(u))
                        nc.scalar.activation(probs[u % 2][:, 2 * e:2 * e + 2, :], e_slot(e), ACT.Exp,
                                             scale=float(DH) ** -0.5).then_inc(e_done, 1)
                    if u == 0 and later:
                        evict(q, 1, -1)
                    if u == NT:
                        evict(q, 0)
                if not more:
                    evict(q, 1)

            act.sem_inc(e_done, 2)
            act.sem_inc(av_done, 2)
            act.sem_inc(rd_ready, 2)
            act.sem_inc(o_evicted, 1)
            body(act, turn)

        @block.vector
        def _(dve):
            def drain(use, q, bank, filled):
                dve.wait_ge(ring_filled, filled)
                if use[0] == "max":
                    _, ahead, u = use
                    kc = u % 2
                    last = nc.vector.tensor_reduce(neg_half[:, q.slot(ahead), u // 2, kc:kc + 1], bank[:, :], AX.X, ALU.max, negate=True)
                elif use[0] == "rows":
                    last = nc.vector.tensor_copy(m_rows[:, use[2], :], bank[0:16, 0:P])
                else:
                    _, ahead, qc = use
                    out = bank[:, :].rearrange("p (i g r) -> p i g r", i=4, g=4)
                    nc.vector.reciprocal(rden[:, qc, :, :], out[:, :, :, DH]).then_inc(rd_ready, 1)
                    dve.wait_ge(rd_ready, q.half(qc, ahead) + 2)
                    b, j = (q.n + ahead) // QUADS, (q.n + ahead) % QUADS
                    dst = Y[:, bass.ds(b * NT + 4 * qc, 4), bass.ds(j * 32, 32)].rearrange("p i (g d) -> p i g d", g=4)
                    last = nc.vector.tensor_tensor(dst, out[:, :, :, 0:DH], rden[:, qc, :, :].unsqueeze(3).broadcast_to([P, 4, 4, DH]), ALU.mult)
                last.then_inc(ring_freed, 1)

            def combine(q, use, uses_done):
                what, ahead, u = use
                if what != "max" or u % (UNITS // 2) != UNITS // 2 - 1:
                    return
                qc = u // (UNITS // 2)
                dve.wait_ge(ring_freed, uses_done)
                nc.vector.tensor_tensor(neg_max[:, qc, :], neg_half[:, q.slot(ahead), 16 * qc:16 * qc + 16, 0],
                                        neg_half[:, q.slot(ahead), 16 * qc:16 * qc + 16, 1], ALU.min).then_inc(combined, 1)

            def stage(q, ahead):
                k = q.n + ahead
                src = V[:, bass.ds(k // QUADS * NT, NT), bass.ds(k % QUADS * 32, 32)].rearrange("p t (h d) -> p t h d", h=4)
                nc.vector.tensor_copy(vq[q.slot(ahead)][:, :, :, 0:DH], src).then_inc(v_staged, 1)

            start = Quad(0, 0)
            for s in range(SLOTS):
                nc.vector.memset(vq[s][:, :, :, :], 1.0)
            nc.vector.memset(O[:, :], 0.0).then_inc(set_up, 1)
            dve.wait_ge(set_up, 1)
            stage(start, 0)
            for k, use in enumerate(first_uses):
                drain(use, start, ring[k % 3], k + 1)
                combine(start, use, k + 1)

            def turn(q, more, later):
                local = 0
                for u, uses in enumerate(ring_uses(more, not later)):
                    for use in uses:
                        drain(use, q, q.bank(local), q.ring(local))
                        combine(q, use, q.ring(local))
                        local += 1
                    if u == 3 and more:
                        stage(q, 1)
                if not more:
                    drain(("out", 0, 1), q, q.bank(local), q.ring(local))

            body(dve, turn)

        @block.sync
        def _(sp):
            def rows(q, ahead, qc, written):
                sp.wait_ge(ring_freed, written)
                half = m_scratch[qc * 16:qc * 16 + 16, :]
                sp.dma_start(half, m_rows[:, qc, :]).then_inc(rows_out, 16)
                sp.wait_ge(rows_out, q.rows(qc, ahead) * 16)
                sp.dma_start(Q[q.slot(ahead)][KROWS:KROWS + 1, :, qc * 512:(qc + 1) * 512],
                             half.rearrange("(a h t) q -> a h (t q)", a=1, h=4)).then_inc(rows_in, 16)

            for slot in range(2):
                sp.sem_inc(stack_in[slot], 16 * LOADS)
            rows(Quad(0, 0), 0, 0, UNITS // 2 + 3)

            def turn(q, more, later):
                order = [use for step in ring_uses(more, not later) for use in step]
                quads_left = not isinstance(q.n, int) or q.n < B * QUADS - 2
                if quads_left and later:
                    sp.wait_ge(ring_freed, q.ring(order.index(("out", -1, 1))))
                if quads_left:
                    k = q.n + 2
                    load_stacks(sp, a, scratch, Q[q.slot(2)], K[q.slot(2)], k // QUADS, k % QUADS, stack_in[q.slot(2)])
                rows(q, 0, 1, q.ring(order.index(("rows", 0, 1))))
                if more:
                    rows(q, 1, 0, q.ring(order.index(("rows", 1, 0))))

            body(sp, turn)


def output_phase(nc, m, Y):
    N = B * T // 512
    ctx = ExitStack()
    with ctx:
        def sem(n):
            return semaphore(nc, m, ctx, f"outp_{n}")

        yT = ctx.enter_context(nc.sbuf_tensor("outp_yT", [P, 2, 512], FP32))
        turned, evicted, projected, added = (sem(s) for s in ("turned", "evicted", "projected", "added"))
        block = ctx.enter_context(nc.Block())

        @block.tensor
        def _(pe):
            for n in range(N + 1):
                if n < N:
                    if n >= 2:
                        pe.wait_ge(evicted, n - 1)
                    for i in range(4):
                        last = nc.tensor.transpose(m.bank[n % 2][:, i * P:(i + 1) * P], Y[:, 4 * n + i, :], m.ident[:, :])
                    last.then_inc(turned, 1)
                if n >= 1:
                    k = n - 1
                    pe.wait_ge(evicted, k + 1)
                    if k >= 2:
                        pe.wait_ge(added, k - 1)
                    nc.tensor.matmul(m.bank[2 + k % 2][:, :], m.att_w[:, 3, :], yT[:, k % 2, :],
                                     start=True, stop=True).then_inc(projected, 1)

        @block.scalar
        def _(act):
            for n in range(N):
                act.wait_ge(turned, n + 1)
                if n >= 2:
                    act.wait_ge(projected, n - 1)
                nc.scalar.activation(yT[:, n % 2, :], m.bank[n % 2][:, :], ACT.Copy).then_inc(evicted, 1)

        @block.vector
        def _(dve):
            for n in range(N):
                x = m.X[:, n * 512:(n + 1) * 512]
                dve.wait_ge(projected, n + 1)
                nc.vector.scalar_tensor_tensor(x, m.bank[2 + n % 2][:, :], m.att_bias[:, 2:3], x,
                                               ALU.add, ALU.add).then_inc(added, 1)


def store_phase(nc, m, a):
    ctx = ExitStack()
    with ctx:
        rows = ctx.enter_context(nc.sbuf_tensor("st_rows", [P, B * NT, C], FP32))
        back = semaphore(nc, m, ctx, "st_back")
        evicted = semaphore(nc, m, ctx, "st_evicted")
        stored = semaphore(nc, m, ctx, "st_stored")
        block = ctx.enter_context(nc.Block())
        N = B * NT // 4

        @block.tensor
        def _(pe):
            for n in range(N):
                if n >= 4:
                    pe.wait_ge(evicted, n - 3)
                for i in range(4):
                    last = nc.tensor.transpose(m.bank[n % 4][:, i * P:(i + 1) * P], m.X[:, (4 * n + i) * P:(4 * n + i + 1) * P], m.ident[:, :])
                last.then_inc(back, 1)

        @block.vector
        def _(dve):
            for n in range(N):
                dve.wait_ge(back, n + 1)
                nc.vector.tensor_copy(rows[:, 4 * n:4 * n + 4, :], m.bank[n % 4][:, :].rearrange("p (i c) -> p i c", i=4)).then_inc(evicted, 1)

        @block.sync
        def _(sp):
            for b in range(B):
                sp.wait_ge(evicted, (b + 1) * NT // 4)
                sp.dma_start(a["out"][b].rearrange("(t p) c -> p t c", p=P), rows[:, b * NT:(b + 1) * NT, :]).then_inc(stored, 16)
            sp.wait_ge(stored, 16 * B)


def build(nc, a):
    ctx = ExitStack()
    with ctx:
        m = Memory()

        def sb(name, shape, dt=FP32):
            return ctx.enter_context(nc.sbuf_tensor(name, shape, dt))

        m.w_cols = 512 + 2 * CH * HC + CH * P
        m.psum = ctx.enter_context(nc.psum_tensor("psum", [P, 8, 512], FP32))
        m.bank = [m.psum[:, i, :] for i in range(8)]
        m.X = sb("X", [P, B * T])
        m.xs = sb("xs", [P, 2, B, T + 1])
        m.wqkv = sb("wqkv", [P, LAYERS, 3 * INNER])
        m.w_all = sb("w_all", [P, LAYERS, m.w_cols])
        m.b1_all = sb("b1_all", [HC, LAYERS, 2 * CH])
        m.b2_all = sb("b2_all", [P, LAYERS])
        m.tab = sb("tab", [P, LAYERS * 2 * NT, 2 * FD])
        m.ident = sb("ident", [P, P])
        m.centre = sb("centre", [P, P])
        m.mean_ones = sb("mean_ones", [P, P])
        m.eps = sb("eps", [P, 1])
        m.ident_b = sb("ident_b", [P, P], BF16)
        m.ones_b = sb("ones_b", [P, P], BF16)
        m.mask_q = sb("mask_q", [P, 2, 2 * P], BF16)
        m.mask_k = sb("mask_k", [P, 2, WIN], BF16)
        scratch = nc.dram_tensor("qk_parts", (2, B, PARTS, DH, H, T), BF16, kind="Internal").ap()
        m_scratch = nc.dram_tensor("maxima", (32, P), BF16, kind="Internal").ap()

        def stream(n):
            return m.xs[:, 0, n // 2, 1 + (n % 2) * 512:1 + (n % 2 + 1) * 512]

        setup_phase(nc, m, a, stream)
        clear_semaphores(nc, m)
        ffn_phase(nc, m, "f0")
        clear_semaphores(nc, m)
        with ExitStack() as branch:
            m.att_w, m.att_bias, m.bv_row, V, Y = (
                branch.enter_context(nc.sbuf_tensor(name, shape, FP32)) for name, shape in (
                    ("att_w", [P, 4, C]), ("att_bias", [P, 3]), ("bv_row", [P, C]),
                    ("V", [P, B * NT, C]), ("Y", [P, B * NT, C])))
            Q, K = ([branch.enter_context(nc.sbuf_tensor(f"{name}{s}", [ROWS, 4, T], BF16)) for s in range(SLOTS)]
                    for name in ("Q", "K"))
            project_phase(nc, m, a, stream, V, Y, Q, K, scratch)
            clear_semaphores(nc, m)
            attention_phase(nc, m, a, V, Y, Q, K, scratch, m_scratch)
            clear_semaphores(nc, m)
            output_phase(nc, m, Y)
            clear_semaphores(nc, m)
        layernorm_phase(nc, m, "ln2", stream)
        clear_semaphores(nc, m)
        ffn_phase(nc, m, "f1")
        clear_semaphores(nc, m)
        store_phase(nc, m, a)


def host_constants():
    return {"rot": rotary_tables(), "consts": constants(), "zeros": np.zeros((1, 4 * T // 2), np.float32)}


INPUTS = ("L0_attn_x", "L0_attn_Wq", "L0_attn_bq", "L0_attn_Wk", "L0_attn_bk", "L0_attn_Wv", "L0_attn_bv",
          "L0_attn_Wp", "L0_attn_bp", "L0_ffn_wqkv", "L0_ffn_q_scale", "L0_ffn_k_scale", "L0_ffn_wo",
          "L0_ffn_ln_g", "L0_ffn_ln_b", "L0_ffn_w1", "L0_ffn_b1", "L0_ffn_w2", "L0_ffn_b2")


def kernel(**inputs):
    import concourse.bacc as bacc
    from concourse.bass_utils import run_bass_kernel_spmd

    nc = bacc.Bacc("TRN2", target_bir_lowering=False, num_devices=1)
    arrays = {name: np.ascontiguousarray(inputs[name]) for name in INPUTS}
    arrays.update(host_constants())
    a = {name: nc.dram_tensor(f"in_{name}", v.shape, mybir.dt.from_np(v.dtype), kind="ExternalInput").ap()
         for name, v in arrays.items()}
    a["out"] = nc.dram_tensor("out", (B, T, C), FP32, kind="ExternalOutput").ap()
    build(nc, a)
    r = run_bass_kernel_spmd(nc, [{f"in_{name}": v for name, v in arrays.items()}], core_ids=[0])
    return r.results[0]["out"]
```
